# Optimizing a Trainium2 kernel written in Bass

```python
import numpy as np
import jax
import jax.numpy as jnp

def _softmax(x, axis=-1):
    return jax.nn.softmax(x, axis=axis)

def _gelu(x):
    return jax.nn.gelu(x, approximate=True)

def _silu(x):
    return jax.nn.silu(x)

def _sigmoid(x):
    return jax.nn.sigmoid(x)

def _layernorm(x, axis=-1, eps=1e-05):
    m = jnp.mean(x, axis=axis, keepdims=True)
    v = jnp.var(x, axis=axis, keepdims=True)
    return (x - m) / jnp.sqrt(v + eps)

def _scatter_add(tgt, idx, src, axis=0):
    return tgt.at[idx].add(src)

def _segment_sum(src, seg, n):
    return jax.ops.segment_sum(src, seg, n)
kernel_name = 'mk_flamingo_gated_d2_seqx_r4_d8367a'

def setup_inputs(seed: int=0):
    np.random.seed(seed)
    _w = jnp.asarray

    def _rec_inputs():
        import jax
        import jax.numpy as jnp
        _rk = jax.random.key(seed)
        x = -0.0002928 + 1 * jax.random.normal(jax.random.fold_in(_rk, 1), (16, 128, 512), jnp.float32)
        _lenS = 128 - jax.random.randint(jax.random.fold_in(_rk, 7), (16,), 0, max(1, 128 // 4) + 1, jnp.int32)
        _lenS2 = 128 - jax.random.randint(jax.random.fold_in(_rk, 8), (16,), 0, max(1, 128 // 4) + 1, jnp.int32)
        _ctx_2048P = jax.random.normal(jax.random.fold_in(_rk, 11), (16, 16, 512), jnp.float32)
        _ctx_2048c = jax.random.dirichlet(jax.random.fold_in(_rk, 511), 0.3 * jnp.ones((16,), jnp.float32), (16, 128))
        _ctx_2048t = jnp.einsum('bsk,bkd->bsd', _ctx_2048c, _ctx_2048P)
        _ctx_2048t = _ctx_2048t * jax.lax.rsqrt(jnp.mean(jnp.square(_ctx_2048t)) + 1e-12) * 0.953939
        ctx_2048 = -1.39393e-06 + 0.999914 * (_ctx_2048t + 0.3 * jax.random.normal(jax.random.fold_in(_rk, 611), (16, 128, 512), jnp.float32))
        _g = jax.random.normal(jax.random.fold_in(_rk, 9001), (2, 2), jnp.float32)
        _g = jnp.sign(_g) * jnp.maximum(jnp.abs(_g), 1.0) + (_g == 0) * 1.0
        g_xattn = _g[0]
        g_ffn = _g[1]
        return (x, ctx_2048, g_xattn, g_ffn)
    x, ctx_2048, g_xattn, g_ffn = _rec_inputs()

    def _L0_xattn_setup():
        import jax, jax.numpy as jnp
        import numpy as np
        HEADS = 8
        DIM_HEAD = 64
        HIDDEN = HEADS * DIM_HEAD
        key = jax.random.key(seed)
        ks = jax.random.split(key, 5)
        b, dim, n = (4, 128, 512)
        ctx_dim, m = (128, 512)
        x = jax.random.normal(ks[0], (b, dim, n), dtype=jnp.float32)
        context = jax.random.normal(ks[1], (b, ctx_dim, m), dtype=jnp.float32)
        Wq = jax.random.normal(ks[2], (HIDDEN, dim), dtype=jnp.float32) / np.sqrt(dim).astype(np.float32)
        Wkv = jax.random.normal(ks[3], (2 * HIDDEN, ctx_dim), dtype=jnp.float32) / np.sqrt(ctx_dim).astype(np.float32)
        Wout = jax.random.normal(ks[4], (dim, HIDDEN), dtype=jnp.float32) / np.sqrt(HIDDEN).astype(np.float32)
        bout = jnp.zeros((dim,), dtype=jnp.float32)
        return {'x': x, 'context': context, 'Wq': Wq, 'Wkv': Wkv, 'Wout': Wout, 'bout': bout}
    _L0_xattn_all = _L0_xattn_setup()
    _L0_xattn_in = {k: v for k, v in _L0_xattn_all.items() if k in ('Wq', 'Wkv', 'Wout', 'bout')}
    del _L0_xattn_all

    def _L0_ffn_setup():
        import jax, jax.numpy as jnp
        import numpy as np
        B, S, D = (2, 1024, 512)
        E, DFF = (8, 2048)
        TOP_K = 2
        key = jax.random.key(seed)
        ks = jax.random.split(key, 4)
        scale_in = 1.0 / np.sqrt(D)
        scale_ff = 1.0 / np.sqrt(DFF)
        return {'hidden_states': jax.random.normal(ks[0], (B, S, D), dtype=jnp.float32), 'gate_w': jax.random.normal(ks[1], (E, D), dtype=jnp.float32) * scale_in, 'w1': jax.random.normal(ks[2], (E, D, DFF), dtype=jnp.float32) * scale_in, 'b1': jnp.zeros((E, DFF), dtype=jnp.float32), 'w2': jax.random.normal(ks[3], (E, DFF, D), dtype=jnp.float32) * scale_ff, 'b2': jnp.zeros((E, D), dtype=jnp.float32)}
    _L0_ffn_all = _L0_ffn_setup()
    _L0_ffn_in = {k: v for k, v in _L0_ffn_all.items() if k in ('gate_w', 'w1', 'b1', 'w2', 'b2')}
    del _L0_ffn_all

    def _L1_xattn_setup():
        import jax, jax.numpy as jnp
        import numpy as np
        N_HEAD = 8
        ALPHA = 5.0
        EPS = 1e-12

        def _l2norm(x, axis):
            n = jnp.sqrt(jnp.sum(x * x, axis=axis, keepdims=True))
            return x / jnp.maximum(n, EPS)
        key = jax.random.key(seed)
        kq, kk, kv = jax.random.split(key, 3)
        B, D, T = (4, 256, 512)
        q = jax.random.normal(kq, (B, D, T), dtype=jnp.float32)
        k = jax.random.normal(kk, (B, D, T), dtype=jnp.float32)
        v = jax.random.normal(kv, (B, D, T), dtype=jnp.float32)
        return {'q': q, 'k': k, 'v': v}
    _L1_xattn_all = _L1_xattn_setup()
    _L1_xattn_in = {k: v for k, v in _L1_xattn_all.items() if k in ()}
    del _L1_xattn_all

    def _L1_ffn_setup():
        import jax, jax.numpy as jnp
        import numpy as np
        LN_EPS = 1e-05
        L2_EPS = 1e-12

        def _l2norm(v, axis):
            n = jnp.sqrt(jnp.sum(v * v, axis=axis, keepdims=True))
            return v / jnp.maximum(n, L2_EPS)
        key = jax.random.key(seed)
        ks = jax.random.split(key, 4)
        B, N, D, E, S, H = (8, 512, 512, 16, 128, 128)
        x = jax.random.normal(ks[0], (B, N, D), dtype=jnp.float32)
        mu = jax.random.normal(ks[1], (D, E, S), dtype=jnp.float32) / np.sqrt(D)
        W1 = jax.random.normal(ks[2], (E, D, H), dtype=jnp.float32) * np.sqrt(2.0 / D)
        W2 = jax.random.normal(ks[3], (E, H, D), dtype=jnp.float32) * np.sqrt(2.0 / (H + D))
        return {'x': x, 'gamma': jnp.ones((D,), jnp.float32), 'beta': jnp.zeros((D,), jnp.float32), 'mu': mu, 'scale': jnp.ones((1,), jnp.float32), 'W1': W1, 'b1': jnp.zeros((E, H), jnp.float32), 'W2': W2, 'b2': jnp.zeros((E, D), jnp.float32)}
    _L1_ffn_all = _L1_ffn_setup()
    _L1_ffn_in = {k: v for k, v in _L1_ffn_all.items() if k in ('gamma', 'beta', 'mu', 'scale', 'W1', 'b1', 'W2', 'b2')}
    del _L1_ffn_all
    return {'x': x, 'ctx_2048': ctx_2048, 'g_xattn': g_xattn, 'g_ffn': g_ffn, 'L0_xattn_Wq': _L0_xattn_in['Wq'], 'L0_xattn_Wkv': _L0_xattn_in['Wkv'], 'L0_xattn_Wout': _L0_xattn_in['Wout'], 'L0_xattn_bout': _L0_xattn_in['bout'], 'L0_ffn_gate_w': _L0_ffn_in['gate_w'], 'L0_ffn_w1': _L0_ffn_in['w1'], 'L0_ffn_b1': _L0_ffn_in['b1'], 'L0_ffn_w2': _L0_ffn_in['w2'], 'L0_ffn_b2': _L0_ffn_in['b2'], 'L1_ffn_gamma': _L1_ffn_in['gamma'], 'L1_ffn_beta': _L1_ffn_in['beta'], 'L1_ffn_mu': _L1_ffn_in['mu'], 'L1_ffn_scale': _L1_ffn_in['scale'], 'L1_ffn_W1': _L1_ffn_in['W1'], 'L1_ffn_b1': _L1_ffn_in['b1'], 'L1_ffn_W2': _L1_ffn_in['W2'], 'L1_ffn_b2': _L1_ffn_in['b2']}

def reference(x, ctx_2048, g_xattn, g_ffn, L0_xattn_Wq, L0_xattn_Wkv, L0_xattn_Wout, L0_xattn_bout, L0_ffn_gate_w, L0_ffn_w1, L0_ffn_b1, L0_ffn_w2, L0_ffn_b2, L1_ffn_gamma, L1_ffn_beta, L1_ffn_mu, L1_ffn_scale, L1_ffn_W1, L1_ffn_b1, L1_ffn_W2, L1_ffn_b2):
    import jax
    import jax.numpy as jnp

    def _L0_xattn_ref(x, context, Wq, Wkv, Wout, bout):
        import jax, jax.numpy as jnp
        import numpy as np
        HEADS = 8
        DIM_HEAD = 64
        HIDDEN = HEADS * DIM_HEAD
        b = x.shape[0]
        q = jnp.einsum('oc,bcn->bon', Wq, x)
        kv = jnp.einsum('oc,bcm->bom', Wkv, context)
        k, v = jnp.split(kv, 2, axis=1)
        split_heads = lambda t: t.reshape(b, HEADS, DIM_HEAD, t.shape[-1])
        q, k, v = (split_heads(q), split_heads(k), split_heads(v))
        sim = jnp.einsum('bhdi,bhdj->bhij', q, k)
        attn = jax.nn.softmax(sim, axis=-1)
        out = jnp.einsum('bhij,bhdj->bhid', attn, v)
        out = jnp.transpose(out, (0, 1, 3, 2)).reshape(b, HIDDEN, -1)
        return jnp.einsum('oc,bcn->bon', Wout, out) + bout[None, :, None]

    def _L0_ffn_ref(hidden_states, gate_w, w1, b1, w2, b2):
        import jax, jax.numpy as jnp
        import numpy as np
        B, S, D = (2, 1024, 512)
        E, DFF = (8, 2048)
        TOP_K = 2
        b, s, d = hidden_states.shape
        x = hidden_states.reshape(-1, d)
        router_logits = x @ gate_w.T
        _, sel = jax.lax.top_k(router_logits.sum(axis=0), TOP_K)
        rw = jax.nn.softmax(router_logits[:, sel].astype(jnp.float32), axis=1)
        rw = rw.astype(x.dtype)
        w1s, b1s = (w1[sel], b1[sel])
        w2s, b2s = (w2[sel], b2[sel])
        h = jax.nn.gelu(jnp.einsum('nd,kdf->knf', x, w1s) + b1s[:, None, :])
        y = jnp.einsum('knf,kfd->knd', h, w2s) + b2s[:, None, :]
        out = jnp.einsum('nk,knd->nd', rw, y)
        return out.reshape(b, s, -1)

    def _L1_xattn_ref(q, k, v):
        import jax, jax.numpy as jnp
        import numpy as np
        N_HEAD = 8
        ALPHA = 5.0
        EPS = 1e-12

        def _l2norm(x, axis):
            n = jnp.sqrt(jnp.sum(x * x, axis=axis, keepdims=True))
            return x / jnp.maximum(n, EPS)
        B, D, Tq = q.shape
        Tk = k.shape[-1]
        Dv = v.shape[-2]
        h = N_HEAD
        d = D // h
        dv = Dv // h
        qh = q.reshape(B, h, d, Tq)
        kh = k.reshape(B, h, d, Tk)
        vh = v.reshape(B, h, dv, Tk)
        qn = _l2norm(qh, axis=-2)
        kn = _l2norm(kh, axis=-2)
        qk = ALPHA * jnp.einsum('bhdq,bhdk->bhqk', qn, kn)
        sm = jax.nn.softmax(qk, axis=-1)
        out = jnp.einsum('bhqk,bhdk->bhdq', sm, vh)
        return out.reshape(B, Dv, Tq)

    def _L1_ffn_ref(x, gamma, beta, mu, scale, W1, b1, W2, b2):
        import jax, jax.numpy as jnp
        import numpy as np
        LN_EPS = 1e-05
        L2_EPS = 1e-12

        def _l2norm(v, axis):
            n = jnp.sqrt(jnp.sum(v * v, axis=axis, keepdims=True))
            return v / jnp.maximum(n, L2_EPS)
        B, N, D = x.shape
        _, E, S = mu.shape
        mean = jnp.mean(x, axis=-1, keepdims=True)
        var = jnp.mean(jnp.square(x - mean), axis=-1, keepdims=True)
        x_ln = (x - mean) / jnp.sqrt(var + LN_EPS) * gamma + beta
        x_n = _l2norm(x_ln, -1) * scale
        mu_n = _l2norm(mu, 0)
        logits = jnp.einsum('bnd,des->bnes', x_n, mu_n)
        dispatch = jax.nn.softmax(logits, axis=1)
        combine = jax.nn.softmax(logits.reshape(B, N, E * S), axis=-1)
        slot_in = jnp.einsum('bnd,bnes->besd', x_ln, dispatch)
        h = jax.nn.gelu(jnp.einsum('besd,edh->besh', slot_in, W1) + b1[None, :, None, :], approximate=False)
        slot_out = jnp.einsum('besh,ehd->besd', h, W2) + b2[None, :, None, :]
        out = jnp.einsum('bsd,bns->bnd', slot_out.reshape(B, E * S, D), combine)
        return out
    x = x + jnp.tanh(g_xattn[0]) * _L0_xattn_ref(_layernorm(x, axis=-1), ctx_2048, L0_xattn_Wq, L0_xattn_Wkv, L0_xattn_Wout, L0_xattn_bout)
    x = x + jnp.tanh(g_ffn[0]) * _L0_ffn_ref(_layernorm(x, axis=-1), L0_ffn_gate_w, L0_ffn_w1, L0_ffn_b1, L0_ffn_w2, L0_ffn_b2)
    x = x + jnp.tanh(g_xattn[1]) * _L1_xattn_ref(_layernorm(x, axis=-1), ctx_2048, ctx_2048)
    x = x + jnp.tanh(g_ffn[1]) * _L1_ffn_ref(_layernorm(x, axis=-1), L1_ffn_gamma, L1_ffn_beta, L1_ffn_mu, L1_ffn_scale, L1_ffn_W1, L1_ffn_b1, L1_ffn_W2, L1_ffn_b2)
    return x

_drawn_inputs = setup_inputs


def setup_inputs(seed=0):
    import zlib

    import numpy as np

    out = dict(_drawn_inputs(seed))
    spreads = {'g_ffn': (-1.0, 0.6),
     'L0_xattn_bout': (0.0, 0.405),
     'L0_ffn_b1': (0.0, 0.319),
     'L0_ffn_b2': (0.0, 0.275),
     'L1_ffn_gamma': (1.0, 0.6),
     'L1_ffn_beta': (0.0, 0.8),
     'L1_ffn_b1': (0.0, 0.8),
     'L1_ffn_b2': (0.0, 1.236)}
    factors = {'L1_ffn_mu': 64.0, 'L1_ffn_W1': 5.855, 'L1_ffn_W2': 4.805}
    for name, (base, spread) in spreads.items():
        noise = np.random.default_rng([zlib.crc32(name.encode()), seed]).standard_normal(out[name].shape)
        drawn = base * np.exp(spread * noise) if base else spread * noise
        out[name] = jnp.asarray(drawn.astype(out[name].dtype))
    for name, factor in factors.items():
        out[name] = (out[name] * factor).astype(out[name].dtype)
    return out
```

```python
from contextlib import ExitStack

import numpy as np
import concourse.bass as bass
from concourse import mybir

F32 = mybir.dt.float32
BF16 = mybir.dt.bfloat16
ALU = mybir.AluOpType
ACT = mybir.ActivationFunctionType
AX_X = mybir.AxisListType.X

B, P, N = 16, 128, 512
HEADS = 8
PAIRS = HEADS // 2
TILES = N // P
LN_EPS = 1e-5


def wait(eng, sem, value):
    if not (isinstance(value, int) and value <= 0):
        eng.wait_ge(sem, value)


def batches(eng, body):
    body(0, True, False)
    with eng.Fori(1, B - 1) as b:
        body(b, False, False)
    body(B - 1, False, True)


def cols(t, width=P):
    return slice(t * width, (t + 1) * width)


class Memory:

    def __init__(self, nc, ctx, stage):
        self.nc, self.ctx, self.stage, self.sems = nc, ctx, stage, []

    def sb(self, name, shape, dt=F32):
        return self.ctx.enter_context(self.nc.sbuf_tensor(f"{self.stage}_{name}", shape, dt))

    def ps(self, name):
        return self.ctx.enter_context(self.nc.psum_tensor(f"{self.stage}_{name}", [P, N], F32))

    def sem(self, name):
        self.sems.append(self.ctx.enter_context(self.nc.semaphore(f"{self.stage}_{name}")))
        return self.sems[-1]

    def block(self):
        self.ctx.callback(self.clear)
        return self.ctx.enter_context(self.nc.Block())

    def clear(self):
        with self.nc.Block() as block:
            @block.sync
            def _(sp):
                for sem in self.sems:
                    sp.sem_clear(sem)


def batch_of(dram, b):
    return dram[bass.ds(b, 1)].rearrange("a p n -> (a p) n")


def stage_load(nc, x_dram, gates_dram, X, stats, mean_rstd, gates):
    with ExitStack() as ctx:
        m = Memory(nc, ctx, "load")
        raw_gates = m.sb("raw_gates", [P, 4])
        x_loaded = [m.sem(f"x_loaded{b}") for b in range(4)]
        gates_loaded = m.sem("gates_loaded")
        gates_done = m.sem("gates_done")
        block = m.block()

        @block.sync
        def _(sp):
            sp.dma_start(raw_gates[:, :], gates_dram.partition_broadcast(P)).then_inc(gates_loaded, 16)
            for q in range(4):
                sp.dma_start(X[:, 4 * q:4 * q + 4, :],
                             x_dram[4 * q:4 * q + 4].rearrange("b p n -> p b n")).then_inc(x_loaded[q], 16)

        @block.scalar
        def _(act):
            act.wait_ge(gates_loaded, 16)
            nc.scalar.activation(gates[:, :], raw_gates[:, :], ACT.Tanh).then_inc(gates_done, 1)
            act.wait_ge(gates_done, 1)

        @block.vector
        def _(dve):
            for q in range(4):
                dve.wait_ge(x_loaded[q], 16)
    row_statistics(nc, "ln0", X, stats, mean_rstd)


def row_statistics(nc, name, X, stats, mean_rstd):
    with ExitStack() as ctx:
        m = Memory(nc, ctx, name)
        moments = m.sb("moments", [P, B, 2])
        spread = m.sb("spread", [P, B, 1])
        row_done = m.sem("row_done")
        moments_done = m.sem("moments_done")
        eps_added = m.sem("eps_added")
        sqrt_done = m.sem("sqrt_done")
        rstd_done = m.sem("rstd_done")
        block = m.block()

        @block.vector
        def _(dve):
            for b in range(B):
                nc.vector.bn_stats(stats[:, b, :], X[:, b, :]).then_inc(row_done, 1)
            dve.wait_ge(row_done, B)
            for b in range(B):
                last = nc.vector.bn_aggr(moments[:, b, :], stats[:, b, :])
                last.then_inc(moments_done, 1)
            dve.wait_ge(moments_done, B)
            nc.vector.tensor_scalar(spread[:, :, :], moments[:, :, 1:2], LN_EPS, None, ALU.add).then_inc(eps_added, 1)
            nc.vector.tensor_copy(mean_rstd[:, :, 0:1], moments[:, :, 0:1]).then_inc(rstd_done, 1)
            dve.wait_ge(sqrt_done, 1)
            nc.vector.reciprocal(mean_rstd[:, :, 1:2], spread[:, :, :]).then_inc(rstd_done, 1)
            dve.wait_ge(rstd_done, 2)

        @block.scalar
        def _(act):
            act.wait_ge(eps_added, 1)
            nc.scalar.activation(spread[:, :, :], spread[:, :, :], ACT.Sqrt).then_inc(sqrt_done, 1)


def stage_attention0(nc, wq_dram, wkv_dram, wout_dram, bout_dram, ctx_dram, X, mean_rstd, gates, ident):
    UNITS = 2 * TILES
    SLOTS = PAIRS * B
    STACK = 12 * 16
    DVE_TURNS = (1, 3)
    ACT_TURNS = tuple(u for u in range(UNITS) if u not in DVE_TURNS)
    with ExitStack() as ctx:
        m = Memory(nc, ctx, "a0")
        w_raw = m.sb("w_raw", [P, 2 * N])
        wq = [m.sb(f"wq_{x}", [P, N], BF16) for x in ("hi", "lo")]
        wkv = [m.sb(f"wkv_{x}", [P, 2 * N], BF16) for x in ("hi", "lo")]
        wo = [m.sb(f"wo_{x}", [P, PAIRS, P], BF16) for x in ("hi", "lo")]
        bout = m.sb("bout", [P, 1])
        gated_bout = m.sb("gated_bout", [P, 1])
        xn = m.sb("xn", [P, N])
        xn_s = [m.sb(f"xn_{x}", [P, N], BF16) for x in ("hi", "lo")]
        cx = m.sb("cx", [P, N])
        cx_s = [m.sb(f"cx_{x}", [P, N], BF16) for x in ("hi", "lo")]
        q_nat = [[m.sb(f"q_nat_{x}{i}", [P, N], BF16) for x in ("hi", "lo")] for i in range(2)]
        k_nat = [[m.sb(f"k_nat_{x}{i}", [P, N], BF16) for x in ("hi", "lo")] for i in range(2)]
        q_hi2 = m.sb("q_hi2", [P, HEADS, N], BF16)
        q_lo2 = m.sb("q_lo2", [P, HEADS, N], BF16)
        k_hilo = m.sb("k_hilo", [P, HEADS, N], BF16)
        v = m.sb("v", [P, PAIRS, TILES, P])
        prob = m.sb("prob", [P, 2, 2, TILES, N])
        prob_t = m.sb("prob_t", [P, 2, 2, TILES, N])
        neg_max = m.sb("neg_max", [P, 2 * UNITS])
        denom = m.sb("denom", [P, 2 * UNITS])
        inv = m.sb("inv", [P, 2 * UNITS])
        o_s = [m.sb(f"o_{x}", [P, PAIRS, N], BF16) for x in ("hi", "lo")]
        x_biased = m.sb("x_biased", [P, N])
        sim = [m.ps(f"sim{i}") for i in range(4)]
        tr = [m.ps(f"tr{i}") for i in range(2)]
        av = m.ps("av")
        misc = m.ps("misc")

        w_loaded = [m.sem(f"w_loaded{i}") for i in range(4)]
        w_split = m.sem("w_split")
        w_free = m.sem("w_free")
        cx_loaded = m.sem("cx_loaded")
        xn_done = m.sem("xn_done")
        hi_done = m.sem("hi_done")
        cxhi_done = m.sem("cxhi_done")
        x_lo_done, ctx_lo_done = m.sem("x_lo_done"), m.sem("ctx_lo_done")
        q_ready, k_ready, v_ready = m.sem("q_ready"), m.sem("k_ready"), m.sem("v_ready")
        q_hi_out, k_hi_out = m.sem("q_hi_out"), m.sem("k_hi_out")
        q_lo_out, k_lo_out, v_out = m.sem("q_lo_out"), m.sem("k_lo_out"), m.sem("v_out")
        stacked = [m.sem(f"stacked{p}") for p in range(PAIRS)]
        sim_ready, max_ready, exp_done = m.sem("sim_ready"), m.sem("max_ready"), m.sem("exp_done")
        inv_done, norm_done = m.sem("inv_done"), m.sem("norm_done")
        tr_ready, tr_out_act, tr_out_dve = m.sem("tr_ready"), m.sem("tr_out_act"), m.sem("tr_out_dve")
        av_ready, o_hi_out, o_lo_out = m.sem("av_ready"), m.sem("o_hi_out"), m.sem("o_lo_out")
        proj_ready, xb_done, x_done = m.sem("proj_ready"), m.sem("xb_done"), m.sem("x_done")
        block = m.block()

        def turns_before(turns, unit):
            return sum(t < unit for t in turns)

        def wait_tr_out(eng, s, u):
            if u in DVE_TURNS:
                wait(eng, tr_out_dve, s * len(DVE_TURNS) + turns_before(DVE_TURNS, u) + 1)
            else:
                wait(eng, tr_out_act, s * len(ACT_TURNS) + turns_before(ACT_TURNS, u) + 1)

        @block.sync
        def _(sp):
            sp.dma_start(w_raw[:, 0:N], wq_dram).then_inc(w_loaded[0], 16)
            sp.dma_start(bout[:, :], bout_dram).then_inc(w_loaded[3], 16)
            sp.dma_start(cx[:, :], ctx_dram[0]).then_inc(cx_loaded, 16)
            sp.wait_ge(w_free, 1)
            sp.dma_start(w_raw[:, :], wkv_dram).then_inc(w_loaded[1], 16)
            sp.wait_ge(w_free, 2)
            sp.dma_start(w_raw[:, 0:N], wout_dram).then_inc(w_loaded[2], 16)

            def load_ctx(b):
                wait(sp, ctx_lo_done, b)
                sp.dma_start(cx[:, :], batch_of(ctx_dram, b)).then_inc(cx_loaded, 16)

            def stack(s, p):
                ready = s + 1
                wait(sp, sim_ready, UNITS * ready - 4 * UNITS)
                sp.wait_ge(q_lo_out, ready)
                for half in range(2):
                    rows = slice(64 * half, 64 * half + 64)
                    for dst, src in ((q_hi2, q_nat[p % 2][0]), (q_lo2, q_nat[p % 2][1])):
                        for to in range(2):
                            sp.dma_start(dst[64 * to:64 * to + 64, 2 * p + half, :], src[rows, :])\
                              .then_inc(stacked[p], 16)
                sp.wait_ge(k_lo_out, ready)
                for half in range(2):
                    rows = slice(64 * half, 64 * half + 64)
                    for to in range(2):
                        sp.dma_start(k_hilo[64 * to:64 * to + 64, 2 * p + half, :], k_nat[p % 2][to][rows, :])\
                          .then_inc(stacked[p], 16)

            stack(0, 0)
            stack(1, 1)

            def body(b, first, last):
                for p in range(PAIRS):
                    if p == 0 and not last:
                        load_ctx(b + 1)
                    if not (last and p >= 2):
                        stack(PAIRS * b + p + 2, (p + 2) % PAIRS)
            batches(sp, body)

        @block.tensor
        def _(pe):
            def three(out, stat, mov, start=True, stop=True):
                nc.tensor.matmul(out, stat[0], mov[0], start=start, stop=False)
                nc.tensor.matmul(out, stat[0], mov[1], start=False, stop=False)
                return nc.tensor.matmul(out, stat[1], mov[0], start=False, stop=stop)

            def project_q(s, p, b_of):
                pe.wait_ge(x_lo_done, b_of + 1)
                wait(pe, v_out, s)
                if p == 0:
                    wait(pe, x_done, b_of - 1)
                three(misc[:, :], [w[:, cols(p)] for w in wq], [t[:, :] for t in xn_s]).then_inc(q_ready, 1)

            def project_k(s, p, b_of):
                pe.wait_ge(ctx_lo_done, b_of + 1)
                pe.wait_ge(q_lo_out, s + 1)
                three(misc[:, :], [w[:, cols(p)] for w in wkv], [t[:, :] for t in cx_s]).then_inc(k_ready, 1)

            def project_v(s, p):
                pe.wait_ge(k_lo_out, s + 1)
                for jt in range(TILES):
                    last = three(misc[:, cols(jt)], [t[:, cols(jt)] for t in cx_s],
                                 [w[:, N + p * P:N + (p + 1) * P] for w in wkv], start=jt == 0, stop=jt == TILES - 1)
                last.then_inc(v_ready, 1)

            def project_out(b, vs):
                pe.wait_ge(o_lo_out, PAIRS * (b + 1))
                wait(pe, v_out, vs)
                for p in range(PAIRS):
                    last = three(misc[:, :], [w[:, p, :] for w in wo], [t[:, p, :] for t in o_s],
                                 start=p == 0, stop=p == PAIRS - 1)
                last.then_inc(proj_ready, 1)

            def scores(s, p, u, b_of):
                if u == 0:
                    pe.wait_ge(stacked[p], STACK * b_of + STACK)
                head, it, U = 2 * p + u // TILES, u % TILES, UNITS * s + u
                wait(pe, exp_done, U - 3)
                bank = sim[u % 4][:, :]
                nc.tensor.matmul(bank, q_hi2[:, head, cols(it)], k_hilo[:, head, :], start=True, stop=False)
                nc.tensor.matmul(bank, q_lo2[:, head, cols(it)], k_hilo[:, head, :], start=False, stop=True)\
                    .then_inc(sim_ready, 1)

            def transposes(s, p, u):
                hh, jt = u // TILES, u % TILES
                if jt == 0:
                    wait(pe, norm_done, UNITS * s + TILES * (hh + 1))
                wait_tr_out(pe, s if u >= 2 else s - 1, u - 2 if u >= 2 else u + UNITS - 2)
                for it in range(TILES):
                    last = nc.tensor.transpose(tr[u % 2][:, cols(it)], prob[:, p % 2, hh, it, cols(jt)], ident[:, :])
                last.then_inc(tr_ready, 1)

            def values(s, p, jt):
                if jt == 0:
                    wait_tr_out(pe, s, UNITS - 1)
                    wait_tr_out(pe, s, UNITS - 2)
                    wait(pe, o_lo_out, s)
                    pe.wait_ge(v_out, s + 1)
                for hh in range(2):
                    last = nc.tensor.matmul(av[64 * hh:64 * hh + 64, :], v[:, p, jt, 64 * hh:64 * hh + 64],
                                            prob_t[:, p % 2, hh, jt, :], start=jt == 0, stop=jt == TILES - 1)
                if jt == TILES - 1:
                    last.then_inc(av_ready, 1)

            pe.wait_ge(w_split, 3)
            for s in range(2):
                project_q(s, s, 0)
                project_k(s, s, 0)
                project_v(s, s)
            scores(0, 0, 0, 0)

            def body(b, first, last):
                for p in range(PAIRS):
                    s = PAIRS * b + p
                    for u in range(UNITS):
                        if u + 1 < UNITS:
                            scores(s, p, u + 1, b)
                        elif not (last and p == PAIRS - 1):
                            scores(s + 1, (p + 1) % PAIRS, 0, b + (p + 1) // PAIRS)
                        if not (first and p == 0):
                            transposes(s - 1, (p - 1) % PAIRS, u)
                        if u % 2 and not (first and p < 2):
                            values(s - 2, (p - 2) % PAIRS, u // 2)
                        if not (last and p >= 2):
                            if u == 2:
                                project_q(s + 2, (p + 2) % PAIRS, b + (p + 2) // PAIRS)
                            if u == 4:
                                project_k(s + 2, (p + 2) % PAIRS, b + (p + 2) // PAIRS)
                            if u == 7:
                                project_v(s + 2, (p + 2) % PAIRS)
                        if p == 2 and u == 1 and not first:
                            project_out(b - 1, s + 2)
            batches(pe, body)
            for u in range(UNITS):
                transposes(SLOTS - 1, PAIRS - 1, u)
            for s in (SLOTS - 2, SLOTS - 1):
                for jt in range(TILES):
                    values(s, s % PAIRS, jt)
            project_out(B - 1, SLOTS)

        @block.scalar
        def _(act):
            def exp(s, p, u):
                U, at = UNITS * s + u, UNITS * (p % 2) + u
                if u == 0:
                    wait(act, tr_ready, UNITS * (s - 1))
                    wait(act, norm_done, UNITS * (s - 1))
                act.wait_ge(max_ready, U + 1)
                nc.scalar.activation(prob[:, p % 2, u // TILES, u % TILES, :], sim[u % 4][:, :], ACT.Exp,
                                     bias=neg_max[:, at:at + 1], scale=-1.0, accum_out=denom[:, at:at + 1])\
                    .then_inc(exp_done, 1)

            def copy_transposes(s, p, u):
                act.wait_ge(tr_ready, UNITS * s + u + 1)
                if u == ACT_TURNS[0]:
                    wait(act, av_ready, s - 1)
                nc.scalar.activation(prob_t[:, p % 2, u // TILES, u % TILES, :], tr[u % 2][:, :], ACT.Copy)\
                    .then_inc(tr_out_act, 1)

            def q_hi(s, p):
                act.wait_ge(q_ready, s + 1)
                nc.scalar.activation(q_nat[p % 2][0][:, :], misc[:, :], ACT.Copy).then_inc(q_hi_out, 1)

            def k_hi(s, p):
                act.wait_ge(k_ready, s + 1)
                nc.scalar.activation(k_nat[p % 2][0][:, :], misc[:, :], ACT.Copy).then_inc(k_hi_out, 1)

            def o_hi(s, p=None):
                act.wait_ge(av_ready, s + 1)
                nc.scalar.activation(o_s[0][:, s % PAIRS if p is None else p, :], av[:, :], ACT.Copy)\
                    .then_inc(o_hi_out, 1)

            def ctx_hi(b):
                act.wait_ge(cx_loaded, 16 * b + 16)
                wait(act, v_ready, PAIRS * b)
                nc.scalar.activation(cx_s[0][:, :], cx[:, :], ACT.Copy).then_inc(cxhi_done, 1)

            ctx_hi(0)
            for s in range(2):
                q_hi(s, s)
                k_hi(s, s)

            def body(b, first, last):
                for p in range(PAIRS):
                    s = PAIRS * b + p
                    for u in range(UNITS):
                        if u == 0 and not (first and p < 3):
                            if p == 3 and not first:
                                act.wait_ge(proj_ready, b)
                            o_hi(s - 3, (p - 3) % PAIRS)
                        exp(s, p, u)
                        if u in ACT_TURNS and not (first and p == 0):
                            copy_transposes(s - 1, (p - 1) % PAIRS, u)
                        if not (last and p >= 2):
                            q = (p + 2) % PAIRS
                            if u == 3:
                                act.wait_ge(stacked[p], STACK * b + STACK)
                                q_hi(s + 2, q)
                            if u == 5:
                                k_hi(s + 2, q)
                        if not last and p == 2 and u == 1:
                            ctx_hi(b + 1)
            batches(act, body)
            o_hi(SLOTS - 3)
            for u in ACT_TURNS:
                copy_transposes(SLOTS - 1, PAIRS - 1, u)
            for s in (SLOTS - 2, SLOTS - 1):
                o_hi(s)

        @block.vector
        def _(dve):
            def less(out, full, hi):
                return nc.vector.tensor_tensor(out, full, hi, ALU.subtract)

            def split_weights(n, width, dst, sign=1.0):
                dve.wait_ge(w_loaded[n], 16)
                src = w_raw[:, 0:width]
                flat = [d[:, :] if n < 2 else d[:, :, :].rearrange("p t n -> p (t n)") for d in dst]
                nc.vector.tensor_scalar(flat[0], src, sign, None, ALU.mult).then_inc(hi_done, 1)
                dve.wait_ge(hi_done, n + 1)
                nc.vector.scalar_tensor_tensor(out=flat[1], in0=src, scalar=sign, in1=flat[0], op0=ALU.mult,
                                               op1=ALU.subtract).then_inc(w_split, 1)
                dve.wait_ge(w_split, n + 1)
                dve.sem_inc(w_free, 1)

            def normalise_x(b):
                wait(dve, x_lo_done, b)
                nc.vector.tensor_scalar(xn[:, :], x_at(b), mr_at(b, 0), mr_at(b, 1), ALU.subtract, ALU.mult)\
                    .then_inc(xn_done, 1)

            def x_at(b):
                return X[:, bass.ds(b, 1), :].rearrange("p a n -> p (a n)")

            def mr_at(b, i):
                return mean_rstd[:, bass.ds(b, 1), i:i + 1].rearrange("p a n -> p (a n)")

            def x_hi(b):
                wait(dve, q_ready, PAIRS * b)
                dve.wait_ge(xn_done, b * 2 + 1)
                nc.vector.tensor_copy(xn_s[0][:, :], xn[:, :]).then_inc(xn_done, 1)

            def ctx_lo(b):
                dve.wait_ge(cxhi_done, b + 1)
                less(cx_s[1][:, :], cx[:, :], cx_s[0][:, :]).then_inc(ctx_lo_done, 1)

            def x_lo(b):
                dve.wait_ge(xn_done, b * 2 + 2)
                less(xn_s[1][:, :], xn[:, :], xn_s[0][:, :]).then_inc(x_lo_done, 1)

            def q_lo(s, p):
                dve.wait_ge(q_hi_out, s + 1)
                less(q_nat[p % 2][1][:, :], misc[:, :], q_nat[p % 2][0][:, :]).then_inc(q_lo_out, 1)

            def k_lo(s, p):
                dve.wait_ge(k_hi_out, s + 1)
                less(k_nat[p % 2][1][:, :], misc[:, :], k_nat[p % 2][0][:, :]).then_inc(k_lo_out, 1)

            def v_copy(s, p):
                dve.wait_ge(v_ready, s + 1)
                wait(dve, av_ready, s - 3)
                nc.vector.tensor_copy(v[:, p, :, :], misc[:, :].rearrange("p (t n) -> p t n", t=TILES))\
                    .then_inc(v_out, 1)

            def row_max(s, p, u):
                at = UNITS * (p % 2) + u
                dve.wait_ge(sim_ready, UNITS * s + u + 1)
                nc.vector.tensor_reduce(neg_max[:, at:at + 1], sim[u % 4][:, :], AX_X, ALU.min).then_inc(max_ready, 1)

            def invert(s, p, u):
                at = UNITS * (p % 2) + u
                dve.wait_ge(exp_done, UNITS * s + u + 1)
                nc.vector.reciprocal(inv[:, at:at + 1], denom[:, at:at + 1]).then_inc(inv_done, 1)

            def normalise(s, p, u):
                at = UNITS * (p % 2) + u
                dve.wait_ge(inv_done, UNITS * s + u + 1)
                row = prob[:, p % 2, u // TILES, u % TILES, :]
                nc.vector.tensor_scalar(row, row, inv[:, at:at + 1], None, ALU.mult).then_inc(norm_done, 1)

            def copy_transposes(s, p, u):
                dve.wait_ge(tr_ready, UNITS * s + u + 1)
                if u == DVE_TURNS[0]:
                    wait(dve, av_ready, s - 1)
                nc.vector.tensor_copy(prob_t[:, p % 2, u // TILES, u % TILES, :], tr[u % 2][:, :])\
                    .then_inc(tr_out_dve, 1)

            def o_lo(s, p):
                dve.wait_ge(o_hi_out, s + 1)
                less(o_s[1][:, p, :], av[:, :], o_s[0][:, p, :]).then_inc(o_lo_out, 1)

            def bias_x(b):
                wait(dve, x_done, b)
                nc.vector.tensor_scalar(x_biased[:, :], x_at(b), gated_bout[:, 0:1], None, ALU.add).then_inc(xb_done, 1)

            def update_x(b):
                dve.wait_ge(xb_done, b + 1)
                dve.wait_ge(proj_ready, b + 1)
                nc.vector.scalar_tensor_tensor(out=x_at(b), in0=misc[:, :], scalar=gates[:, 0:1], in1=x_biased[:, :],
                                               op0=ALU.mult, op1=ALU.add).then_inc(x_done, 1)

            split_weights(0, N, wq, -1.0)
            normalise_x(0)
            split_weights(1, 2 * N, wkv)
            x_hi(0)
            ctx_lo(0)
            split_weights(2, N, wo)
            x_lo(0)
            dve.wait_ge(w_loaded[3], 16)
            nc.vector.tensor_scalar(gated_bout[:, :], bout[:, :], gates[:, 0:1], None, ALU.mult).then_inc(w_split, 1)
            dve.wait_ge(w_split, 4)
            for s in range(2):
                q_lo(s, s)
                k_lo(s, s)
                v_copy(s, s)
            bias_x(0)

            def body(b, first, last):
                for p in range(PAIRS):
                    s = PAIRS * b + p
                    for u in range(UNITS):
                        row_max(s, p, u)
                        if u == 0 and not (first and p == 0) and not (last and p == PAIRS - 1):
                            v_copy(s + 1, (p + 1) % PAIRS)
                        if p == 2 and not first and u == 2:
                            update_x(b - 1)
                        if not (last and p >= 2):
                            if u == 4:
                                q_lo(s + 2, (p + 2) % PAIRS)
                            if u == 6:
                                k_lo(s + 2, (p + 2) % PAIRS)
                        for step, lag in ((invert, 2), (normalise, 3)):
                            if u >= lag:
                                step(s, p, u - lag)
                            elif not (first and p == 0):
                                step(s - 1, (p - 1) % PAIRS, u - lag + UNITS)
                        if u in DVE_TURNS and not (first and p == 0):
                            copy_transposes(s - 1, (p - 1) % PAIRS, u)
                        if u == 0 and not (first and p < 3):
                            o_lo(s - 3, (p - 3) % PAIRS)
                        if not last and p == 1:
                            if u == 4:
                                normalise_x(b + 1)
                            if u == 5:
                                x_hi(b + 1)
                            if u == 6:
                                x_lo(b + 1)
                        if not last and p == 2 and u == 1:
                            ctx_lo(b + 1)
                        if p == 2 and not first and u == 3:
                            bias_x(b)
            batches(dve, body)
            for step, lag in ((invert, 2), (normalise, 3)):
                for u in range(UNITS - lag, UNITS):
                    step(SLOTS - 1, PAIRS - 1, u)
            o_lo(SLOTS - 3, (SLOTS - 3) % PAIRS)
            for u in DVE_TURNS:
                copy_transposes(SLOTS - 1, PAIRS - 1, u)
            for s in (SLOTS - 2, SLOTS - 1):
                o_lo(s, s % PAIRS)
            update_x(B - 1)
            dve.wait_ge(x_done, B)


E, TOP_K, DFF = 8, 2, 2048
CHUNKS = 2 * DFF // N
TOKENS = B * P


def stage_route(nc, gate_dram, iota_dram, X, xt, mean_rstd, gates, ident, chosen, route_gain):
    with ExitStack() as ctx:
        m = Memory(nc, ctx, "route")
        gate_raw = m.sb("gate_raw", [P, TILES, E])
        gate = [m.sb(f"gate_{x}", [P, TILES, E], BF16) for x in ("hi", "lo")]
        iota = m.sb("iota", [P, E])
        ones = m.sb("ones", [P, P])
        xn = m.sb("xn", [P, 2, N])
        logits = m.sb("logits", [P, B, E])
        picked = m.sb("picked", [P, B, E])
        token_sum = m.sb("token_sum", [P, E])
        total = m.sb("total", [P, E])
        top = m.sb("top", [P, E])
        top_index = m.sb("top_index", [P, E], mybir.dt.uint32)
        index_f = m.sb("index_f", [P, E])
        onehot = m.sb("onehot", [P, TOP_K, E])
        pair = m.sb("pair", [P, TOP_K, B])
        largest = m.sb("largest", [P, B])
        inv = m.sb("inv", [P, B])
        tr = [m.ps(f"tr{i}") for i in range(4)]
        logits_ps = m.ps("logits_ps")
        total_ps = m.ps("total_ps")
        loaded = m.sem("loaded")
        small = m.sem("small")
        xn_done, tr_ready, hi_out, lo_out = m.sem("xn_done"), m.sem("tr_ready"), m.sem("hi_out"), m.sem("lo_out")
        logits_ready, total_ready, exp_ready, exp_done = (m.sem("logits_ready"), m.sem("total_ready"),
                                                          m.sem("exp_ready"), m.sem("exp_done"))
        gate_split, sum_done, ones_done = m.sem("gate_split"), m.sem("sum_done"), m.sem("ones_done")
        block = m.block()

        @block.sync
        def _(sp):
            sp.dma_start(gate_raw[:, :, :], gate_dram).then_inc(loaded, 16)
            sp.dma_start(iota[:, :], iota_dram.partition_broadcast(P)).then_inc(loaded, 16)

        @block.tensor
        def _(pe):
            def transposes(b):
                pe.wait_ge(xn_done, b + 1)
                wait(pe, lo_out, b - 3)
                for dt in range(TILES):
                    last = nc.tensor.transpose(tr[b % 4][:, cols(dt)], xn[:, b % 2, cols(dt)], ident[:, :])
                last.then_inc(tr_ready, 1)

            def logit(b):
                pe.wait_ge(lo_out, b + 1)
                for dt in range(TILES):
                    for i, j in ((0, 0), (1, 0), (0, 1)):
                        last = nc.tensor.matmul(logits_ps[:, b * E:(b + 1) * E], xt[i][:, dt, b * P:(b + 1) * P],
                                                gate[j][:, dt, :], start=(dt, i, j) == (0, 0, 0),
                                                stop=(dt, i, j) == (TILES - 1, 0, 1))
                last.then_inc(logits_ready, 1)

            pe.wait_ge(gate_split, 2)
            for b in range(B + 1):
                if b < B:
                    transposes(b)
                if b:
                    logit(b - 1)
            pe.wait_ge(sum_done, 1)
            pe.wait_ge(ones_done, 1)
            nc.tensor.matmul(total_ps[:, 0:E], ones[:, :], token_sum[:, :], start=True, stop=True)\
                .then_inc(total_ready, 1)

        @block.scalar
        def _(act):
            for b in range(B):
                act.wait_ge(tr_ready, b + 1)
                nc.scalar.activation(xt[0][:, :, b * P:(b + 1) * P], tr[b % 4][:, :].rearrange("p (t n) -> p t n", t=TILES),
                                     ACT.Copy).then_inc(hi_out, 1)
            act.wait_ge(exp_ready, 1)
            nc.scalar.activation(pair[:, :, :], pair[:, :, :], ACT.Exp).then_inc(exp_done, 1)

        @block.vector
        def _(dve):
            steps = [0]

            def step(ins):
                steps[0] += 1
                ins.then_inc(small, 1)
                dve.wait_ge(small, steps[0])

            nc.vector.memset(ones[:, :], 1.0).then_inc(ones_done, 1)
            dve.wait_ge(loaded, 32)
            nc.vector.tensor_copy(gate[0][:, :, :], gate_raw[:, :, :]).then_inc(gate_split, 1)
            dve.wait_ge(gate_split, 1)
            nc.vector.tensor_tensor(gate[1][:, :, :], gate_raw[:, :, :], gate[0][:, :, :], ALU.subtract)\
                .then_inc(gate_split, 1)

            def normalise(b):
                wait(dve, tr_ready, b - 1)
                nc.vector.tensor_scalar(xn[:, b % 2, :], X[:, b, :], mean_rstd[:, b, 0:1], mean_rstd[:, b, 1:2],
                                        ALU.subtract, ALU.mult).then_inc(xn_done, 1)
            normalise(0)
            for b in range(B):
                if b + 1 < B:
                    normalise(b + 1)
                dve.wait_ge(hi_out, b + 1)
                nc.vector.tensor_tensor(xt[1][:, :, b * P:(b + 1) * P], tr[b % 4][:, :].rearrange("p (t n) -> p t n", t=TILES),
                                        xt[0][:, :, b * P:(b + 1) * P], ALU.subtract).then_inc(lo_out, 1)
            dve.wait_ge(logits_ready, B)
            step(nc.vector.tensor_copy(logits[:, :, :].rearrange("p b e -> p (b e)"), logits_ps[:, 0:B * E]))
            nc.vector.tensor_reduce(token_sum[:, :], logits[:, :, :].rearrange("p b e -> p e b"), AX_X, ALU.add)\
                .then_inc(sum_done, 1)
            dve.wait_ge(total_ready, 1)
            step(nc.vector.tensor_copy(total[:, :], total_ps[:, 0:E]))
            step(nc.vector.max(top[:, :], total[:, :]))
            step(nc.vector.max_index(top_index[:, :], top[:, :], total[:, :]))
            step(nc.vector.tensor_copy(chosen[:, :], top_index[:, 0:TOP_K]))
            step(nc.vector.tensor_copy(index_f[:, :], top_index[:, :]))
            for k in range(TOP_K):
                step(nc.vector.tensor_scalar(onehot[:, k, :], iota[:, :], index_f[:, k:k + 1], None, ALU.is_equal))
                step(nc.vector.tensor_tensor(picked[:, :, :], logits[:, :, :],
                                             onehot[:, k:k + 1, :].to_broadcast([P, B, E]), ALU.mult))
                step(nc.vector.tensor_reduce(pair[:, k, :], picked[:, :, :], AX_X, ALU.add))
            step(nc.vector.tensor_tensor(largest[:, :], pair[:, 0, :], pair[:, 1, :], ALU.max))
            for k in range(TOP_K):
                ins = nc.vector.tensor_tensor(pair[:, k, :], pair[:, k, :], largest[:, :], ALU.subtract)
                ins.then_inc(exp_ready if k else small, 1)
                steps[0] += 1 - k
                dve.wait_ge(exp_ready if k else small, 1 if k else steps[0])
            dve.wait_ge(exp_done, 1)
            step(nc.vector.tensor_tensor(largest[:, :], pair[:, 0, :], pair[:, 1, :], ALU.add))
            step(nc.vector.reciprocal(inv[:, :], largest[:, :]))
            step(nc.vector.tensor_scalar(inv[:, :], inv[:, :], gates[:, 2:3], None, ALU.mult))
            for c in range(CHUNKS):
                step(nc.vector.tensor_tensor(route_gain[:, c, :], pair[:, c // (CHUNKS // 2), :], inv[:, :], ALU.mult))


def stage_ffn0(nc, w1_dram, b1_dram, w2_dram, b2_dram, X, xt, chosen, route_gain):
    GROUPS = TOKENS // N
    STEP_UNITS = TILES
    with ExitStack() as ctx:
        m = Memory(nc, ctx, "f0")
        raw = [m.sb(f"raw{i}", [P, TILES, N]) for i in range(2)]
        w1 = [[m.sb(f"w1_{x}{i}", [P, TILES, N], BF16) for x in ("hi", "lo")] for i in range(2)]
        w2 = [[m.sb(f"w2_{x}{i}", [P, TILES, N], BF16) for x in ("hi", "lo")] for i in range(2)]
        b1 = m.sb("b1", [P, 2, TILES])
        b2 = [m.sb(f"b2_{k}", [P, N]) for k in range(TOP_K)]
        hidden = m.sb("hidden", [P, TILES, N])
        h = [[m.sb(f"h_{x}{i}", [P, TILES, N], BF16) for x in ("hi", "lo")] for i in range(2)]
        h_ps = [m.ps(f"h{i}") for i in range(4)]
        y_ps = [m.ps(f"y{i}") for i in range(4)]
        w1_loaded, w2_loaded = m.sem("w1_loaded"), m.sem("w2_loaded")
        b1_loaded, b2_loaded, b2_added = m.sem("b1_loaded"), m.sem("b2_loaded"), m.sem("b2_added")
        w_hi, w_split = m.sem("w_hi"), m.sem("w_split")
        h_ready, gelu_done, h_hi, h_split = m.sem("h_ready"), m.sem("gelu_done"), m.sem("h_hi"), m.sem("h_split")
        y_ready, y_added = m.sem("y_ready"), m.sem("y_added")
        block = m.block()

        def chunks(eng, body):
            body(0, 0, False)
            body(1, 1, False)
            with eng.Fori(1, CHUNKS // 2 - 1) as i:
                for parity in range(2):
                    body(2 * i + parity, parity, False)
            body(CHUNKS - 2, 0, False)
            body(CHUNKS - 1, 1, True)

        @block.sync
        def _(sp):
            expert = [sp.value_load(chosen[0:1, k:k + 1], min_val=0, max_val=E - 1) for k in range(TOP_K)]
            for k in range(TOP_K):
                sp.dma_start(b2[k][:, :], b2_dram[bass.ds(expert[k], 1), :].partition_broadcast(P)
                             .rearrange("p a n -> p (a n)")).then_inc(b2_loaded, 16)
            for c in range(CHUNKS):
                k, f = c // (CHUNKS // 2), c % (CHUNKS // 2)
                wait(sp, gelu_done, 16 * (c - 1))
                sp.dma_start(b1[:, c % 2, :], b1_dram[bass.ds(expert[k], 1), :, f * TILES:(f + 1) * TILES]
                             .rearrange("a p t -> (a p) t")).then_inc(b1_loaded, 16)
                wait(sp, w_split, 2 * c - 1)
                sp.dma_start(raw[0][:, :, :], w1_dram[bass.ds(expert[k], 1), :, f * N:(f + 1) * N]
                             .rearrange("a (t p) n -> p (a t) n", p=P)).then_inc(w1_loaded, 16)
                wait(sp, w_split, 2 * c)
                sp.dma_start(raw[1][:, :, :], w2_dram[bass.ds(expert[k], 1), f * N:(f + 1) * N, :]
                             .rearrange("a (t p) n -> p (a t) n", p=P)).then_inc(w2_loaded, 16)

        @block.tensor
        def _(pe):
            def hidden_units(c, parity, g):
                for ft in range(STEP_UNITS):
                    unit = 4 * STEP_UNITS * c + STEP_UNITS * g + ft
                    if not (isinstance(c, int) and c == 0 and g == 0):
                        wait(pe, gelu_done, unit - 3)
                    bank = h_ps[ft][:, :]
                    for dt in range(TILES):
                        for i, j in ((0, 0), (0, 1), (1, 0)):
                            last = nc.tensor.matmul(bank, w1[parity][i][:, dt, cols(ft)], xt[j][:, dt, g * N:(g + 1) * N],
                                                    start=(dt, i, j) == (0, 0, 0), stop=(dt, i, j) == (TILES - 1, 1, 0))
                    last.then_inc(h_ready, 1)

            def output_units(c, parity, g):
                pe.wait_ge(h_split, 4 * STEP_UNITS * c + STEP_UNITS * g + STEP_UNITS)
                for nt in range(STEP_UNITS):
                    unit = 4 * STEP_UNITS * c + STEP_UNITS * g + nt
                    if not (isinstance(c, int) and c == 0 and g == 0):
                        wait(pe, y_added, unit - 3)
                    bank = y_ps[nt][:, :]
                    for ft in range(TILES):
                        for i, j in ((0, 0), (0, 1), (1, 0)):
                            last = nc.tensor.matmul(bank, h[g % 2][i][:, ft, cols(nt)], w2[parity][j][:, ft, :],
                                                    start=(ft, i, j) == (0, 0, 0), stop=(ft, i, j) == (TILES - 1, 1, 0))
                    last.then_inc(y_ready, 1)

            def body(c, parity, last):
                pe.wait_ge(w_split, 2 * c + 2)
                hidden_units(c, parity, 0)
                for g in range(GROUPS):
                    if g + 1 < GROUPS:
                        hidden_units(c, parity, g + 1)
                    output_units(c, parity, g)
            chunks(pe, body)

        @block.scalar
        def _(act):
            def split_hi(c, parity):
                for n, (loaded, w) in enumerate(((w1_loaded, w1), (w2_loaded, w2))):
                    act.wait_ge(loaded, 16 * c + 16)
                    if not (isinstance(c, int) and c < 2):
                        wait(act, y_ready, 16 * c - 16)
                    nc.scalar.activation(w[parity][0][:, :, :], raw[n][:, :, :], ACT.Copy).then_inc(w_hi, 1)

            split_hi(0, 0)

            def body(c, parity, last):
                for g in range(GROUPS):
                    if g == 0:
                        act.wait_ge(b1_loaded, 16 * c + 16)
                    for ft in range(STEP_UNITS):
                        unit = 4 * STEP_UNITS * c + STEP_UNITS * g + ft
                        act.wait_ge(h_ready, unit + 1)
                        if not (isinstance(c, int) and c == 0 and g == 0):
                            wait(act, h_split, unit - 3)
                        nc.scalar.activation(hidden[:, ft, :], h_ps[ft][:, :], ACT.Gelu_apprx_tanh,
                                             bias=b1[:, parity, ft:ft + 1])\
                            .then_inc(gelu_done, 1)
                    if g == 1 and not last:
                        split_hi(c + 1, 1 - parity)
            chunks(act, body)

        @block.vector
        def _(dve):
            def split_lo(c, parity):
                for n, w in enumerate((w1, w2)):
                    dve.wait_ge(w_hi, 2 * c + n + 1)
                    nc.vector.tensor_tensor(w[parity][1][:, :, :], raw[n][:, :, :], w[parity][0][:, :, :],
                                            ALU.subtract).then_inc(w_split, 1)

            split_lo(0, 0)
            dve.wait_ge(b2_loaded, 16 * TOP_K)
            for k in range(TOP_K):
                for b in range(B):
                    if k:
                        dve.wait_ge(b2_added, b + 1)
                    nc.vector.scalar_tensor_tensor(out=X[:, b, :], in0=b2[k][:, :],
                                                   scalar=route_gain[:, k * (CHUNKS // 2), b:b + 1], in1=X[:, b, :],
                                                   op0=ALU.mult, op1=ALU.add).then_inc(b2_added, 1)

            def split_hidden(c, g):
                first_step = isinstance(c, int) and c == 0
                for ft in range(STEP_UNITS):
                    unit = 4 * STEP_UNITS * c + STEP_UNITS * g + ft
                    dve.wait_ge(gelu_done, unit + 1)
                    if not (first_step and g < 2):
                        wait(dve, y_ready, 16 * c + 4 * g - 4)
                    nc.vector.tensor_copy(h[g % 2][0][:, ft, :], hidden[:, ft, :]).then_inc(h_hi, 1)
                    dve.wait_ge(h_hi, unit + 1)
                    nc.vector.tensor_tensor(h[g % 2][1][:, ft, :], hidden[:, ft, :], h[g % 2][0][:, ft, :],
                                            ALU.subtract).then_inc(h_split, 1)

            def add_output(c, g):
                for nt in range(STEP_UNITS):
                    b = STEP_UNITS * g + nt
                    dve.wait_ge(y_ready, 16 * c + b + 1)
                    if isinstance(c, int) and c == 0:
                        dve.wait_ge(b2_added, B + b + 1)
                    else:
                        wait(dve, y_added, 16 * c + b - 15)
                    nc.vector.scalar_tensor_tensor(
                        out=X[:, b, :], in0=y_ps[nt][:, :],
                        scalar=route_gain[:, bass.ds(c, 1), b:b + 1].rearrange("p a n -> p (a n)"),
                        in1=X[:, b, :], op0=ALU.mult, op1=ALU.add).then_inc(y_added, 1)

            def body(c, parity, last):
                split_hidden(c, 0)
                for g in range(GROUPS):
                    if g + 1 < GROUPS:
                        split_hidden(c, g + 1)
                    add_output(c, g)
                    if g == 1 and not last:
                        split_lo(c + 1, 1 - parity)
            dve.wait_ge(b2_added, 2 * B)
            chunks(dve, body)
            dve.wait_ge(y_added, 16 * CHUNKS)


D16 = 16
BLOCKS = 4


def head_selectors():
    stack = np.zeros((P, 4, PAIRS, P), np.float32)
    for t in range(PAIRS):
        for r in range(P):
            row, block = D16 * (2 * t + r // 64) + r % D16, r % 64 // D16
            stack[row, block % 2, t, r] = 1
            stack[row, 2 + block // 2, t, r] = 1
    pick = np.zeros((P, 4, P), np.float32)
    for h in range(HEADS):
        for c in range(D16):
            for i in range(2):
                pick[32 * (h % 4) + 16 * i + c, 2 * (h // 4) + i, D16 * h + c] = 1
    heads = np.zeros((P, HEADS), np.float32)
    heads[np.arange(P), np.arange(P) // D16] = 1
    return stack, pick, heads


def stage_unit_heads(nc, ctx_dram, heads_dram, X, mean_rstd, ident, units):
    with ExitStack() as ctx:
        m = Memory(nc, ctx, "uh")
        heads = m.sb("heads", [P, HEADS])
        cx = m.sb("cx", [P, 2, N])
        src = m.sb("src", [P, 2, N])
        square = m.sb("square", [P, 2, N])
        norm = m.sb("norm", [P, 2, B * TILES * HEADS])
        inv = m.sb("inv", [P, 2, B * TILES * HEADS])
        wide = m.sb("wide", [P, 2, N])
        unit = m.sb("unit", [P, 2, N])
        sum_ps = [m.ps(f"sum{i}") for i in range(2)]
        wide_ps = [m.ps(f"wide{i}") for i in range(2)]
        heads_loaded, cx_loaded = m.sem("heads_loaded"), [m.sem(f"cx_loaded{i}") for i in range(2)]
        src_done, square_done, sum_ready = m.sem("src_done"), m.sem("square_done"), m.sem("sum_ready")
        norm_done, sqrt_done, inv_done = m.sem("norm_done"), m.sem("sqrt_done"), m.sem("inv_done")
        wide_done, wide_ready, unit_done = m.sem("wide_done"), m.sem("wide_ready"), m.sem("unit_done")
        hi_done, lo_done = m.sem("hi_done"), m.sem("lo_done")
        block = m.block()
        JOBS = 2 * B

        def source(turn, job):
            b, i = job // 2, job % 2
            return cx[:, b % 2, :] if i else src[:, b % 2, :]

        @block.sync
        def _(sp):
            sp.dma_start(heads[:, :], heads_dram).then_inc(heads_loaded, 16)
            for turn in range(2):
                for b in range(B):
                    if turn == 0:
                        wait(sp, square_done, 2 * (b - 2) + 2)
                    else:
                        sp.wait_ge(square_done, JOBS)
                        wait(sp, unit_done, 2 * (b - 2) + 2)
                    sp.dma_start(cx[:, b % 2, :], ctx_dram[b]).then_inc(cx_loaded[b % 2], 16)

        def wait_source(eng, turn, job):
            b, i = job // 2, job % 2
            if i:
                eng.wait_ge(cx_loaded[b % 2], 16 * (B // 2 * turn + b // 2 + 1))
            else:
                eng.wait_ge(src_done, B * turn + b + 1)

        @block.scalar
        def _(act):
            for job in range(JOBS):
                wait_source(act, 0, job)
                wait(act, sum_ready, job - 1)
                nc.scalar.activation(square[:, job % 2, :], source(0, job), ACT.Square).then_inc(square_done, 1)
            act.wait_ge(norm_done, 2)
            nc.scalar.activation(norm[:, :, :], norm[:, :, :], ACT.Sqrt).then_inc(sqrt_done, 1)
            for job in range(JOBS):
                act.wait_ge(unit_done, job + 1)
                nc.scalar.activation(units[job % 2][0][:, job // 2, :], unit[:, job % 2, :], ACT.Copy).then_inc(hi_done, 1)

        @block.tensor
        def _(pe):
            pe.wait_ge(heads_loaded, 16)
            for job in range(JOBS):
                b, i = job // 2, job % 2
                pe.wait_ge(square_done, job + 1)
                for t in range(TILES):
                    at = (TILES * b + t) * HEADS
                    last = nc.tensor.matmul(sum_ps[i][:, at:at + HEADS], square[:, i, cols(t)], heads[:, :],
                                            start=True, stop=True)
                last.then_inc(sum_ready, 1)
            for job in range(JOBS):
                pe.wait_ge(wide_done, job + 1)
                wait(pe, unit_done, job - 1)
                for t in range(TILES):
                    last = nc.tensor.transpose(wide_ps[job % 2][:, cols(t)], wide[:, job % 2, cols(t)], ident[:, :])
                last.then_inc(wide_ready, 1)

        @block.gpsimd
        def _(pool):
            pool.wait_ge(inv_done, 2)
            for job in range(JOBS):
                b, i = job // 2, job % 2
                wait(pool, wide_ready, job - 1)
                per_head = inv[:, i, TILES * HEADS * b:TILES * HEADS * (b + 1)]
                nc.gpsimd.tensor_copy(wide[:, job % 2, :].rearrange("p (h c) -> p h c", c=D16),
                                      per_head.rearrange("p (h c) -> p h c", c=1).to_broadcast([P, TILES * HEADS, D16]))\
                    .then_inc(wide_done, 1)

        @block.vector
        def _(dve):
            def normalise(turn, b):
                if turn == 0:
                    wait(dve, square_done, 2 * (b - 2) + 1)
                else:
                    dve.wait_ge(square_done, JOBS)
                    wait(dve, unit_done, 2 * (b - 2) + 1)
                nc.vector.tensor_scalar(src[:, b % 2, :], X[:, b, :], mean_rstd[:, b, 0:1], mean_rstd[:, b, 1:2],
                                        ALU.subtract, ALU.mult).then_inc(src_done, 1)

            for b in range(B):
                normalise(0, b)
            dve.wait_ge(sum_ready, JOBS)
            for i in range(2):
                nc.vector.tensor_scalar(norm[:, i, :], sum_ps[i][:, :], 1e-24, None, ALU.max).then_inc(norm_done, 1)
            dve.wait_ge(sqrt_done, 1)
            for i in range(2):
                nc.vector.reciprocal(inv[:, i, :], norm[:, i, :]).then_inc(inv_done, 1)
            normalise(1, 0)
            for job in range(JOBS):
                if job % 2 == 0 and job // 2 + 1 < B:
                    normalise(1, job // 2 + 1)
                wait_source(dve, 1, job)
                dve.wait_ge(wide_ready, job + 1)
                wait(dve, lo_done, job - 1)
                wait(dve, hi_done, job - 1)
                nc.vector.tensor_tensor(unit[:, job % 2, :], wide_ps[job % 2][:, :], source(1, job), ALU.mult)\
                    .then_inc(unit_done, 1)
                dve.wait_ge(hi_done, job + 1)
                dve.wait_ge(unit_done, job + 1)
                nc.vector.tensor_tensor(units[job % 2][1][:, job // 2, :], unit[:, job % 2, :],
                                        units[job % 2][0][:, job // 2, :], ALU.subtract).then_inc(lo_done, 1)


def stage_attention1(nc, ctx_dram, stack_dram, pick_dram, X, gates, ident, units):
    ALPHA = 5.0
    GROUP = HEADS // 2
    STEPS = 2 * TILES
    with ExitStack() as ctx:
        m = Memory(nc, ctx, "a1")
        stack_raw = m.sb("stack_raw", [P, PAIRS * P])
        stack = m.sb("stack", [P, 4, PAIRS, P], BF16)
        pick = m.sb("pick", [P, 4, P])
        cx = m.sb("cx", [P, 2, N])
        k_stack = [m.sb(f"k_stack{i}", [P, PAIRS, N], BF16) for i in range(2)]
        q_stack = [m.sb(f"q_stack{i}", [P, HEADS, N], BF16) for i in range(2)]
        v = [m.sb(f"v{i}", [P, TILES, HEADS, 32]) for i in range(2)]
        prob = m.sb("prob", [P, TILES, GROUP, N])
        summed = m.sb("summed", [P, 2, N])
        inv = m.sb("inv", [P, N])
        attended = m.sb("attended", [P, N])
        sim = [m.ps(f"sim{i}") for i in range(4)]
        av = [m.ps(f"av{i}") for i in range(2)]
        misc = [m.ps(f"misc{i}") for i in range(2)]
        stack_loaded, pick_loaded, cx_loaded = m.sem("stack_loaded"), m.sem("pick_loaded"), m.sem("cx_loaded")
        stack_done, ones_done = m.sem("stack_done"), m.sem("ones_done")
        sim_ready, exp_done, av_ready, av_out = m.sem("sim_ready"), m.sem("exp_done"), m.sem("av_ready"), m.sem("av_out")
        misc_ready, misc_out = m.sem("misc_ready"), m.sem("misc_out")
        x_done = m.sem("x_done")
        block = m.block()

        PREPARE = [("k", t) for t in range(PAIRS)] + [("q", t) for t in range(PAIRS)] + [("v", 0)]
        FINISH = [("pick", 1), ("pick", 0)]
        PLAN = {0: [("k", 0)], 1: [("k", 1)], 2: [("pick", 1)], 3: [("pick", 0), ("k", 2)], 4: [("k", 3), ("q", 0)],
                5: [("q", 1)], 6: [("q", 2), ("v", 0)], 7: [("q", 3)]}
        PER_BATCH = sum(len(x) for x in PLAN.values())
        assert sorted(x for st in range(STEPS) for x in PLAN[st]) == sorted(PREPARE + FINISH)

        def uses(first, last):
            todo = [(st, what, t) for st in range(STEPS) for what, t in PLAN[st]
                    if not (first and what == "pick") and not (last and what != "pick")]
            return [(n, *x) for n, x in enumerate(todo)]

        def use(b, n, first=False):
            return len(PREPARE) + n if first else 2 * len(PREPARE) - PER_BATCH + PER_BATCH * b + n

        def bank(parity, n, first=False):
            return misc[use(parity, n, first) % 2]

        LAST = use(B - 1, len(FINISH))

        def two_by_two(eng, body):
            body(0, 0, True, False)
            with eng.Fori(0, (B - 2) // 2) as i:
                for parity in (1, 0):
                    body(2 * i + 2 - parity, parity, False, False)
            body(B - 1, 1, False, True)

        @block.sync
        def _(sp):
            for i in range(4):
                wait(sp, stack_done, i)
                sp.dma_start(stack_raw[:, :], stack_dram[:, i, :]).then_inc(stack_loaded, 16)
            sp.dma_start(pick[:, :, :], pick_dram).then_inc(pick_loaded, 16)
            sp.dma_start(cx[:, 0, :], ctx_dram[0]).then_inc(cx_loaded, 16)

            def body(b, parity, first, last):
                if not last:
                    sp.wait_ge(misc_ready, use(b, 0, first))
                    sp.dma_start(cx[:, 1 - parity, :], batch_of(ctx_dram, b + 1)).then_inc(cx_loaded, 16)
            two_by_two(sp, body)

        def source(i, half, b):
            return units[i][half][:, bass.ds(b, 1), :].rearrange("p a n -> p (a n)")

        @block.tensor
        def _(pe):
            def prepare(b, parity, what, t, out):
                if what == "v":
                    pe.wait_ge(cx_loaded, 16 * b + 16)
                    for jt in range(TILES):
                        last = nc.tensor.transpose(out[:, cols(jt)], cx[:, parity, cols(jt)], ident[:, :])
                    return last
                i = 0 if what == "q" else 1
                at = 2 if what == "q" else 0
                nc.tensor.matmul(out[:, :], stack[:, at, t, :], source(i, 0, b), start=True, stop=False)
                return nc.tensor.matmul(out[:, :], stack[:, at + 1, t, :], source(i, 1, b), start=False, stop=True)

            def pick_heads(b, i, out):
                pe.wait_ge(av_out, 2 * b + 2)
                for g in range(2):
                    last = nc.tensor.matmul(out[:, :], pick[:, 2 * g + i, :], summed[:, g, :], start=g == 0, stop=g == 1)
                return last

            def scores(b, parity, g, jt):
                for q in range(GROUP):
                    h = GROUP * g + q
                    unit = GROUP * (STEPS * b + TILES * g + jt) + q
                    wait(pe, exp_done, unit - 3)
                    nc.tensor.matmul(sim[q][:, :], k_stack[parity][:, h // 2, cols(jt)], q_stack[parity][:, h, :],
                                     start=True, stop=True).then_inc(sim_ready, 1)

            def values(b, parity, g, jt):
                pe.wait_ge(exp_done, GROUP * (STEPS * b + TILES * g + jt) + GROUP)
                if jt == 0:
                    wait(pe, av_out, 2 * b + g - 1)
                for q in range(GROUP):
                    last = nc.tensor.matmul(av[g][32 * q:32 * q + 32, :], v[parity][:, jt, GROUP * g + q, :],
                                            prob[:, jt, q, :], start=jt == 0, stop=jt == TILES - 1)
                last.then_inc(av_ready, 1)

            pe.wait_ge(stack_done, 4)
            pe.wait_ge(pick_loaded, 16)
            for n, (what, t) in enumerate(PREPARE):
                wait(pe, misc_out, n - 1)
                prepare(0, 0, what, t, misc[n % 2]).then_inc(misc_ready, 1)

            def body(b, parity, first, last):
                pe.wait_ge(misc_out, use(b, 0, first))
                for st in range(STEPS):
                    scores(b, parity, st // TILES, st % TILES)
                    if st:
                        values(b, parity, (st - 1) // TILES, (st - 1) % TILES)
                    elif not first:
                        values(b - 1, 1 - parity, 1, TILES - 1)
                    for n, at, what, t in uses(first, last):
                        if at != st:
                            continue
                        pe.wait_ge(misc_out, use(b, n, first) - 1)
                        if what == "pick":
                            pick_heads(b - 1, t, bank(parity, n, first)).then_inc(misc_ready, 1)
                        else:
                            prepare(b + 1, 1 - parity, what, t, bank(parity, n, first)).then_inc(misc_ready, 1)
            two_by_two(pe, body)
            values(B - 1, 1, 1, TILES - 1)
            for n, (what, t) in enumerate(FINISH):
                pe.wait_ge(misc_out, LAST + n - 1)
                pick_heads(B - 1, t, misc[(LAST + n) % 2]).then_inc(misc_ready, 1)

        @block.scalar
        def _(act):
            def body(b, parity, first, last):
                for st in range(STEPS):
                    for q in range(GROUP):
                        unit = GROUP * (STEPS * b + st) + q
                        act.wait_ge(sim_ready, unit + 1)
                        if q == 0:
                            wait(act, av_ready, STEPS * b + st - 3)
                        nc.scalar.activation(prob[:, st % TILES, q, :], sim[q][:, :], ACT.Exp, scale=ALPHA)\
                            .then_inc(exp_done, 1)
            two_by_two(act, body)

        @block.vector
        def _(dve):
            for i in range(4):
                dve.wait_ge(stack_loaded, 16 * i + 16)
                nc.vector.tensor_copy(stack[:, i, :, :].rearrange("p t n -> p (t n)"), stack_raw[:, :])\
                    .then_inc(stack_done, 1)
            for i in range(2):
                nc.vector.memset(v[i][:, :, :, :], 1.0).then_inc(ones_done, 1)
                nc.vector.memset(q_stack[i][:, :, :], 0.0).then_inc(ones_done, 1)
            dve.wait_ge(ones_done, 4)

            def prepared(parity, what, t, out):
                if what == "k":
                    return nc.vector.tensor_copy(k_stack[parity][:, t, :], out[:, :])
                if what == "q":
                    nc.vector.tensor_copy(q_stack[parity][0:64, 2 * t, :], out[0:64, :]).then_inc(ones_done, 1)
                    return nc.vector.tensor_copy(q_stack[parity][64:128, 2 * t + 1, :], out[64:128, :])
                return nc.vector.tensor_copy(v[parity][:, :, :, 0:D16],
                                             out[:, :].rearrange("p (t h c) -> p t h c", t=TILES, h=HEADS))

            def finished(b, i, out, n):
                if i == 1:
                    nc.vector.reciprocal(inv[:, :], out[:, :]).then_inc(misc_out, 1)
                    return
                dve.wait_ge(misc_out, n)
                nc.vector.tensor_tensor(attended[:, :], out[:, :], inv[:, :], ALU.mult).then_inc(misc_out, 1)
                dve.wait_ge(misc_out, n + 1)
                row = X[:, bass.ds(b, 1), :].rearrange("p a n -> p (a n)")
                nc.vector.scalar_tensor_tensor(out=row, in0=attended[:, :], scalar=gates[:, 1:2], in1=row,
                                               op0=ALU.mult, op1=ALU.add).then_inc(x_done, 1)

            def values_out(b, g):
                dve.wait_ge(av_ready, STEPS * b + TILES * g + TILES)
                nc.vector.tensor_copy(summed[:, g, :], av[g][:, :]).then_inc(av_out, 1)

            for n, (what, t) in enumerate(PREPARE):
                dve.wait_ge(misc_ready, n + 1)
                prepared(0, what, t, misc[n % 2]).then_inc(misc_out, 1)

            def body(b, parity, first, last):
                for st in range(STEPS):
                    if st == 1 and not first:
                        values_out(b - 1, 1)
                    if st == 5:
                        values_out(b, 0)
                    for n, at, what, t in uses(first, last):
                        if at != st:
                            continue
                        dve.wait_ge(misc_ready, use(b, n, first) + 1)
                        if what == "pick":
                            finished(b - 1, t, bank(parity, n, first), use(b, n, first))
                        else:
                            prepared(1 - parity, what, t, bank(parity, n, first)).then_inc(misc_out, 1)
            two_by_two(dve, body)
            values_out(B - 1, 1)
            for n, (what, t) in enumerate(FINISH):
                dve.wait_ge(misc_ready, LAST + n + 1)
                finished(B - 1, t, misc[(LAST + n) % 2], LAST + n)
            dve.wait_ge(x_done, B)


EXPERTS, SLOTS1, HID = 16, 128, 128
ES = EXPERTS * SLOTS1
QUADS = ES // N


def stage_soft_prepare(nc, gamma_dram, beta_dram, scale_dram, mu_dram, w1_dram, w2_dram, X, token_scale, split,
                       x_dram, xln_dram):
    with ExitStack() as ctx:
        m = Memory(nc, ctx, "sp")
        gamma, beta, scale = m.sb("gamma", [P, N]), m.sb("beta", [P, N]), m.sb("scale", [P, 1])
        RING = B // 2
        xln = m.sb("xln", [P, RING, N])
        xln_square = m.sb("xln_square", [P, N])
        stats = m.sb("stats", [P, B, 6])
        moments = m.sb("moments", [P, B, 2])
        spread = m.sb("spread", [P, B, 1])
        rstd = m.sb("rstd", [P, B, 1])
        rstd2 = m.sb("rstd2", [P, B, 1])
        length = m.sb("length", [P, B])
        raw = [[m.sb(f"raw_{x}", [P, TILES, N]) for x in names] for names in (("mu0", "mu1"), ("w1",), ("w2",))]
        square = m.sb("square", [P, TILES, N])
        ones = m.sb("ones", [P, P])
        mu_length = m.sb("mu_length", [P, N])
        mu_inv = m.sb("mu_inv", [P, N])
        sum_ps = m.ps("sum")
        loaded, x_stored = m.sem("loaded"), m.sem("x_stored")
        stored = [m.sem(f"stored{i}") for i in range(4)]
        row_done, moments_done, small, spread_done, sqrt_done = (
            m.sem(x) for x in ("row_done", "moments_done", "small", "spread_done", "sqrt_done"))
        centred, by_gamma, xln_done, squared, clamped = (
            m.sem(x) for x in ("centred", "by_gamma", "xln_done", "squared", "clamped"))
        raw_loaded = [[m.sem(f"raw_loaded_{x}") for x in names] for names in (("mu0", "mu1"), ("w1",), ("w2",))]
        hi_done = [m.sem(f"hi_done_{x}") for x in ("mu", "w1", "w2")]
        lo_done = [m.sem(f"lo_done_{x}") for x in ("mu", "w1", "w2")]
        ones_done, mu_squared, sum_ready, mu_clamped = (
            m.sem(x) for x in ("ones_done", "mu_squared", "sum_ready", "mu_clamped"))
        mu_sqrt_done, mu_inv_done, unit_done = m.sem("mu_sqrt_done"), m.sem("mu_inv_done"), m.sem("unit_done")
        block = m.block()
        MU, W1, W2 = range(3)

        def quad(c):
            return slice(TILES * c, TILES * c + TILES)

        def wait_raw(eng, w, c):
            eng.wait_ge(raw_loaded[w][c % len(raw[w])], 16 * (c // len(raw[w])) + 16)

        def buffer(w, c):
            return raw[w][c % len(raw[w])][:, :, :]

        @block.sync
        def _(sp):
            def load(w, c):
                wait(sp, lo_done[w], c - len(raw[w]) + 1)
                sp.dma_start(buffer(w, c), (mu_dram, w1_dram, w2_dram)[w][:, quad(c), :])\
                    .then_inc(raw_loaded[w][c % len(raw[w])], 16)

            load(MU, 0)
            for c in range(QUADS):
                load(W1, c)
                load(W2, c)
                if c + 1 < QUADS:
                    load(MU, c + 1)
                if c == 0:
                    sp.dma_start(gamma[:, :], gamma_dram.partition_broadcast(P)).then_inc(loaded, 16)
                    sp.dma_start(beta[:, :], beta_dram.partition_broadcast(P)).then_inc(loaded, 16)
                    sp.dma_start(scale[:, :], scale_dram.partition_broadcast(P)).then_inc(loaded, 16)
                    sp.dma_start(x_dram.rearrange("b p n -> p b n"), X[:, :, :]).then_inc(x_stored, 16)
                else:
                    for b in range(4 * c - 4, 4 * c):
                        sp.wait_ge(xln_done, b + 1)
                        sp.dma_start(xln_dram[b], xln[:, b % RING, :]).then_inc(stored[b // 4], 16)
            for b in range(B - 4, B):
                sp.wait_ge(xln_done, b + 1)
                sp.dma_start(xln_dram[b], xln[:, b % RING, :]).then_inc(stored[b // 4], 16)
            sp.wait_ge(x_stored, 16)
            for group in stored:
                sp.wait_ge(group, 64)

        @block.tensor
        def _(pe):
            pe.wait_ge(ones_done, 1)
            for c in range(QUADS):
                pe.wait_ge(mu_squared, c + 1)
                wait(pe, mu_clamped, c)
                for t in range(TILES):
                    last = nc.tensor.matmul(sum_ps[:, :], ones[:, :], square[:, t, :], start=t == 0, stop=t == TILES - 1)
                last.then_inc(sum_ready, 1)

        @block.scalar
        def _(act):
            def split_hi(w, c):
                wait_raw(act, w, c)
                nc.scalar.activation(split[w][0][:, quad(c), :], buffer(w, c), ACT.Copy).then_inc(hi_done[w], 1)

            for n in range(2):
                act.wait_ge(spread_done, n + 1)
                nc.scalar.activation(spread[:, :, :], spread[:, :, :], ACT.Sqrt).then_inc(sqrt_done, 1)
            def square_mu(c):
                wait_raw(act, MU, c)
                wait(act, sum_ready, c)
                nc.scalar.activation(square[:, :, :], buffer(MU, c), ACT.Square).then_inc(mu_squared, 1)

            square_mu(0)
            for c in range(QUADS):
                split_hi(W1, c)
                act.wait_ge(mu_clamped, c + 1)
                nc.scalar.activation(mu_length[:, :], mu_length[:, :], ACT.Sqrt).then_inc(mu_sqrt_done, 1)
                split_hi(W2, c)
                if c + 1 < QUADS:
                    square_mu(c + 1)
                act.wait_ge(unit_done, c + 1)
                split_hi(MU, c)
                for b in range(4 * c, 4 * c + 4):
                    act.wait_ge(xln_done, b + 1)
                    wait(act, squared, b)
                    nc.scalar.activation(xln_square[:, :], xln[:, b % RING, :], ACT.Square, accum_out=length[:, b:b + 1])\
                        .then_inc(squared, 1)
            act.wait_ge(clamped, 1)
            nc.scalar.activation(length[:, :], length[:, :], ACT.Sqrt).then_inc(sqrt_done, 1)

        @block.gpsimd
        def _(pool):
            def plus_beta(b):
                pool.wait_ge(by_gamma, b + 1)
                nc.gpsimd.tensor_tensor(xln[:, b % RING, :], xln[:, b % RING, :], beta[:, :], ALU.add).then_inc(xln_done, 1)

            pool.wait_ge(loaded, 48)
            for b in range(B):
                pool.wait_ge(centred, b + 1)
                nc.gpsimd.tensor_tensor(xln[:, b % RING, :], xln[:, b % RING, :], gamma[:, :], ALU.mult).then_inc(by_gamma, 1)
                if b:
                    plus_beta(b - 1)
            plus_beta(B - 1)

        @block.vector
        def _(dve):
            nc.vector.memset(ones[:, :], 1.0).then_inc(ones_done, 1)
            for b in range(B):
                nc.vector.bn_stats(stats[:, b, :], X[:, b, :]).then_inc(row_done, 1)
            dve.wait_ge(row_done, B)
            for b in range(B):
                nc.vector.bn_aggr(moments[:, b, :], stats[:, b, :]).then_inc(moments_done, 1)
            dve.wait_ge(moments_done, B)
            variance = moments[:, :, 1:2]
            nc.vector.tensor_scalar(spread[:, :, :], variance, LN_EPS, None, ALU.add).then_inc(spread_done, 1)
            dve.wait_ge(sqrt_done, 1)
            nc.vector.reciprocal(rstd[:, :, :], spread[:, :, :]).then_inc(small, 1)
            dve.wait_ge(small, 1)
            nc.vector.tensor_tensor(rstd2[:, :, :], variance, rstd[:, :, :], ALU.mult).then_inc(small, 1)
            dve.wait_ge(small, 2)
            nc.vector.tensor_tensor(rstd2[:, :, :], rstd2[:, :, :], rstd[:, :, :], ALU.mult).then_inc(small, 1)
            dve.wait_ge(small, 3)
            nc.vector.tensor_scalar(spread[:, :, :], rstd2[:, :, :], LN_EPS, None, ALU.add).then_inc(spread_done, 1)
            dve.wait_ge(sqrt_done, 2)
            nc.vector.reciprocal(rstd2[:, :, :], spread[:, :, :]).then_inc(small, 1)
            dve.wait_ge(small, 4)
            nc.vector.tensor_tensor(rstd[:, :, :], rstd[:, :, :], rstd2[:, :, :], ALU.mult).then_inc(small, 1)
            dve.wait_ge(small, 5)

            def centre(b):
                if b >= RING:
                    dve.wait_ge(stored[(b - RING) // 4], 64)
                wait(dve, squared, b - RING + 1)
                nc.vector.tensor_scalar(xln[:, b % RING, :], X[:, b, :], moments[:, b, 0:1], rstd[:, b, :],
                                        ALU.subtract, ALU.mult).then_inc(centred, 1)

            for b in range(RING):
                centre(b)

            def split_lo(w, c):
                dve.wait_ge(hi_done[w], c + 1)
                nc.vector.tensor_tensor(split[w][1][:, quad(c), :], buffer(w, c), split[w][0][:, quad(c), :],
                                        ALU.subtract).then_inc(lo_done[w], 1)

            for c in range(QUADS):
                dve.wait_ge(sum_ready, c + 1)
                nc.vector.tensor_scalar(mu_length[:, :], sum_ps[:, :], 1e-24, None, ALU.max).then_inc(mu_clamped, 1)
                split_lo(W1, c)
                dve.wait_ge(mu_sqrt_done, c + 1)
                nc.vector.reciprocal(mu_inv[:, :], mu_length[:, :]).then_inc(mu_inv_done, 1)
                dve.wait_ge(mu_inv_done, c + 1)
                for t in range(TILES):
                    last = nc.vector.tensor_tensor(raw[MU][c % 2][:, t, :], raw[MU][c % 2][:, t, :], mu_inv[:, :],
                                                   ALU.mult)
                last.then_inc(unit_done, 1)
                split_lo(W2, c)
                split_lo(MU, c)
                if 0 < c < 3:
                    for b in range(RING + 4 * c - 4, RING + 4 * c):
                        centre(b)
            dve.wait_ge(squared, B)
            nc.vector.tensor_scalar(length[:, :], length[:, :], 1e-24, None, ALU.max).then_inc(clamped, 1)
            dve.wait_ge(sqrt_done, 3)
            nc.vector.reciprocal(length[:, :], length[:, :]).then_inc(small, 1)
            dve.wait_ge(small, 6)
            dve.wait_ge(loaded, 48)
            nc.vector.tensor_scalar(token_scale[:, :], length[:, :], scale[:, 0:1], None, ALU.mult).then_inc(small, 1)
            dve.wait_ge(small, 7)


def stage_soft(nc, x_dram, xln_dram, b1_dram, b2_dram, out_dram, gates, ident, token_scale, split, X):
    mu, w1, w2 = split
    with ExitStack() as ctx:
        m = Memory(nc, ctx, "so")
        b1 = m.sb("b1", [P, ES])
        b2 = m.sb("b2", [EXPERTS, N])
        x = m.sb("x", [P, N])
        x_out = m.sb("x_out", [P, N])
        xln = m.sb("xln", [P, N])
        xt = [m.sb(f"xt_{i}", [P, TILES, P], BF16) for i in ("hi", "lo")]
        logits, combine, dispatch_flat, hidden = (X[:, QUADS * i:QUADS * i + QUADS, :].rearrange("p q n -> p (q n)")
                                                  for i in range(4))
        dispatch_t = dispatch_flat.rearrange("p (e n) -> p e n", e=EXPERTS)
        xw = [m.sb(f"xw_{i}", [P, ES], BF16) for i in ("hi", "lo")]
        disp = [m.sb(f"disp_{i}", [P, ES], BF16) for i in ("hi", "lo")]
        comb_t = [m.sb(f"comb_t_{i}", [P, ES], BF16) for i in ("hi", "lo")]
        h = [m.sb(f"h_{i}", [P, ES], BF16) for i in ("hi", "lo")]
        g = [m.sb(f"g_{i}", [P, ES], BF16) for i in ("hi", "lo")]
        neg_scale = m.sb("neg_scale", [P, 1])
        neg_row_max = m.sb("neg_row_max", [P, 1])
        row_sum = m.sb("row_sum", [P, 1])
        out_gain = m.sb("out_gain", [P, 2])
        neg_slot_max = m.sb("neg_slot_max", [P, EXPERTS])
        slot_sum = m.sb("slot_sum", [P, EXPERTS])
        slot_inv = m.sb("slot_inv", [P, EXPERTS])
        comb_sum = m.sb("comb_sum", [P, EXPERTS])
        comb_sum_t = m.sb("comb_sum_t", [EXPERTS, P])
        big = [m.ps(f"big{i}") for i in range(2)]
        tr = [m.ps(f"tr{i}") for i in range(2)]
        small = [m.ps(f"small{i}") for i in range(2)]
        x_ps = m.ps("x_ps")
        out_ps = m.ps("out_ps")

        scale_negated = m.sem("scale_negated")
        b_loaded, x_loaded, xln_loaded, stored = m.sem("b_loaded"), m.sem("x_loaded"), m.sem("xln_loaded"), m.sem("stored")
        xt_ready, xt_hi, xt_lo = m.sem("xt_ready"), m.sem("xt_hi"), m.sem("xt_lo")
        logits_ready, logits_out = m.sem("logits_ready"), m.sem("logits_out")
        xw_ready, xw_hi, xw_lo = m.sem("xw_ready"), m.sem("xw_hi"), m.sem("xw_lo")
        row_max, combine_done = m.sem("row_max"), m.sem("combine_done")
        lt_ready, slot_max, dispatch_done, slot_inverted = m.sem("lt_ready"), m.sem("slot_max"), m.sem("dispatch_done"), m.sem("slot_inverted")
        disp_ready, disp_hi, disp_lo = m.sem("disp_ready"), m.sem("disp_hi"), m.sem("disp_lo")
        comb_ready, comb_hi, comb_lo = m.sem("comb_ready"), m.sem("comb_hi"), m.sem("comb_lo")
        comb_summed, comb_sum_ready, comb_sum_out = m.sem("comb_summed"), m.sem("comb_sum_ready"), m.sem("comb_sum_out")
        h_ready, h_biased, gelu_done, h_hi, h_lo = m.sem("h_ready"), m.sem("h_biased"), m.sem("gelu_done"), m.sem("h_hi"), m.sem("h_lo")
        g_ready, g_hi, g_lo = m.sem("g_ready"), m.sem("g_hi"), m.sem("g_lo")
        out_ready, gain_done, out_done = m.sem("out_ready"), m.sem("gain_done"), m.sem("out_done")
        block = m.block()

        def loop(eng, body):
            body(0)
            with eng.Fori(1, B - 1) as b:
                body(b)

        @block.sync
        def _(sp):
            def store(b):
                sp.wait_ge(out_done, b + 1)
                sp.dma_start(batch_of(out_dram, b), x_out[:, :]).then_inc(stored, 16)

            sp.dma_start(b1[:, :], b1_dram.partition_broadcast(P)).then_inc(b_loaded, 16)
            sp.dma_start(b2[:, :], b2_dram).then_inc(b_loaded, 16)
            sp.dma_start(xln[:, :], xln_dram[0]).then_inc(xln_loaded, 16)
            sp.dma_start(x[:, :], x_dram[0]).then_inc(x_loaded, 16)
            sp.wait_ge(xt_ready, 1)
            sp.dma_start(xln[:, :], xln_dram[1]).then_inc(xln_loaded, 16)

            def next_xln(b):
                sp.wait_ge(xt_ready, b + 2)
                sp.dma_start(xln[:, :], batch_of(xln_dram, b + 2)).then_inc(xln_loaded, 16)

            def store_and_next_x(b):
                store(b)
                sp.wait_ge(stored, 16 * b + 16)
                sp.dma_start(x[:, :], batch_of(x_dram, b + 1)).then_inc(x_loaded, 16)

            def body(b):
                next_xln(b)
                store_and_next_x(b)

            body(0)
            with sp.Fori(1, B - 2) as b:
                body(b)
            store_and_next_x(B - 2)
            store(B - 1)
            sp.wait_ge(stored, 16 * B)

        @block.tensor
        def _(pe):
            def three(out, stat, mov, start=True, stop=True):
                nc.tensor.matmul(out, stat[0], mov[0], start=start, stop=False)
                nc.tensor.matmul(out, stat[0], mov[1], start=False, stop=False)
                return nc.tensor.matmul(out, stat[1], mov[0], start=False, stop=stop)

            def transpose_x(b):
                pe.wait_ge(xln_loaded, 16 * b + 16)
                wait(pe, comb_sum_out, b - 1)
                for t in range(TILES):
                    last = nc.tensor.transpose(x_ps[:, cols(t)], xln[:, cols(t)], ident[:, :])
                last.then_inc(xt_ready, 1)

            def times(weights, c, out):
                for t in range(TILES):
                    last = three(out, [a[:, t, :] for a in xt], [w[:, TILES * c + t, :] for w in weights],
                                 start=t == 0, stop=t == TILES - 1)
                return last

            def make_logits(b, c):
                pe.wait_ge(xt_lo, b + 1)
                if c < 2:
                    wait(pe, xw_lo, 4 * b + c - 1)
                else:
                    pe.wait_ge(logits_out, 4 * b + c - 1)
                times(mu, c, big[c % 2][:, :]).then_inc(logits_ready, 1)

            def make_xw(b, c):
                if c < 2:
                    pe.wait_ge(logits_out, 4 * b + c + 3)
                else:
                    pe.wait_ge(xw_lo, 4 * b + c - 1)
                times(w1, c, big[c % 2][:, :]).then_inc(xw_ready, 1)

            def transpose_logits(b, c):
                pe.wait_ge(logits_out, 4 * b + c + 1)
                if c < 2:
                    wait(pe, comb_lo, 4 * b + c - 1)
                else:
                    pe.wait_ge(dispatch_done, EXPERTS * b + 4 * (c - 1))
                for i in range(4):
                    last = nc.tensor.transpose(tr[c % 2][:, cols(i)], logits[:, cols(4 * c + i)], ident[:, :])
                last.then_inc(lt_ready, 1)

            def transpose_dispatch(b, c):
                pe.wait_ge(dispatch_done, EXPERTS * b + 4 * (c + 3 if c < 2 else c + 1))
                if c >= 2:
                    pe.wait_ge(dispatch_done, EXPERTS * b + EXPERTS)
                    pe.wait_ge(disp_lo, 4 * b + c - 1)
                for i in range(4):
                    last = nc.tensor.transpose(tr[c % 2][:, cols(i)], dispatch_t[:, 4 * c + i, :], ident[:, :])
                last.then_inc(disp_ready, 1)

            def transpose_combine(b, c):
                pe.wait_ge(combine_done, b + 1)
                if c < 2:
                    pe.wait_ge(disp_lo, 4 * b + c + 3)
                else:
                    pe.wait_ge(comb_lo, 4 * b + c - 1)
                for i in range(4):
                    last = nc.tensor.transpose(tr[c % 2][:, cols(i)], combine[:, cols(4 * c + i)], ident[:, :])
                last.then_inc(comb_ready, 1)

            def make_h(b, c):
                pe.wait_ge(disp_lo, 4 * b + c + 1)
                pe.wait_ge(xw_lo, 4 * b + c + 1)
                if c < 2:
                    wait(pe, g_lo, 4 * b + c - 1)
                else:
                    pe.wait_ge(h_biased, EXPERTS * b + 4 * (c - 1))
                for i in range(4):
                    e = 4 * c + i
                    last = three(small[c % 2][:, cols(i)], [a[:, cols(e)] for a in disp], [a[:, cols(e)] for a in xw])
                last.then_inc(h_ready, 1)

            def make_g(b, c):
                pe.wait_ge(h_lo, 4 * b + c + 1)
                pe.wait_ge(comb_lo, 4 * b + c + 1)
                if c < 2:
                    pe.wait_ge(h_biased, EXPERTS * b + 4 * (c + 3))
                else:
                    pe.wait_ge(g_lo, 4 * b + c - 1)
                for i in range(4):
                    e = 4 * c + i
                    last = three(small[c % 2][:, cols(i)], [a[:, cols(e)] for a in h], [a[:, cols(e)] for a in comb_t])
                last.then_inc(g_ready, 1)

            def transpose_sums(b, xts):
                pe.wait_ge(comb_summed, b + 1)
                pe.wait_ge(xt_lo, xts)
                nc.tensor.transpose(x_ps[0:EXPERTS, 0:P], comb_sum[:, :], ident[:, :]).then_inc(comb_sum_ready, 1)

            def make_out(b, c):
                if c == 0:
                    pe.wait_ge(comb_sum_out, b + 1)
                    wait(pe, out_done, b)
                    nc.tensor.matmul(out_ps[:, :], comb_sum_t[:, :], b2[:, :], start=True, stop=False)
                pe.wait_ge(g_lo, 4 * b + c + 1)
                for e in range(4 * c, 4 * c + 4):
                    last = three(out_ps[:, :], [a[:, cols(e)] for a in g], [w[:, e, :] for w in w2],
                                 start=False, stop=e == EXPERTS - 1)
                if c == QUADS - 1:
                    last.then_inc(out_ready, 1)

            pe.wait_ge(b_loaded, 32)
            transpose_x(0)
            for c in range(QUADS):
                make_logits(0, c)
            for c in range(QUADS):
                make_xw(0, c)
            for c in range(QUADS):
                transpose_logits(0, c)

            def body(b):
                transpose_x(b + 1)
                transpose_dispatch(b, 0)
                transpose_dispatch(b, 1)
                make_logits(b + 1, 0)
                transpose_dispatch(b, 2)
                make_logits(b + 1, 1)
                transpose_dispatch(b, 3)
                make_logits(b + 1, 2)
                make_logits(b + 1, 3)
                transpose_combine(b, 0)
                transpose_combine(b, 1)
                make_h(b, 0)
                make_xw(b + 1, 0)
                transpose_combine(b, 2)
                make_h(b, 1)
                make_xw(b + 1, 1)
                transpose_combine(b, 3)
                make_h(b, 2)
                make_xw(b + 1, 2)
                make_h(b, 3)
                transpose_sums(b, b + 2)
                transpose_logits(b + 1, 0)
                transpose_logits(b + 1, 1)
                make_g(b, 0)
                make_g(b, 1)
                make_xw(b + 1, 3)
                make_out(b, 0)
                transpose_logits(b + 1, 2)
                make_g(b, 2)
                make_out(b, 1)
                transpose_logits(b + 1, 3)
                make_g(b, 3)
                make_out(b, 2)
                make_out(b, 3)
            loop(pe, body)
            for c in range(QUADS):
                transpose_dispatch(B - 1, c)
            for c in range(QUADS):
                transpose_combine(B - 1, c)
            for c in range(QUADS):
                make_h(B - 1, c)
            transpose_sums(B - 1, B)
            for c in range(QUADS):
                make_g(B - 1, c)
            for c in range(QUADS):
                make_out(B - 1, c)

        @block.scalar
        def _(act):
            def hi(ready, count, out, bank, done):
                act.wait_ge(ready, count)
                nc.scalar.activation(out, bank, ACT.Copy).then_inc(done, 1)

            def x_hi(b):
                wait(act, xw_ready, 4 * b)
                hi(xt_ready, b + 1, xt[0][:, :, :].rearrange("p t n -> p (t n)"), x_ps[:, :], xt_hi)

            def scale_logits(b, c):
                wait(act, lt_ready, 4 * b)
                wait(act, row_max, b)
                if c == 0:
                    act.wait_ge(scale_negated, b + 1)
                act.wait_ge(logits_ready, 4 * b + c + 1)
                nc.scalar.activation(logits[:, cols(c, N)], big[c % 2][:, :], ACT.Copy,
                                     scale=neg_scale[:, :]).then_inc(logits_out, 1)

            def xw_hi_out(b, c):
                wait(act, h_ready, 4 * (b - 1) + c + 1)
                hi(xw_ready, 4 * b + c + 1, xw[0][:, cols(c, N)], big[c % 2][:, :], xw_hi)

            def disp_hi_out(b, c):
                wait(act, h_ready, 4 * (b - 1) + c + 1)
                hi(disp_ready, 4 * b + c + 1, disp[0][:, cols(c, N)], tr[c % 2][:, :], disp_hi)

            def comb_hi_out(b, c):
                wait(act, g_ready, 4 * (b - 1) + c + 1)
                hi(comb_ready, 4 * b + c + 1, comb_t[0][:, cols(c, N)], tr[c % 2][:, :], comb_hi)

            def gelu(b, c):
                act.wait_ge(h_biased, EXPERTS * b + 4 * c + 4)
                nc.scalar.activation(hidden[:, cols(c, N)], hidden[:, cols(c, N)], ACT.Gelu).then_inc(gelu_done, 1)

            def g_hi_out(b, c):
                wait(act, out_ready, b)
                hi(g_ready, 4 * b + c + 1, g[0][:, cols(c, N)], small[c % 2][:, :], g_hi)

            def exp_combine(b):
                act.wait_ge(row_max, b + 1)
                wait(act, comb_ready, 4 * b)
                wait(act, comb_summed, b)
                wait(act, gain_done, 2 * b)
                nc.scalar.activation(combine[:, :], logits[:, :], ACT.Exp, bias=neg_row_max[:, :], scale=-1.0,
                                     accum_out=row_sum[:, :]).then_inc(combine_done, 1)

            def exp_dispatch(b, c):
                act.wait_ge(slot_max, 4 * b + c + 1)
                wait(act, disp_ready, 4 * b)
                wait(act, slot_inverted, 4 * b)
                for i in range(4):
                    e = 4 * c + i
                    nc.scalar.activation(dispatch_t[:, e, :], tr[c % 2][:, cols(i)], ACT.Exp,
                                         bias=neg_slot_max[:, e:e + 1], scale=-1.0,
                                         accum_out=slot_sum[:, e:e + 1]).then_inc(dispatch_done, 1)

            x_hi(0)
            for c in range(QUADS):
                scale_logits(0, c)
            for c in range(QUADS):
                xw_hi_out(0, c)
            exp_combine(0)
            for c in range(QUADS):
                exp_dispatch(0, c)

            def body(b):
                x_hi(b + 1)
                disp_hi_out(b, 0)
                disp_hi_out(b, 1)
                scale_logits(b + 1, 0)
                disp_hi_out(b, 2)
                scale_logits(b + 1, 1)
                disp_hi_out(b, 3)
                scale_logits(b + 1, 2)
                scale_logits(b + 1, 3)
                comb_hi_out(b, 0)
                comb_hi_out(b, 1)
                xw_hi_out(b + 1, 0)
                comb_hi_out(b, 2)
                gelu(b, 0)
                xw_hi_out(b + 1, 1)
                comb_hi_out(b, 3)
                gelu(b, 1)
                xw_hi_out(b + 1, 2)
                gelu(b, 2)
                gelu(b, 3)
                exp_dispatch(b + 1, 0)
                g_hi_out(b, 0)
                g_hi_out(b, 1)
                exp_dispatch(b + 1, 1)
                xw_hi_out(b + 1, 3)
                exp_dispatch(b + 1, 2)
                g_hi_out(b, 2)
                exp_dispatch(b + 1, 3)
                g_hi_out(b, 3)
                exp_combine(b + 1)
            loop(act, body)
            for c in range(QUADS):
                disp_hi_out(B - 1, c)
            for c in range(QUADS):
                comb_hi_out(B - 1, c)
            for c in range(QUADS):
                gelu(B - 1, c)
            for c in range(QUADS):
                g_hi_out(B - 1, c)

        @block.vector
        def _(dve):
            def lo(hi_done, count, out, bank, hi, done):
                dve.wait_ge(hi_done, count)
                nc.vector.tensor_tensor(out, bank, hi, ALU.subtract).then_inc(done, 1)

            def x_lo(b):
                lo(xt_hi, b + 1, *[t[:, :, :].rearrange("p t n -> p (t n)") for t in (xt[1],)], x_ps[:, :],
                   xt[0][:, :, :].rearrange("p t n -> p (t n)"), xt_lo)

            def quad_lo(hi_done, b, c, dst, bank, done):
                lo(hi_done, 4 * b + c + 1, dst[1][:, cols(c, N)], bank[c % 2][:, :], dst[0][:, cols(c, N)], done)

            def max_of_rows(b):
                dve.wait_ge(logits_out, 4 * b + 4)
                wait(dve, combine_done, b)
                nc.vector.tensor_reduce(neg_row_max[:, :], logits[:, :], AX_X, ALU.min).then_inc(row_max, 1)

            def max_of_slots(b, c):
                dve.wait_ge(lt_ready, 4 * b + c + 1)
                wait(dve, dispatch_done, EXPERTS * b)
                nc.vector.tensor_reduce(neg_slot_max[:, 4 * c:4 * c + 4], tr[c % 2][:, :].rearrange("p (i n) -> p i n", i=4),
                                        AX_X, ALU.min).then_inc(slot_max, 1)

            def sum_combine(b):
                dve.wait_ge(combine_done, b + 1)
                wait(dve, comb_sum_ready, b)
                nc.vector.tensor_reduce(comb_sum[:, :], combine[:, :].rearrange("p (e s) -> p e s", e=EXPERTS), AX_X, ALU.add)\
                    .then_inc(comb_summed, 1)

            def sums_out(b):
                dve.wait_ge(comb_sum_ready, b + 1)
                wait(dve, out_ready, b)
                nc.vector.tensor_copy(comb_sum_t[:, :], x_ps[0:EXPERTS, 0:P]).then_inc(comb_sum_out, 1)

            def bias_h(b, c):
                e = 4 * c
                if c == 0:
                    dve.wait_ge(dispatch_done, EXPERTS * b + EXPERTS)
                    wait(dve, h_biased, EXPERTS * b)
                    nc.vector.reciprocal(slot_inv[:, :], slot_sum[:, :]).then_inc(slot_inverted, 4)
                    dve.wait_ge(slot_inverted, 4 * b + 4)
                dve.wait_ge(h_ready, 4 * b + c + 1)
                wait(dve, h_lo, 4 * (b - 1) + c + 1)
                for i in range(4):
                    nc.vector.scalar_tensor_tensor(out=hidden[:, cols(e + i)], in0=small[c % 2][:, cols(i)],
                                                   scalar=slot_inv[:, e + i:e + i + 1], in1=b1[:, cols(e + i)],
                                                   op0=ALU.mult, op1=ALU.add).then_inc(h_biased, 1)

            def split_h(b, c):
                dve.wait_ge(gelu_done, 4 * b + c + 1)
                wait(dve, g_ready, 4 * (b - 1) + c + 1)
                nc.vector.tensor_copy(h[0][:, cols(c, N)], hidden[:, cols(c, N)]).then_inc(h_hi, 1)
                lo(h_hi, 4 * b + c + 1, h[1][:, cols(c, N)], hidden[:, cols(c, N)], h[0][:, cols(c, N)], h_lo)

            def finish(b):
                dve.wait_ge(combine_done, b + 1)
                wait(dve, out_done, b)
                nc.vector.reciprocal(out_gain[:, 0:1], row_sum[:, :]).then_inc(gain_done, 1)
                dve.wait_ge(gain_done, 2 * b + 1)
                nc.vector.tensor_scalar(out_gain[:, 1:2], out_gain[:, 0:1], gates[:, 3:4], None, ALU.mult)\
                    .then_inc(gain_done, 1)

            def add_out(b):
                dve.wait_ge(out_ready, b + 1)
                dve.wait_ge(gain_done, 2 * b + 2)
                dve.wait_ge(x_loaded, 16 * b + 16)
                nc.vector.scalar_tensor_tensor(out=x_out[:, :], in0=out_ps[:, :], scalar=out_gain[:, 1:2], in1=x[:, :],
                                               op0=ALU.mult, op1=ALU.add).then_inc(out_done, 1)

            def negate_scale(b):
                wait(dve, logits_out, 4 * b)
                nc.vector.tensor_scalar(neg_scale[:, :], token_scale[:, bass.ds(b, 1)], -1.0, None, ALU.mult)\
                    .then_inc(scale_negated, 1)

            negate_scale(0)
            x_lo(0)
            max_of_rows(0)
            for c in range(QUADS):
                quad_lo(xw_hi, 0, c, xw, big, xw_lo)
            for c in range(QUADS):
                max_of_slots(0, c)
            dve.wait_ge(b_loaded, 32)

            def body(b):
                negate_scale(b + 1)
                x_lo(b + 1)
                for c in range(QUADS):
                    quad_lo(disp_hi, b, c, disp, tr, disp_lo)
                    if c == 1:
                        wait(dve, out_ready, b)
                        if not (isinstance(b, int) and b == 0):
                            add_out(b - 1)
                        finish(b)
                        sum_combine(b)
                quad_lo(comb_hi, b, 0, comb_t, tr, comb_lo)
                quad_lo(comb_hi, b, 1, comb_t, tr, comb_lo)
                bias_h(b, 0)
                quad_lo(xw_hi, b + 1, 0, xw, big, xw_lo)
                quad_lo(comb_hi, b, 2, comb_t, tr, comb_lo)
                bias_h(b, 1)
                quad_lo(xw_hi, b + 1, 1, xw, big, xw_lo)
                split_h(b, 0)
                quad_lo(comb_hi, b, 3, comb_t, tr, comb_lo)
                bias_h(b, 2)
                quad_lo(xw_hi, b + 1, 2, xw, big, xw_lo)
                split_h(b, 1)
                bias_h(b, 3)
                sums_out(b)
                split_h(b, 2)
                max_of_slots(b + 1, 0)
                max_of_slots(b + 1, 1)
                split_h(b, 3)
                quad_lo(g_hi, b, 0, g, small, g_lo)
                quad_lo(g_hi, b, 1, g, small, g_lo)
                quad_lo(xw_hi, b + 1, 3, xw, big, xw_lo)
                max_of_slots(b + 1, 2)
                quad_lo(g_hi, b, 2, g, small, g_lo)
                max_of_slots(b + 1, 3)
                max_of_rows(b + 1)
                quad_lo(g_hi, b, 3, g, small, g_lo)
            loop(dve, body)
            for c in range(QUADS):
                quad_lo(disp_hi, B - 1, c, disp, tr, disp_lo)
            add_out(B - 2)
            finish(B - 1)
            sum_combine(B - 1)
            for c in range(QUADS):
                quad_lo(comb_hi, B - 1, c, comb_t, tr, comb_lo)
            for c in range(QUADS):
                bias_h(B - 1, c)
            for c in range(QUADS):
                split_h(B - 1, c)
            sums_out(B - 1)
            for c in range(QUADS):
                quad_lo(g_hi, B - 1, c, g, small, g_lo)
            add_out(B - 1)
            dve.wait_ge(out_done, B)


def program(nc, ins, out, stages=9):
    with ExitStack() as ctx:
        m = Memory(nc, ctx, "all")
        gates = m.sb("gates", [P, 4])
        ident = m.sb("ident", [P, P])
        token_scale = m.sb("token_scale", [P, B])
        loaded = m.sem("ident_loaded")
        x_dram = nc.dram_tensor("x_between", (B, P, N), F32, kind="Internal").ap()
        xln_dram = nc.dram_tensor("xln_between", (B, P, N), F32, kind="Internal").ap()
        with nc.Block() as block:
            @block.sync
            def _(sp):
                sp.dma_start(ident[:, :], ins["ident"]).then_inc(loaded, 16)
                sp.wait_ge(loaded, 16)
        with ExitStack() as resident:
            mr = Memory(nc, resident, "resident")
            X = mr.sb("x", [P, B, N])
            stats = mr.sb("stats", [P, B, 6])
            mean_rstd = mr.sb("mean_rstd", [P, B, 2])
            stage_load(nc, ins["x"], ins["gates"], X, stats, mean_rstd, gates)
            if stages >= 1:
                stage_attention0(nc, ins["wq"], ins["wkv"], ins["wout"], ins["bout"], ins["ctx"], X, mean_rstd, gates, ident)
            if stages >= 2:
                with ExitStack() as stage2:
                    m2 = Memory(nc, stage2, "xt")
                    xt = [m2.sb(f"xt_{x}", [P, TILES, TOKENS], BF16) for x in ("hi", "lo")]
                    chosen = m2.sb("chosen", [P, TOP_K], mybir.dt.int32)
                    route_gain = m2.sb("route_gain", [P, CHUNKS, B])
                    row_statistics(nc, "ln1", X, stats, mean_rstd)
                    stage_route(nc, ins["gate"], ins["iota"], X, xt, mean_rstd, gates, ident, chosen, route_gain)
                    stage_ffn0(nc, ins["w1"], ins["b1"], ins["w2"], ins["b2"], X, xt, chosen, route_gain)
            if stages >= 3:
                with ExitStack() as stage3:
                    m3 = Memory(nc, stage3, "unit_heads")
                    units = [[m3.sb(f"{t}_{x}", [P, B, N], BF16) for x in ("hi", "lo")] for t in ("q", "k")]
                    row_statistics(nc, "ln2", X, stats, mean_rstd)
                    stage_unit_heads(nc, ins["ctx"], ins["heads"], X, mean_rstd, ident, units)
                    stage_attention1(nc, ins["ctx"], ins["stack"], ins["pick"], X, gates, ident, units)
            if stages < 4:
                stored = m.sem("stored")
                with nc.Block() as block:
                    @block.sync
                    def _(sp):
                        sp.dma_start(out.rearrange("b p n -> p b n"), X[:, :, :]).then_inc(stored, 16)
                        sp.wait_ge(stored, 16)
                return
            m4 = Memory(nc, resident, "soft")
            split = [[m4.sb(f"{t}_{x}", [P, EXPERTS, N], BF16) for x in ("hi", "lo")] for t in ("mu", "w1", "w2")]
            stage_soft_prepare(nc, ins["gamma"], ins["beta"], ins["scale"], ins["mu"], ins["soft_w1"], ins["soft_w2"], X,
                               token_scale, split, x_dram, xln_dram)
            stage_soft(nc, x_dram, xln_dram, ins["soft_b1"], ins["soft_b2"], out, gates, ident, token_scale, split, X)


def pieces(w):
    return np.ascontiguousarray(w.reshape(TILES, P, QUADS, N).transpose(1, 2, 0, 3).reshape(P, QUADS * TILES, N))


def layouts(i):
    a = {k: np.ascontiguousarray(np.asarray(v)) for k, v in i.items()}
    stack, pick, heads = head_selectors()
    return {
        "x": a["x"], "ctx": a["ctx_2048"],
        "gates": np.concatenate([a["g_xattn"], a["g_ffn"]])[None, :],
        "ident": np.eye(P, dtype=np.float32),
        "wq": np.ascontiguousarray(a["L0_xattn_Wq"].T), "wkv": np.ascontiguousarray(a["L0_xattn_Wkv"].T),
        "wout": np.ascontiguousarray(a["L0_xattn_Wout"].T.reshape(PAIRS, P, P).transpose(1, 0, 2).reshape(P, N)),
        "bout": a["L0_xattn_bout"][:, None],
        "stack": stack.reshape(P, 4, PAIRS * P), "pick": pick, "heads": heads,
        "gamma": a["L1_ffn_gamma"][None, :], "beta": a["L1_ffn_beta"][None, :], "scale": a["L1_ffn_scale"][None, :],
        "mu": pieces(a["L1_ffn_mu"].reshape(N, ES)),
        "soft_w1": pieces(a["L1_ffn_W1"].transpose(1, 0, 2).reshape(N, ES)),
        "soft_w2": np.ascontiguousarray(a["L1_ffn_W2"].transpose(1, 0, 2)),
        "soft_b1": a["L1_ffn_b1"].reshape(1, ES), "soft_b2": a["L1_ffn_b2"],
        "gate": np.ascontiguousarray(a["L0_ffn_gate_w"].T.reshape(TILES, P, E).transpose(1, 0, 2)),
        "iota": np.arange(E, dtype=np.float32)[None, :],
        "w1": a["L0_ffn_w1"], "w2": a["L0_ffn_w2"], "b2": a["L0_ffn_b2"],
        "b1": np.ascontiguousarray(a["L0_ffn_b1"].reshape(E, DFF // P, P).transpose(0, 2, 1)),
    }


OUT_SHAPE = (B, P, N)


def kernel(**inputs):
    import concourse.bacc as _bacc
    from concourse.bass_utils import run_bass_kernel_spmd as _run

    arrays = {f"in_{name}_dram": a for name, a in layouts(inputs).items()}
    nc = _bacc.Bacc("TRN2", target_bir_lowering=False, num_devices=1)
    ins = {name[3:-5]: nc.dram_tensor(name, a.shape, mybir.dt.from_np(a.dtype), kind="ExternalInput").ap()
           for name, a in arrays.items()}
    out = nc.dram_tensor("out_0_dram", OUT_SHAPE, F32, kind="ExternalOutput").ap()
    program(nc, ins, out)
    r = _run(nc, [arrays], core_ids=[0])
    return r.results[0]["out_0_dram"]
```

```python
from contextlib import ExitStack

import numpy as np
import concourse.bass as bass
from concourse import mybir

F32 = mybir.dt.float32
BF16 = mybir.dt.bfloat16
ALU = mybir.AluOpType
ACT = mybir.ActivationFunctionType
AX_X = mybir.AxisListType.X

B, P, N = 16, 128, 512
HEADS = 8
PAIRS = HEADS // 2
TILES = N // P
LN_EPS = 1e-5


def wait(eng, sem, value):
    if not (isinstance(value, int) and value <= 0):
        eng.wait_ge(sem, value)


def batches(eng, body):
    body(0, True, False)
    with eng.Fori(1, B - 1) as b:
        body(b, False, False)
    body(B - 1, False, True)


def cols(t, width=P):
    return slice(t * width, (t + 1) * width)


class Memory:

    def __init__(self, nc, ctx, stage):
        self.nc, self.ctx, self.stage, self.sems = nc, ctx, stage, []

    def sb(self, name, shape, dt=F32):
        return self.ctx.enter_context(self.nc.sbuf_tensor(f"{self.stage}_{name}", shape, dt))

    def ps(self, name):
        return self.ctx.enter_context(self.nc.psum_tensor(f"{self.stage}_{name}", [P, N], F32))

    def sem(self, name):
        self.sems.append(self.ctx.enter_context(self.nc.semaphore(f"{self.stage}_{name}")))
        return self.sems[-1]

    def block(self):
        self.ctx.callback(self.clear)
        return self.ctx.enter_context(self.nc.Block())

    def clear(self):
        with self.nc.Block() as block:
            @block.sync
            def _(sp):
                for sem in self.sems:
                    sp.sem_clear(sem)


def batch_of(dram, b):
    return dram[bass.ds(b, 1)].rearrange("a p n -> (a p) n")


def stage_load(nc, x_dram, gates_dram, ident_dram, X, mean_rstd, gates, ident):
    PARTS = 4
    with ExitStack() as ctx:
        m = Memory(nc, ctx, "load")
        raw_gates = m.sb("raw_gates", [P, 4])
        stats = m.sb("stats", [P, B, 6])
        x_loaded = [m.sem(f"x_loaded{q}") for q in range(PARTS)]
        gates_loaded, ident_loaded, gates_done = m.sem("gates_loaded"), m.sem("ident_loaded"), m.sem("gates_done")
        statistics = RowStatistics(m)
        block = m.block()

        @block.sync
        def _(sp):
            for q in range(PARTS):
                batches_q = slice(q * B // PARTS, (q + 1) * B // PARTS)
                sp.dma_start(X[:, batches_q, :], x_dram[batches_q].rearrange("b p n -> p b n")).then_inc(x_loaded[q], 16)
            sp.dma_start(raw_gates[:, :], gates_dram.partition_broadcast(P)).then_inc(gates_loaded, 16)
            sp.dma_start(ident[:, :], ident_dram).then_inc(ident_loaded, 16)
            sp.wait_ge(ident_loaded, 16)

        @block.scalar
        def _(act):
            act.wait_ge(gates_loaded, 16)
            nc.scalar.activation(gates[:, :], raw_gates[:, :], ACT.Tanh).then_inc(gates_done, 1)
            act.wait_ge(gates_done, 1)
            statistics.square_root(nc, act)

        @block.vector
        def _(dve):
            for b in range(B):
                if b % (B // PARTS) == 0:
                    dve.wait_ge(x_loaded[b // (B // PARTS)], 16)
                nc.vector.bn_stats(stats[:, b, :], X[:, b, :]).then_inc(statistics.row_done, 1)
            dve.wait_ge(statistics.row_done, B)
            statistics.finish(nc, dve, stats, mean_rstd)


class RowStatistics:

    def __init__(self, m):
        self.moments = m.sb("moments", [P, B, 2])
        self.spread = m.sb("spread", [P, B, 1])
        self.row_done, self.moments_done, self.eps_added, self.sqrt_done, self.rstd_done = (
            m.sem(x) for x in ("row_done", "moments_done", "eps_added", "sqrt_done", "rstd_done"))

    def finish(self, nc, dve, stats, mean_rstd):
        for b in range(B):
            nc.vector.bn_aggr(self.moments[:, b, :], stats[:, b, :]).then_inc(self.moments_done, 1)
        dve.wait_ge(self.moments_done, B)
        nc.vector.tensor_scalar(self.spread[:, :, :], self.moments[:, :, 1:2], LN_EPS, None, ALU.add)\
            .then_inc(self.eps_added, 1)
        nc.vector.tensor_copy(mean_rstd[:, :, 0:1], self.moments[:, :, 0:1]).then_inc(self.rstd_done, 1)
        dve.wait_ge(self.sqrt_done, 1)
        nc.vector.reciprocal(mean_rstd[:, :, 1:2], self.spread[:, :, :]).then_inc(self.rstd_done, 1)
        dve.wait_ge(self.rstd_done, 2)

    def square_root(self, nc, act):
        act.wait_ge(self.eps_added, 1)
        nc.scalar.activation(self.spread[:, :, :], self.spread[:, :, :], ACT.Sqrt).then_inc(self.sqrt_done, 1)


def stage_attention0(nc, wq_dram, wkv_dram, wout_dram, bout_dram, ctx_dram, X, stats, mean_rstd, gates, ident):
    UNITS = 2 * TILES
    SLOTS = PAIRS * B
    STACK = 12 * 16
    VALUE_UNITS = (2, 4, 6, 7)
    DVE_TURNS = (3,)
    ACT_TURNS = tuple(u for u in range(UNITS) if u not in DVE_TURNS)
    with ExitStack() as ctx:
        m = Memory(nc, ctx, "a0")
        w_raw = m.sb("w_raw", [P, 4 * N])
        WQ, WKV, WO = slice(0, N), slice(N, 3 * N), slice(3 * N, 4 * N)
        wq = [m.sb(f"wq_{x}", [P, N], BF16) for x in ("hi", "lo")]
        wkv = [m.sb(f"wkv_{x}", [P, 2 * N], BF16) for x in ("hi", "lo")]
        wo = [m.sb(f"wo_{x}", [P, PAIRS, P], BF16) for x in ("hi", "lo")]
        bout = m.sb("bout", [P, 1])
        gated_bout = m.sb("gated_bout", [P, 1])
        xn = m.sb("xn", [P, N])
        xn_s = [m.sb(f"xn_{x}", [P, N], BF16) for x in ("hi", "lo")]
        cx = m.sb("cx", [P, N])
        cx_s = [m.sb(f"cx_{x}", [P, N], BF16) for x in ("hi", "lo")]
        q_nat = [[m.sb(f"q_nat_{x}{i}", [P, N], BF16) for x in ("hi", "lo")] for i in range(2)]
        k_nat = [[m.sb(f"k_nat_{x}{i}", [P, N], BF16) for x in ("hi", "lo")] for i in range(2)]
        q_hi2 = m.sb("q_hi2", [P, HEADS, N], BF16)
        q_lo2 = m.sb("q_lo2", [P, HEADS, N], BF16)
        k_hilo = m.sb("k_hilo", [P, HEADS, N], BF16)
        v = m.sb("v", [P, PAIRS, TILES, P])
        prob = m.sb("prob", [P, 2, 2, TILES, N])
        prob_t = m.sb("prob_t", [P, 2, 2, TILES, N])
        neg_max = m.sb("neg_max", [P, 2 * UNITS])
        denom = m.sb("denom", [P, 2 * UNITS])
        inv = m.sb("inv", [P, 2 * UNITS])
        o_s = [m.sb(f"o_{x}", [P, PAIRS, N], BF16) for x in ("hi", "lo")]
        x_biased = m.sb("x_biased", [P, N])
        sim = [m.ps(f"sim{i}") for i in range(4)]
        tr = [m.ps(f"tr{i}") for i in range(2)]
        av = m.ps("av")
        misc = m.ps("misc")

        w_loaded = [m.sem(f"w_loaded{i}") for i in range(4)]
        w_split = m.sem("w_split")
        cx_loaded = m.sem("cx_loaded")
        xn_done = m.sem("xn_done")
        hi_done = m.sem("hi_done")
        cxhi_done = m.sem("cxhi_done")
        x_lo_done, ctx_lo_done = m.sem("x_lo_done"), m.sem("ctx_lo_done")
        q_ready, k_ready, v_ready = m.sem("q_ready"), m.sem("k_ready"), m.sem("v_ready")
        q_hi_out, k_hi_out = m.sem("q_hi_out"), m.sem("k_hi_out")
        q_lo_out, k_lo_out, v_out = m.sem("q_lo_out"), m.sem("k_lo_out"), m.sem("v_out")
        stacked = [m.sem(f"stacked{p}") for p in range(PAIRS)]
        sim_ready, max_ready, exp_done = m.sem("sim_ready"), m.sem("max_ready"), m.sem("exp_done")
        inv_done, norm_done = m.sem("inv_done"), m.sem("norm_done")
        tr_ready, tr_out_act, tr_out_dve = m.sem("tr_ready"), m.sem("tr_out_act"), m.sem("tr_out_dve")
        av_ready, o_hi_out, o_lo_out = m.sem("av_ready"), m.sem("o_hi_out"), m.sem("o_lo_out")
        proj_ready, xb_done, x_done = m.sem("proj_ready"), m.sem("xb_done"), m.sem("x_done")
        stats_done = m.sem("stats_done")
        block = m.block()

        def turns_before(turns, unit):
            return sum(t < unit for t in turns)

        def wait_tr_out(eng, s, u):
            if u in DVE_TURNS:
                wait(eng, tr_out_dve, s * len(DVE_TURNS) + turns_before(DVE_TURNS, u) + 1)
            else:
                wait(eng, tr_out_act, s * len(ACT_TURNS) + turns_before(ACT_TURNS, u) + 1)

        @block.sync
        def _(sp):
            sp.dma_start(w_raw[:, WQ], wq_dram).then_inc(w_loaded[0], 16)
            sp.dma_start(w_raw[:, WKV], wkv_dram).then_inc(w_loaded[1], 16)
            sp.dma_start(cx[:, :], ctx_dram[0]).then_inc(cx_loaded, 16)
            sp.dma_start(w_raw[:, WO], wout_dram).then_inc(w_loaded[2], 16)
            sp.dma_start(bout[:, :], bout_dram).then_inc(w_loaded[3], 16)

            def load_ctx(b):
                wait(sp, ctx_lo_done, b)
                sp.dma_start(cx[:, :], batch_of(ctx_dram, b)).then_inc(cx_loaded, 16)

            def stack(s, p):
                ready = s + 1
                wait(sp, sim_ready, UNITS * ready - 4 * UNITS)
                sp.wait_ge(q_lo_out, ready)
                for half in range(2):
                    rows = slice(64 * half, 64 * half + 64)
                    for dst, src in ((q_hi2, q_nat[p % 2][0]), (q_lo2, q_nat[p % 2][1])):
                        for to in range(2):
                            sp.dma_start(dst[64 * to:64 * to + 64, 2 * p + half, :], src[rows, :])\
                              .then_inc(stacked[p], 16)
                sp.wait_ge(k_lo_out, ready)
                for half in range(2):
                    rows = slice(64 * half, 64 * half + 64)
                    for to in range(2):
                        sp.dma_start(k_hilo[64 * to:64 * to + 64, 2 * p + half, :], k_nat[p % 2][to][rows, :])\
                          .then_inc(stacked[p], 16)

            stack(0, 0)
            stack(1, 1)

            def body(b, first, last):
                for p in range(PAIRS):
                    if p == 0 and not last:
                        load_ctx(b + 1)
                    if not (last and p >= 2):
                        stack(PAIRS * b + p + 2, (p + 2) % PAIRS)
            batches(sp, body)

        @block.tensor
        def _(pe):
            def three(out, stat, mov, start=True, stop=True):
                nc.tensor.matmul(out, stat[0], mov[0], start=start, stop=False)
                nc.tensor.matmul(out, stat[0], mov[1], start=False, stop=False)
                return nc.tensor.matmul(out, stat[1], mov[0], start=False, stop=stop)

            def project_q(s, p, b_of):
                pe.wait_ge(x_lo_done, b_of + 1)
                wait(pe, v_out, s)
                if p == 0:
                    wait(pe, x_done, b_of - 1)
                three(misc[:, :], [w[:, cols(p)] for w in wq], [t[:, :] for t in xn_s]).then_inc(q_ready, 1)

            def project_k(s, p, b_of):
                pe.wait_ge(ctx_lo_done, b_of + 1)
                pe.wait_ge(q_lo_out, s + 1)
                three(misc[:, :], [w[:, cols(p)] for w in wkv], [t[:, :] for t in cx_s]).then_inc(k_ready, 1)

            def project_v(s, p):
                pe.wait_ge(k_lo_out, s + 1)
                for jt in range(TILES):
                    last = three(misc[:, cols(jt)], [t[:, cols(jt)] for t in cx_s],
                                 [w[:, N + p * P:N + (p + 1) * P] for w in wkv], start=jt == 0, stop=jt == TILES - 1)
                last.then_inc(v_ready, 1)

            def project_out(b, vs):
                pe.wait_ge(w_split, 3)
                pe.wait_ge(o_lo_out, PAIRS * (b + 1))
                wait(pe, v_out, vs)
                for p in range(PAIRS):
                    last = three(misc[:, :], [w[:, p, :] for w in wo], [t[:, p, :] for t in o_s],
                                 start=p == 0, stop=p == PAIRS - 1)
                last.then_inc(proj_ready, 1)

            def scores(s, p, u, b_of):
                if u == 0:
                    pe.wait_ge(stacked[p], STACK * b_of + STACK)
                head, it, U = 2 * p + u // TILES, u % TILES, UNITS * s + u
                wait(pe, exp_done, U - 3)
                bank = sim[u % 4][:, :]
                nc.tensor.matmul(bank, q_hi2[:, head, cols(it)], k_hilo[:, head, :], start=True, stop=False)
                nc.tensor.matmul(bank, q_lo2[:, head, cols(it)], k_hilo[:, head, :], start=False, stop=True)\
                    .then_inc(sim_ready, 1)

            def transposes(s, p, u):
                hh, jt = u // TILES, u % TILES
                if jt == 0:
                    wait(pe, norm_done, UNITS * s + TILES * (hh + 1))
                wait_tr_out(pe, s if u >= 2 else s - 1, u - 2 if u >= 2 else u + UNITS - 2)
                for it in range(TILES):
                    last = nc.tensor.transpose(tr[u % 2][:, cols(it)], prob[:, p % 2, hh, it, cols(jt)], ident[:, :])
                last.then_inc(tr_ready, 1)

            def values(s, p, jt):
                if jt == 0:
                    wait_tr_out(pe, s, UNITS - 1)
                    wait_tr_out(pe, s, UNITS - 2)
                    wait(pe, o_lo_out, s)
                    pe.wait_ge(v_out, s + 1)
                for hh in range(2):
                    last = nc.tensor.matmul(av[64 * hh:64 * hh + 64, :], v[:, p, jt, 64 * hh:64 * hh + 64],
                                            prob_t[:, p % 2, hh, jt, :], start=jt == 0, stop=jt == TILES - 1)
                if jt == TILES - 1:
                    last.then_inc(av_ready, 1)

            for s in range(2):
                pe.wait_ge(w_split, 1)
                project_q(s, s, 0)
                pe.wait_ge(w_split, 2)
                project_k(s, s, 0)
                project_v(s, s)
            scores(0, 0, 0, 0)

            def body(b, first, last):
                for p in range(PAIRS):
                    s = PAIRS * b + p
                    for u in range(UNITS):
                        if not (first and p == 0):
                            transposes(s - 1, (p - 1) % PAIRS, u)
                        if u + 1 < UNITS:
                            scores(s, p, u + 1, b)
                        elif not (last and p == PAIRS - 1):
                            scores(s + 1, (p + 1) % PAIRS, 0, b + (p + 1) // PAIRS)
                        if u in VALUE_UNITS and not (first and p < 2):
                            values(s - 2, (p - 2) % PAIRS, VALUE_UNITS.index(u))
                        if not (last and p >= 2):
                            if u == 2:
                                project_q(s + 2, (p + 2) % PAIRS, b + (p + 2) // PAIRS)
                            if u == 5:
                                project_k(s + 2, (p + 2) % PAIRS, b + (p + 2) // PAIRS)
                            if u == 7:
                                project_v(s + 2, (p + 2) % PAIRS)
                        if p == 2 and u == 1 and not first:
                            project_out(b - 1, s + 2)
            batches(pe, body)
            for u in range(UNITS):
                transposes(SLOTS - 1, PAIRS - 1, u)
            for s in (SLOTS - 2, SLOTS - 1):
                for jt in range(TILES):
                    values(s, s % PAIRS, jt)
            project_out(B - 1, SLOTS)

        @block.scalar
        def _(act):
            def exp(s, p, u):
                U, at = UNITS * s + u, UNITS * (p % 2) + u
                if u == 0:
                    wait(act, tr_ready, UNITS * (s - 1))
                    wait(act, norm_done, UNITS * (s - 1))
                act.wait_ge(max_ready, U + 1)
                nc.scalar.activation(prob[:, p % 2, u // TILES, u % TILES, :], sim[u % 4][:, :], ACT.Exp,
                                     bias=neg_max[:, at:at + 1], scale=-1.0, accum_out=denom[:, at:at + 1])\
                    .then_inc(exp_done, 1)

            def copy_transposes(s, p, u):
                act.wait_ge(tr_ready, UNITS * s + u + 1)
                if u == ACT_TURNS[0]:
                    wait(act, av_ready, s - 1)
                nc.scalar.activation(prob_t[:, p % 2, u // TILES, u % TILES, :], tr[u % 2][:, :], ACT.Copy)\
                    .then_inc(tr_out_act, 1)

            def q_hi(s, p):
                act.wait_ge(q_ready, s + 1)
                nc.scalar.activation(q_nat[p % 2][0][:, :], misc[:, :], ACT.Copy).then_inc(q_hi_out, 1)

            def k_hi(s, p):
                act.wait_ge(k_ready, s + 1)
                nc.scalar.activation(k_nat[p % 2][0][:, :], misc[:, :], ACT.Copy).then_inc(k_hi_out, 1)

            def o_hi(s, p=None):
                act.wait_ge(av_ready, s + 1)
                nc.scalar.activation(o_s[0][:, s % PAIRS if p is None else p, :], av[:, :], ACT.Copy)\
                    .then_inc(o_hi_out, 1)

            def ctx_hi(b):
                act.wait_ge(cx_loaded, 16 * b + 16)
                wait(act, v_ready, PAIRS * b)
                nc.scalar.activation(cx_s[0][:, :], cx[:, :], ACT.Copy).then_inc(cxhi_done, 1)

            ctx_hi(0)
            for s in range(2):
                q_hi(s, s)
                k_hi(s, s)

            def body(b, first, last):
                for p in range(PAIRS):
                    s = PAIRS * b + p
                    for u in range(UNITS):
                        if u == 0 and not (first and p < 3):
                            if p == 3 and not first:
                                act.wait_ge(proj_ready, b)
                            o_hi(s - 3, (p - 3) % PAIRS)
                        if u in ACT_TURNS and not (first and p == 0):
                            copy_transposes(s - 1, (p - 1) % PAIRS, u)
                        exp(s, p, u)
                        if not (last and p >= 2):
                            q = (p + 2) % PAIRS
                            if u == 3:
                                act.wait_ge(stacked[p], STACK * b + STACK)
                                q_hi(s + 2, q)
                            if u == 6:
                                k_hi(s + 2, q)
                        if not last and p == 2 and u == 1:
                            ctx_hi(b + 1)
            batches(act, body)
            o_hi(SLOTS - 3)
            for u in ACT_TURNS:
                copy_transposes(SLOTS - 1, PAIRS - 1, u)
            for s in (SLOTS - 2, SLOTS - 1):
                o_hi(s)

        @block.vector
        def _(dve):
            def less(out, full, hi):
                return nc.vector.tensor_tensor(out, full, hi, ALU.subtract)

            def split_weights(n, where, dst, sign=1.0):
                dve.wait_ge(w_loaded[n], 16)
                src = w_raw[:, where]
                flat = [d[:, :] if n < 2 else d[:, :, :].rearrange("p t n -> p (t n)") for d in dst]
                nc.vector.tensor_scalar(flat[0], src, sign, None, ALU.mult).then_inc(hi_done, 1)
                dve.wait_ge(hi_done, n + 1)
                nc.vector.scalar_tensor_tensor(out=flat[1], in0=src, scalar=sign, in1=flat[0], op0=ALU.mult,
                                               op1=ALU.subtract).then_inc(w_split, 1)

            def normalise_x(b):
                wait(dve, x_lo_done, b)
                nc.vector.tensor_scalar(xn[:, :], x_at(b), mr_at(b, 0), mr_at(b, 1), ALU.subtract, ALU.mult)\
                    .then_inc(xn_done, 1)

            def x_at(b):
                return X[:, bass.ds(b, 1), :].rearrange("p a n -> p (a n)")

            def mr_at(b, i):
                return mean_rstd[:, bass.ds(b, 1), i:i + 1].rearrange("p a n -> p (a n)")

            def x_hi(b):
                wait(dve, q_ready, PAIRS * b)
                dve.wait_ge(xn_done, b * 2 + 1)
                nc.vector.tensor_copy(xn_s[0][:, :], xn[:, :]).then_inc(xn_done, 1)

            def ctx_lo(b):
                dve.wait_ge(cxhi_done, b + 1)
                less(cx_s[1][:, :], cx[:, :], cx_s[0][:, :]).then_inc(ctx_lo_done, 1)

            def x_lo(b):
                dve.wait_ge(xn_done, b * 2 + 2)
                less(xn_s[1][:, :], xn[:, :], xn_s[0][:, :]).then_inc(x_lo_done, 1)

            def q_lo(s, p):
                dve.wait_ge(q_hi_out, s + 1)
                less(q_nat[p % 2][1][:, :], misc[:, :], q_nat[p % 2][0][:, :]).then_inc(q_lo_out, 1)

            def k_lo(s, p):
                dve.wait_ge(k_hi_out, s + 1)
                less(k_nat[p % 2][1][:, :], misc[:, :], k_nat[p % 2][0][:, :]).then_inc(k_lo_out, 1)

            def v_copy(s, p):
                dve.wait_ge(v_ready, s + 1)
                wait(dve, av_ready, s - 3)
                nc.vector.tensor_copy(v[:, p, :, :], misc[:, :].rearrange("p (t n) -> p t n", t=TILES))\
                    .then_inc(v_out, 1)

            def row_max(s, p, u):
                at = UNITS * (p % 2) + u
                dve.wait_ge(sim_ready, UNITS * s + u + 1)
                nc.vector.tensor_reduce(neg_max[:, at:at + 1], sim[u % 4][:, :], AX_X, ALU.min).then_inc(max_ready, 1)

            def invert(s, p, u):
                at = UNITS * (p % 2) + u
                dve.wait_ge(exp_done, UNITS * s + u + 1)
                nc.vector.reciprocal(inv[:, at:at + 1], denom[:, at:at + 1]).then_inc(inv_done, 1)

            def normalise(s, p, u):
                at = UNITS * (p % 2) + u
                dve.wait_ge(inv_done, UNITS * s + u + 1)
                row = prob[:, p % 2, u // TILES, u % TILES, :]
                nc.vector.tensor_scalar(row, row, inv[:, at:at + 1], None, ALU.mult).then_inc(norm_done, 1)

            def copy_transposes(s, p, u):
                dve.wait_ge(tr_ready, UNITS * s + u + 1)
                if u == DVE_TURNS[0]:
                    wait(dve, av_ready, s - 1)
                nc.vector.tensor_copy(prob_t[:, p % 2, u // TILES, u % TILES, :], tr[u % 2][:, :])\
                    .then_inc(tr_out_dve, 1)

            def o_lo(s, p):
                dve.wait_ge(o_hi_out, s + 1)
                less(o_s[1][:, p, :], av[:, :], o_s[0][:, p, :]).then_inc(o_lo_out, 1)

            def bias_x(b):
                wait(dve, x_done, b)
                nc.vector.tensor_scalar(x_biased[:, :], x_at(b), gated_bout[:, 0:1], None, ALU.add).then_inc(xb_done, 1)

            def update_x(b):
                dve.wait_ge(xb_done, b + 1)
                dve.wait_ge(proj_ready, b + 1)
                nc.vector.scalar_tensor_tensor(out=x_at(b), in0=misc[:, :], scalar=gates[:, 0:1], in1=x_biased[:, :],
                                               op0=ALU.mult, op1=ALU.add).then_inc(x_done, 1)

            def row_statistics(b):
                wait(dve, x_done, b + 1)
                nc.vector.bn_stats(stats[:, bass.ds(b, 1), :].rearrange("p a n -> p (a n)"), x_at(b))\
                    .then_inc(stats_done, 1)

            normalise_x(0)
            split_weights(0, WQ, wq, -1.0)
            x_hi(0)
            x_lo(0)
            split_weights(1, WKV, wkv)
            ctx_lo(0)
            for s in range(2):
                q_lo(s, s)
                k_lo(s, s)
                v_copy(s, s)
            split_weights(2, WO, wo)
            dve.wait_ge(w_loaded[3], 16)
            nc.vector.tensor_scalar(gated_bout[:, :], bout[:, :], gates[:, 0:1], None, ALU.mult).then_inc(w_split, 1)
            dve.wait_ge(w_split, 4)
            bias_x(0)

            def body(b, first, last):
                for p in range(PAIRS):
                    s = PAIRS * b + p
                    for u in range(UNITS):
                        row_max(s, p, u)
                        if u == 0 and not (first and p == 0) and not (last and p == PAIRS - 1):
                            v_copy(s + 1, (p + 1) % PAIRS)
                        if p == 2 and not first and u == 2:
                            update_x(b - 1)
                        if not (last and p >= 2):
                            if u == 4:
                                q_lo(s + 2, (p + 2) % PAIRS)
                            if u == 7:
                                k_lo(s + 2, (p + 2) % PAIRS)
                        for step, lag in ((invert, 2), (normalise, 3)):
                            if u >= lag:
                                step(s, p, u - lag)
                            elif not (first and p == 0):
                                step(s - 1, (p - 1) % PAIRS, u - lag + UNITS)
                        if u in DVE_TURNS and not (first and p == 0):
                            copy_transposes(s - 1, (p - 1) % PAIRS, u)
                        if u == 0 and not (first and p < 3):
                            o_lo(s - 3, (p - 3) % PAIRS)
                        if not last and p == 1:
                            if u == 4:
                                normalise_x(b + 1)
                            if u == 5:
                                x_hi(b + 1)
                            if u == 6:
                                x_lo(b + 1)
                        if not last and p == 2 and u == 1:
                            ctx_lo(b + 1)
                        if p == 2 and not first and u == 3:
                            bias_x(b)
                        if p == 2 and not first and u == 5:
                            row_statistics(b - 1)
            batches(dve, body)
            for step, lag in ((invert, 2), (normalise, 3)):
                for u in range(UNITS - lag, UNITS):
                    step(SLOTS - 1, PAIRS - 1, u)
            o_lo(SLOTS - 3, (SLOTS - 3) % PAIRS)
            for u in DVE_TURNS:
                copy_transposes(SLOTS - 1, PAIRS - 1, u)
            for s in (SLOTS - 2, SLOTS - 1):
                o_lo(s, s % PAIRS)
            update_x(B - 1)
            dve.wait_ge(x_done, B)
            row_statistics(B - 1)
            dve.wait_ge(stats_done, B)


E, TOP_K, DFF = 8, 2, 2048
CHUNKS = 2 * DFF // N
TOKENS = B * P


def stage_route(nc, gate_dram, iota_dram, X, xt, stats, mean_rstd, gates, ident, chosen, route_gain):
    with ExitStack() as ctx:
        m = Memory(nc, ctx, "route")
        gate_raw = m.sb("gate_raw", [P, TILES, E])
        gate = [m.sb(f"gate_{x}", [P, TILES, E], BF16) for x in ("hi", "lo")]
        iota = m.sb("iota", [P, E])
        ones = m.sb("ones", [P, P])
        xn = m.sb("xn", [P, 2, N])
        logits = m.sb("logits", [P, B, E])
        picked = m.sb("picked", [P, B, E])
        token_sum = m.sb("token_sum", [P, E])
        total = m.sb("total", [P, E])
        top = m.sb("top", [P, E])
        top_index = m.sb("top_index", [P, E], mybir.dt.uint32)
        index_f = m.sb("index_f", [P, E])
        onehot = m.sb("onehot", [P, TOP_K, E])
        pair = m.sb("pair", [P, TOP_K, B])
        largest = m.sb("largest", [P, B])
        inv = m.sb("inv", [P, B])
        tr = [m.ps(f"tr{i}") for i in range(4)]
        logits_ps = m.ps("logits_ps")
        total_ps = m.ps("total_ps")
        loaded = m.sem("loaded")
        small = m.sem("small")
        xn_done, tr_ready, hi_out, lo_out = m.sem("xn_done"), m.sem("tr_ready"), m.sem("hi_out"), m.sem("lo_out")
        logits_ready, total_ready, exp_ready, exp_done = (m.sem("logits_ready"), m.sem("total_ready"),
                                                          m.sem("exp_ready"), m.sem("exp_done"))
        gate_split, sum_done, ones_done = m.sem("gate_split"), m.sem("sum_done"), m.sem("ones_done")
        statistics = RowStatistics(m)
        block = m.block()

        @block.sync
        def _(sp):
            sp.dma_start(gate_raw[:, :, :], gate_dram).then_inc(loaded, 16)
            sp.dma_start(iota[:, :], iota_dram.partition_broadcast(P)).then_inc(loaded, 16)

        @block.tensor
        def _(pe):
            def transposes(b):
                pe.wait_ge(xn_done, b + 1)
                wait(pe, lo_out, b - 3)
                for dt in range(TILES):
                    last = nc.tensor.transpose(tr[b % 4][:, cols(dt)], xn[:, b % 2, cols(dt)], ident[:, :])
                last.then_inc(tr_ready, 1)

            def logit(b):
                pe.wait_ge(lo_out, b + 1)
                for dt in range(TILES):
                    for i, j in ((0, 0), (1, 0), (0, 1)):
                        last = nc.tensor.matmul(logits_ps[:, b * E:(b + 1) * E], xt[i][:, dt, b * P:(b + 1) * P],
                                                gate[j][:, dt, :], start=(dt, i, j) == (0, 0, 0),
                                                stop=(dt, i, j) == (TILES - 1, 0, 1))
                last.then_inc(logits_ready, 1)

            pe.wait_ge(gate_split, 2)
            for b in range(B + 1):
                if b < B:
                    transposes(b)
                if b:
                    logit(b - 1)
            pe.wait_ge(sum_done, 1)
            pe.wait_ge(ones_done, 1)
            nc.tensor.matmul(total_ps[:, 0:E], ones[:, :], token_sum[:, :], start=True, stop=True)\
                .then_inc(total_ready, 1)

        @block.scalar
        def _(act):
            statistics.square_root(nc, act)
            for b in range(B):
                act.wait_ge(tr_ready, b + 1)
                nc.scalar.activation(xt[0][:, :, b * P:(b + 1) * P], tr[b % 4][:, :].rearrange("p (t n) -> p t n", t=TILES),
                                     ACT.Copy).then_inc(hi_out, 1)
            act.wait_ge(exp_ready, 1)
            nc.scalar.activation(pair[:, :, :], pair[:, :, :], ACT.Exp).then_inc(exp_done, 1)

        @block.vector
        def _(dve):
            steps = [0]

            def step(ins):
                steps[0] += 1
                ins.then_inc(small, 1)
                dve.wait_ge(small, steps[0])

            nc.vector.memset(ones[:, :], 1.0).then_inc(ones_done, 1)
            dve.wait_ge(loaded, 32)
            nc.vector.tensor_copy(gate[0][:, :, :], gate_raw[:, :, :]).then_inc(gate_split, 1)
            dve.wait_ge(gate_split, 1)
            nc.vector.tensor_tensor(gate[1][:, :, :], gate_raw[:, :, :], gate[0][:, :, :], ALU.subtract)\
                .then_inc(gate_split, 1)

            statistics.finish(nc, dve, stats, mean_rstd)

            def normalise(b):
                wait(dve, tr_ready, b - 1)
                nc.vector.tensor_scalar(xn[:, b % 2, :], X[:, b, :], mean_rstd[:, b, 0:1], mean_rstd[:, b, 1:2],
                                        ALU.subtract, ALU.mult).then_inc(xn_done, 1)
            normalise(0)
            for b in range(B):
                if b + 1 < B:
                    normalise(b + 1)
                dve.wait_ge(hi_out, b + 1)
                nc.vector.tensor_tensor(xt[1][:, :, b * P:(b + 1) * P], tr[b % 4][:, :].rearrange("p (t n) -> p t n", t=TILES),
                                        xt[0][:, :, b * P:(b + 1) * P], ALU.subtract).then_inc(lo_out, 1)
            dve.wait_ge(logits_ready, B)
            step(nc.vector.tensor_copy(logits[:, :, :].rearrange("p b e -> p (b e)"), logits_ps[:, 0:B * E]))
            nc.vector.tensor_reduce(token_sum[:, :], logits[:, :, :].rearrange("p b e -> p e b"), AX_X, ALU.add)\
                .then_inc(sum_done, 1)
            dve.wait_ge(total_ready, 1)
            step(nc.vector.tensor_copy(total[:, :], total_ps[:, 0:E]))
            step(nc.vector.max(top[:, :], total[:, :]))
            step(nc.vector.max_index(top_index[:, :], top[:, :], total[:, :]))
            step(nc.vector.tensor_copy(chosen[:, :], top_index[:, 0:TOP_K]))
            step(nc.vector.tensor_copy(index_f[:, :], top_index[:, :]))
            for k in range(TOP_K):
                step(nc.vector.tensor_scalar(onehot[:, k, :], iota[:, :], index_f[:, k:k + 1], None, ALU.is_equal))
                step(nc.vector.tensor_tensor(picked[:, :, :], logits[:, :, :],
                                             onehot[:, k:k + 1, :].to_broadcast([P, B, E]), ALU.mult))
                step(nc.vector.tensor_reduce(pair[:, k, :], picked[:, :, :], AX_X, ALU.add))
            step(nc.vector.tensor_tensor(largest[:, :], pair[:, 0, :], pair[:, 1, :], ALU.max))
            for k in range(TOP_K):
                ins = nc.vector.tensor_tensor(pair[:, k, :], pair[:, k, :], largest[:, :], ALU.subtract)
                ins.then_inc(exp_ready if k else small, 1)
                steps[0] += 1 - k
                dve.wait_ge(exp_ready if k else small, 1 if k else steps[0])
            dve.wait_ge(exp_done, 1)
            step(nc.vector.tensor_tensor(largest[:, :], pair[:, 0, :], pair[:, 1, :], ALU.add))
            step(nc.vector.reciprocal(inv[:, :], largest[:, :]))
            step(nc.vector.tensor_scalar(inv[:, :], inv[:, :], gates[:, 2:3], None, ALU.mult))
            for c in range(CHUNKS):
                step(nc.vector.tensor_tensor(route_gain[:, c, :], pair[:, c // (CHUNKS // 2), :], inv[:, :], ALU.mult))


def stage_ffn0(nc, w1_dram, b1_dram, w2_dram, b2_dram, X, xt, chosen, route_gain):
    GROUPS = TOKENS // N
    STEP_UNITS = TILES
    with ExitStack() as ctx:
        m = Memory(nc, ctx, "f0")
        raw = [m.sb(f"raw{i}", [P, TILES, N]) for i in range(2)]
        w1 = [[m.sb(f"w1_{x}{i}", [P, TILES, N], BF16) for x in ("hi", "lo")] for i in range(2)]
        w2 = [[m.sb(f"w2_{x}{i}", [P, TILES, N], BF16) for x in ("hi", "lo")] for i in range(2)]
        b1 = m.sb("b1", [P, 2, TILES])
        b2 = [m.sb(f"b2_{k}", [P, N]) for k in range(TOP_K)]
        hidden = m.sb("hidden", [P, TILES, N])
        h = [[m.sb(f"h_{x}{i}", [P, TILES, N], BF16) for x in ("hi", "lo")] for i in range(2)]
        h_ps = [m.ps(f"h{i}") for i in range(4)]
        y_ps = [m.ps(f"y{i}") for i in range(4)]
        w1_loaded, w2_loaded = m.sem("w1_loaded"), m.sem("w2_loaded")
        b1_loaded, b2_loaded, b2_added = m.sem("b1_loaded"), m.sem("b2_loaded"), m.sem("b2_added")
        w_hi, w_split = m.sem("w_hi"), m.sem("w_split")
        h_ready, gelu_done, h_hi, h_split = m.sem("h_ready"), m.sem("gelu_done"), m.sem("h_hi"), m.sem("h_split")
        y_ready, y_added = m.sem("y_ready"), m.sem("y_added")
        block = m.block()

        def chunks(eng, body):
            body(0, 0, False)
            body(1, 1, False)
            with eng.Fori(1, CHUNKS // 2 - 1) as i:
                for parity in range(2):
                    body(2 * i + parity, parity, False)
            body(CHUNKS - 2, 0, False)
            body(CHUNKS - 1, 1, True)

        @block.sync
        def _(sp):
            expert = [sp.value_load(chosen[0:1, k:k + 1], min_val=0, max_val=E - 1) for k in range(TOP_K)]
            for k in range(TOP_K):
                sp.dma_start(b2[k][:, :], b2_dram[bass.ds(expert[k], 1), :].partition_broadcast(P)
                             .rearrange("p a n -> p (a n)")).then_inc(b2_loaded, 16)
            for c in range(CHUNKS):
                k, f = c // (CHUNKS // 2), c % (CHUNKS // 2)
                wait(sp, gelu_done, 16 * (c - 1))
                sp.dma_start(b1[:, c % 2, :], b1_dram[bass.ds(expert[k], 1), :, f * TILES:(f + 1) * TILES]
                             .rearrange("a p t -> (a p) t")).then_inc(b1_loaded, 16)
                wait(sp, w_split, 2 * c - 1)
                sp.dma_start(raw[0][:, :, :], w1_dram[bass.ds(expert[k], 1), :, f * N:(f + 1) * N]
                             .rearrange("a (t p) n -> p (a t) n", p=P)).then_inc(w1_loaded, 16)
                wait(sp, w_split, 2 * c)
                sp.dma_start(raw[1][:, :, :], w2_dram[bass.ds(expert[k], 1), f * N:(f + 1) * N, :]
                             .rearrange("a (t p) n -> p (a t) n", p=P)).then_inc(w2_loaded, 16)

        @block.tensor
        def _(pe):
            def hidden_units(c, parity, g):
                for ft in range(STEP_UNITS):
                    unit = 4 * STEP_UNITS * c + STEP_UNITS * g + ft
                    if not (isinstance(c, int) and c == 0 and g == 0):
                        wait(pe, gelu_done, unit - 3)
                    bank = h_ps[ft][:, :]
                    for dt in range(TILES):
                        for i, j in ((0, 0), (0, 1), (1, 0)):
                            last = nc.tensor.matmul(bank, w1[parity][i][:, dt, cols(ft)], xt[j][:, dt, g * N:(g + 1) * N],
                                                    start=(dt, i, j) == (0, 0, 0), stop=(dt, i, j) == (TILES - 1, 1, 0))
                    last.then_inc(h_ready, 1)

            def output_units(c, parity, g):
                pe.wait_ge(h_split, 4 * STEP_UNITS * c + STEP_UNITS * g + STEP_UNITS)
                if g == 0:
                    pe.wait_ge(w_split, 2 * c + 2)
                for nt in range(STEP_UNITS):
                    unit = 4 * STEP_UNITS * c + STEP_UNITS * g + nt
                    if not (isinstance(c, int) and c == 0 and g == 0):
                        wait(pe, y_added, unit - 3)
                    bank = y_ps[nt][:, :]
                    for ft in range(TILES):
                        for i, j in ((0, 0), (0, 1), (1, 0)):
                            last = nc.tensor.matmul(bank, h[g % 2][i][:, ft, cols(nt)], w2[parity][j][:, ft, :],
                                                    start=(ft, i, j) == (0, 0, 0), stop=(ft, i, j) == (TILES - 1, 1, 0))
                    last.then_inc(y_ready, 1)

            def body(c, parity, last):
                pe.wait_ge(w_split, 2 * c + 1)
                hidden_units(c, parity, 0)
                for g in range(GROUPS):
                    if g + 1 < GROUPS:
                        hidden_units(c, parity, g + 1)
                    output_units(c, parity, g)
            chunks(pe, body)

        @block.scalar
        def _(act):
            def split_hi(c, parity):
                for n, (loaded, w) in enumerate(((w1_loaded, w1), (w2_loaded, w2))):
                    act.wait_ge(loaded, 16 * c + 16)
                    if not (isinstance(c, int) and c < 2):
                        wait(act, y_ready, 16 * c - 16)
                    nc.scalar.activation(w[parity][0][:, :, :], raw[n][:, :, :], ACT.Copy).then_inc(w_hi, 1)

            split_hi(0, 0)

            def body(c, parity, last):
                for g in range(GROUPS):
                    if g == 0:
                        act.wait_ge(b1_loaded, 16 * c + 16)
                    for ft in range(STEP_UNITS):
                        unit = 4 * STEP_UNITS * c + STEP_UNITS * g + ft
                        act.wait_ge(h_ready, unit + 1)
                        if not (isinstance(c, int) and c == 0 and g == 0):
                            wait(act, h_split, unit - 3)
                        nc.scalar.activation(hidden[:, ft, :], h_ps[ft][:, :], ACT.Gelu_apprx_tanh,
                                             bias=b1[:, parity, ft:ft + 1])\
                            .then_inc(gelu_done, 1)
                    if g == 1 and not last:
                        split_hi(c + 1, 1 - parity)
            chunks(act, body)

        @block.vector
        def _(dve):
            def split_lo(c, parity):
                for n, w in enumerate((w1, w2)):
                    dve.wait_ge(w_hi, 2 * c + n + 1)
                    nc.vector.tensor_tensor(w[parity][1][:, :, :], raw[n][:, :, :], w[parity][0][:, :, :],
                                            ALU.subtract).then_inc(w_split, 1)

            split_lo(0, 0)

            def add_b2(g):
                dve.wait_ge(b2_loaded, 16 * TOP_K)
                for k in range(TOP_K):
                    for nt in range(STEP_UNITS):
                        b = STEP_UNITS * g + nt
                        if k:
                            dve.wait_ge(b2_added, TOP_K * STEP_UNITS * g + nt + 1)
                        nc.vector.scalar_tensor_tensor(out=X[:, b, :], in0=b2[k][:, :],
                                                       scalar=route_gain[:, k * (CHUNKS // 2), b:b + 1], in1=X[:, b, :],
                                                       op0=ALU.mult, op1=ALU.add).then_inc(b2_added, 1)

            def split_hidden(c, g):
                first_step = isinstance(c, int) and c == 0
                for ft in range(STEP_UNITS):
                    unit = 4 * STEP_UNITS * c + STEP_UNITS * g + ft
                    dve.wait_ge(gelu_done, unit + 1)
                    if not (first_step and g < 2):
                        wait(dve, y_ready, 16 * c + 4 * g - 4)
                    nc.vector.tensor_copy(h[g % 2][0][:, ft, :], hidden[:, ft, :]).then_inc(h_hi, 1)
                    dve.wait_ge(h_hi, unit + 1)
                    nc.vector.tensor_tensor(h[g % 2][1][:, ft, :], hidden[:, ft, :], h[g % 2][0][:, ft, :],
                                            ALU.subtract).then_inc(h_split, 1)

            def add_output(c, g):
                for nt in range(STEP_UNITS):
                    b = STEP_UNITS * g + nt
                    dve.wait_ge(y_ready, 16 * c + b + 1)
                    if isinstance(c, int) and c == 0:
                        dve.wait_ge(b2_added, TOP_K * STEP_UNITS * g + STEP_UNITS + nt + 1)
                    else:
                        wait(dve, y_added, 16 * c + b - 15)
                    nc.vector.scalar_tensor_tensor(
                        out=X[:, b, :], in0=y_ps[nt][:, :],
                        scalar=route_gain[:, bass.ds(c, 1), b:b + 1].rearrange("p a n -> p (a n)"),
                        in1=X[:, b, :], op0=ALU.mult, op1=ALU.add).then_inc(y_added, 1)

            def body(c, parity, last):
                split_hidden(c, 0)
                for g in range(GROUPS):
                    if g + 1 < GROUPS:
                        split_hidden(c, g + 1)
                    if isinstance(c, int) and c == 0:
                        add_b2(g)
                    add_output(c, g)
                    if g == 1 and not last:
                        split_lo(c + 1, 1 - parity)
            chunks(dve, body)
            dve.wait_ge(y_added, 16 * CHUNKS)


D16 = 16
BLOCKS = 4


def head_selectors():
    stack = np.zeros((P, 4, PAIRS, P), np.float32)
    for t in range(PAIRS):
        for r in range(P):
            row, block = D16 * (2 * t + r // 64) + r % D16, r % 64 // D16
            stack[row, block % 2, t, r] = 1
            stack[row, 2 + block // 2, t, r] = 1
    pick = np.zeros((P, 4, P), np.float32)
    for h in range(HEADS):
        for c in range(D16):
            for i in range(2):
                pick[32 * (h % 4) + 16 * i + c, 2 * (h // 4) + i, D16 * h + c] = 1
    channel = np.arange(P)
    head = channel // D16
    gather = np.zeros((P, 2 * P - HEADS), np.float32)
    gather[channel, HEADS * (B - 1) + head] = 1
    scatter = np.zeros((P, B, P), np.float32)
    for b in range(B):
        scatter[HEADS * b + head, b, channel] = 1
    return stack, pick, gather, scatter


def stage_unit_heads(nc, ctx_dram, gather_dram, scatter_dram, X, units):
    JOBS = 2 * B
    RING = 4
    CTX_LOADS = 4
    with ExitStack() as ctx:
        m = Memory(nc, ctx, "uh")
        gather = m.sb("gather", [P, 2 * P - HEADS])
        scatter = m.sb("scatter", [P, B, P])
        cx = m.sb("cx", [P, B, N])
        xn = m.sb("xn", [P, B, N])
        stats = m.sb("stats", [P, B, 6])
        moments = m.sb("moments", [P, B, 2])
        spread = m.sb("spread", [P, B, 1])
        rstd = m.sb("rstd", [P, B, 1])
        square = m.sb("square", [P, 2, N])
        length = [m.sb(f"length_{x}", [P, N]) for x in ("x", "ctx")]
        inv = [m.sb(f"inv_{x}", [P, N]) for x in ("x", "ctx")]
        unit = m.sb("unit", [P, RING, N])
        sum_ps = [m.ps(f"sum_{x}") for x in ("x", "ctx")]
        wide_ps = [m.ps(f"wide{i}") for i in range(RING)]
        gather_loaded, scatter_loaded = m.sem("gather_loaded"), m.sem("scatter_loaded")
        cx_loaded = [m.sem(f"cx_loaded{i}") for i in range(CTX_LOADS)]
        row_done, moments_done, eps_added, rstd_sqrt, rstd_done, xn_done = (
            m.sem(x) for x in ("row_done", "moments_done", "eps_added", "rstd_sqrt", "rstd_done", "xn_done"))
        square_done, sum_ready = m.sem("square_done"), m.sem("sum_ready")
        clamped = [m.sem(f"clamped_{x}") for x in ("x", "ctx")]
        sqrt_done = [m.sem(f"sqrt_done_{x}") for x in ("x", "ctx")]
        inv_done = [m.sem(f"inv_done_{x}") for x in ("x", "ctx")]
        wide_ready, unit_done, hi_done = m.sem("wide_ready"), m.sem("unit_done"), m.sem("hi_done")
        lo_dve, lo_pool = m.sem("lo_dve"), m.sem("lo_pool")
        block = m.block()

        def parts(job):
            return (1 if job < B else 0), job % B

        def rows(job):
            i, b = parts(job)
            return (xn, cx)[i][:, b, :]

        def wait_rows(eng, job):
            i, b = parts(job)
            if i:
                eng.wait_ge(cx_loaded[b // (B // CTX_LOADS)], 16)
            else:
                eng.wait_ge(xn_done, b + 1)

        @block.sync
        def _(sp):
            sp.dma_start(gather[:, :], gather_dram).then_inc(gather_loaded, 16)
            for q in range(CTX_LOADS):
                bs = slice(q * (B // CTX_LOADS), (q + 1) * (B // CTX_LOADS))
                sp.dma_start(cx[:, bs, :], ctx_dram[bs].rearrange("b p n -> p b n")).then_inc(cx_loaded[q], 16)
            sp.dma_start(scatter[:, :, :], scatter_dram).then_inc(scatter_loaded, 16)

        @block.scalar
        def _(act):
            def lengths(i):
                act.wait_ge(clamped[i], 1)
                nc.scalar.activation(length[i][:, :], length[i][:, :], ACT.Sqrt).then_inc(sqrt_done[i], 1)

            for job in range(JOBS):
                if job == B - 4:
                    act.wait_ge(eps_added, 1)
                    nc.scalar.activation(spread[:, :, :], spread[:, :, :], ACT.Sqrt).then_inc(rstd_sqrt, 1)
                if job == B + 5:
                    lengths(1)
                wait_rows(act, job)
                wait(act, sum_ready, job - 1)
                nc.scalar.activation(square[:, job % 2, :], rows(job), ACT.Square).then_inc(square_done, 1)
            for job in range(JOBS):
                if job == 6:
                    lengths(0)
                i, b = parts(job)
                act.wait_ge(unit_done, job + 1)
                nc.scalar.activation(units[i][0][:, b, :], unit[:, job % RING, :], ACT.Copy).then_inc(hi_done, 1)

        @block.tensor
        def _(pe):
            pe.wait_ge(gather_loaded, 16)
            for job in range(JOBS):
                i, b = parts(job)
                at = HEADS * (B - 1 - b)
                pe.wait_ge(square_done, job + 1)
                nc.tensor.matmul(sum_ps[i][:, :], gather[:, at:at + P], square[:, job % 2, :], start=b == 0,
                                 stop=b == B - 1).then_inc(sum_ready, 1)
            pe.wait_ge(scatter_loaded, 16)
            for job in range(JOBS):
                i, b = parts(job)
                pe.wait_ge(inv_done[i], 1)
                wait(pe, unit_done, job - RING + 1)
                nc.tensor.matmul(wide_ps[job % RING][:, :], scatter[:, b, :], inv[i][:, :], start=True, stop=True)\
                    .then_inc(wide_ready, 1)

        @block.gpsimd
        def _(pool):
            for job in range(1, JOBS, 2):
                i, b = parts(job)
                pool.wait_ge(hi_done, job + 1)
                nc.gpsimd.tensor_tensor(units[i][1][:, b, :], unit[:, job % RING, :], units[i][0][:, b, :],
                                        ALU.subtract).then_inc(lo_pool, 1)

        @block.vector
        def _(dve):
            def clamp(i):
                dve.wait_ge(sum_ready, B if i else JOBS)
                nc.vector.tensor_scalar(length[i][:, :], sum_ps[i][:, :], 1e-24, None, ALU.max).then_inc(clamped[i], 1)

            def invert(i):
                dve.wait_ge(sqrt_done[i], 1)
                nc.vector.reciprocal(inv[i][:, :], length[i][:, :]).then_inc(inv_done[i], 1)

            def scale(job):
                dve.wait_ge(wide_ready, job + 1)
                wait(dve, hi_done, job - RING + 1)
                wait(dve, lo_pool if job % 2 else lo_dve, (job - RING) // 2 + 1)
                nc.vector.tensor_tensor(unit[:, job % RING, :], wide_ps[job % RING][:, :], rows(job), ALU.mult)\
                    .then_inc(unit_done, 1)

            def split_lo(job):
                i, b = parts(job)
                dve.wait_ge(hi_done, job + 1)
                nc.vector.tensor_tensor(units[i][1][:, b, :], unit[:, job % RING, :], units[i][0][:, b, :],
                                        ALU.subtract).then_inc(lo_dve, 1)

            for b in range(B):
                nc.vector.bn_stats(stats[:, b, :], X[:, b, :]).then_inc(row_done, 1)
            dve.wait_ge(row_done, B)
            for b in range(B):
                nc.vector.bn_aggr(moments[:, b, :], stats[:, b, :]).then_inc(moments_done, 1)
            dve.wait_ge(moments_done, B)
            nc.vector.tensor_scalar(spread[:, :, :], moments[:, :, 1:2], LN_EPS, None, ALU.add).then_inc(eps_added, 1)
            dve.wait_ge(rstd_sqrt, 1)
            nc.vector.reciprocal(rstd[:, :, :], spread[:, :, :]).then_inc(rstd_done, 1)
            dve.wait_ge(rstd_done, 1)
            for b in range(B):
                if b == 6:
                    clamp(1)
                if b == 12:
                    invert(1)
                nc.vector.tensor_scalar(xn[:, b, :], X[:, b, :], moments[:, b, 0:1], rstd[:, b, :],
                                        ALU.subtract, ALU.mult).then_inc(xn_done, 1)
            for job in range(JOBS):
                if job == 4:
                    clamp(0)
                if job == 8:
                    invert(0)
                scale(job)
                if job % 2:
                    split_lo(job - 1)
            dve.wait_ge(lo_dve, B)


def stage_attention1(nc, ctx_dram, stack_dram, pick_dram, X, gates, ident, units):
    ALPHA = 5.0
    GROUP = HEADS // 2
    STEPS = 2 * TILES
    with ExitStack() as ctx:
        m = Memory(nc, ctx, "a1")
        stack_raw = m.sb("stack_raw", [P, 4, PAIRS * P])
        pick_raw = m.sb("pick_raw", [P, 4, P])
        stack = m.sb("stack", [P, 4, PAIRS, P], BF16)
        pick = m.sb("pick", [P, 4, P], BF16)
        cx = m.sb("cx", [P, 2, N])
        k_stack = [m.sb(f"k_stack{i}", [P, PAIRS, N], BF16) for i in range(2)]
        q_stack = [m.sb(f"q_stack{i}", [P, HEADS, N], BF16) for i in range(2)]
        v = [m.sb(f"v{i}", [P, TILES, HEADS, 32]) for i in range(2)]
        prob = m.sb("prob", [P, TILES, GROUP, N])
        summed = [m.sb(f"summed_{x}", [P, 2, N], BF16) for x in ("hi", "lo")]
        inv = m.sb("inv", [P, N])
        attended = m.sb("attended", [P, N])
        sim = [m.ps(f"sim{i}") for i in range(4)]
        av = [m.ps(f"av{i}") for i in range(2)]
        misc = [m.ps(f"misc{i}") for i in range(2)]
        pick_loaded, cx_loaded = m.sem("pick_loaded"), m.sem("cx_loaded")
        stack_loaded = [m.sem(f"stack_loaded_{x}") for x in "kq"]
        stack_done, filled, half_out = m.sem("stack_done"), m.sem("filled"), m.sem("half_out")
        sim_ready, exp_done, av_ready, av_out = m.sem("sim_ready"), m.sem("exp_done"), m.sem("av_ready"), m.sem("av_out")
        misc_ready, misc_out, av_hi = m.sem("misc_ready"), m.sem("misc_out"), m.sem("av_hi")
        x_done = m.sem("x_done")
        block = m.block()

        PREPARE = [("k", t) for t in range(PAIRS)] + [("q", t) for t in range(PAIRS)] + [("v", 0)]
        FINISH = [("pick", 1), ("pick", 0)]
        PLAN = {0: [("k", 0), ("k", 1)], 1: [("k", 2)], 2: [("pick", 1)], 3: [("pick", 0)], 4: [("k", 3), ("q", 0)],
                5: [("q", 1), ("v", 0)], 6: [("q", 2), ("q", 3)], 7: []}
        PER_BATCH = sum(len(x) for x in PLAN.values())
        assert sorted(x for st in range(STEPS) for x in PLAN[st]) == sorted(PREPARE + FINISH)

        def uses(first, last):
            todo = [(st, what, t) for st in range(STEPS) for what, t in PLAN[st]
                    if not (first and what == "pick") and not (last and what != "pick")]
            return [(n, *x) for n, x in enumerate(todo)]

        def use(b, n, first=False):
            return len(PREPARE) + n if first else 2 * len(PREPARE) - PER_BATCH + PER_BATCH * b + n

        def bank(parity, n, first=False):
            return misc[use(parity, n, first) % 2]

        def picked(b):
            if isinstance(b, int) and b < 0:
                return 0
            todo = uses(False, isinstance(b, int) and b == B - 2)
            return use(b + 1, 1 + max(n for n, _, what, _ in todo if what == "pick"))

        LAST = use(B - 1, len(FINISH))

        def two_by_two(eng, body):
            body(0, 0, True, False)
            with eng.Fori(0, (B - 2) // 2) as i:
                for parity in (1, 0):
                    body(2 * i + 2 - parity, parity, False, False)
            body(B - 1, 1, False, True)

        @block.sync
        def _(sp):
            for i in range(2):
                sp.dma_start(stack_raw[:, 2 * i:2 * i + 2, :], stack_dram[:, 2 * i:2 * i + 2, :])\
                  .then_inc(stack_loaded[i], 16)
            sp.dma_start(pick_raw[:, :, :], pick_dram).then_inc(pick_loaded, 16)
            sp.dma_start(cx[:, 0, :], ctx_dram[0]).then_inc(cx_loaded, 16)

            def body(b, parity, first, last):
                if not last:
                    sp.wait_ge(misc_ready, use(b, 0, first))
                    sp.dma_start(cx[:, 1 - parity, :], batch_of(ctx_dram, b + 1)).then_inc(cx_loaded, 16)
            two_by_two(sp, body)

        def source(i, half, b):
            return units[i][half][:, bass.ds(b, 1), :].rearrange("p a n -> p (a n)")

        @block.tensor
        def _(pe):
            def prepare(b, parity, what, t, out):
                if what == "v":
                    pe.wait_ge(cx_loaded, 16 * b + 16)
                    for jt in range(TILES):
                        last = nc.tensor.transpose(out[:, cols(jt)], cx[:, parity, cols(jt)], ident[:, :])
                    return last
                i = 0 if what == "q" else 1
                at = 2 if what == "q" else 0
                nc.tensor.matmul(out[:, :], stack[:, at, t, :], source(i, 0, b), start=True, stop=False)
                return nc.tensor.matmul(out[:, :], stack[:, at + 1, t, :], source(i, 1, b), start=False, stop=True)

            def pick_heads(b, i, out):
                pe.wait_ge(stack_done, 5)
                pe.wait_ge(av_out, 2 * b + 2)
                for g in range(2):
                    for half in range(2):
                        last = nc.tensor.matmul(out[:, :], pick[:, 2 * g + i, :], summed[half][:, g, :],
                                                start=(g, half) == (0, 0), stop=(g, half) == (1, 1))
                return last

            def scores(b, parity, g, jt):
                for q in range(GROUP):
                    h = GROUP * g + q
                    unit = GROUP * (STEPS * b + TILES * g + jt) + q
                    wait(pe, exp_done, unit - 3)
                    nc.tensor.matmul(sim[q][:, :], k_stack[parity][:, h // 2, cols(jt)], q_stack[parity][:, h, :],
                                     start=True, stop=True).then_inc(sim_ready, 1)

            def values(b, parity, g, jt):
                pe.wait_ge(exp_done, GROUP * (STEPS * b + TILES * g + jt) + GROUP)
                if jt == 0:
                    wait(pe, av_out, 2 * b + g - 1)
                for q in range(GROUP):
                    last = nc.tensor.matmul(av[g][32 * q:32 * q + 32, :], v[parity][:, jt, GROUP * g + q, :],
                                            prob[:, jt, q, :], start=jt == 0, stop=jt == TILES - 1)
                last.then_inc(av_ready, 1)

            for n, (what, t) in enumerate(PREPARE):
                pe.wait_ge(stack_done, 2 if what == "k" else 4)
                wait(pe, misc_out, n - 1)
                prepare(0, 0, what, t, misc[n % 2]).then_inc(misc_ready, 1)

            def body(b, parity, first, last):
                pe.wait_ge(misc_out, use(b, 0, first))
                for st in range(STEPS):
                    scores(b, parity, st // TILES, st % TILES)
                    if st:
                        values(b, parity, (st - 1) // TILES, (st - 1) % TILES)
                    elif not first:
                        values(b - 1, 1 - parity, 1, TILES - 1)
                    for n, at, what, t in uses(first, last):
                        if at != st:
                            continue
                        pe.wait_ge(misc_out, use(b, n, first) - 1)
                        if what == "pick":
                            pick_heads(b - 1, t, bank(parity, n, first)).then_inc(misc_ready, 1)
                        else:
                            prepare(b + 1, 1 - parity, what, t, bank(parity, n, first)).then_inc(misc_ready, 1)
            two_by_two(pe, body)
            values(B - 1, 1, 1, TILES - 1)
            for n, (what, t) in enumerate(FINISH):
                pe.wait_ge(misc_out, LAST + n - 1)
                pick_heads(B - 1, t, misc[(LAST + n) % 2]).then_inc(misc_ready, 1)

        @block.scalar
        def _(act):
            def values_hi(b, g):
                act.wait_ge(av_ready, STEPS * b + TILES * g + TILES)
                wait(act, misc_ready, picked(b - 1))
                nc.scalar.activation(summed[0][:, g, :], av[g][:, :], ACT.Copy).then_inc(av_hi, 1)

            def body(b, parity, first, last):
                for st in range(STEPS):
                    if st == 1 and not first:
                        values_hi(b - 1, 1)
                    if st == 5:
                        values_hi(b, 0)
                    for q in range(GROUP):
                        unit = GROUP * (STEPS * b + st) + q
                        act.wait_ge(sim_ready, unit + 1)
                        if q == 0:
                            wait(act, av_ready, STEPS * b + st - 3)
                        nc.scalar.activation(prob[:, st % TILES, q, :], sim[q][:, :], ACT.Exp, scale=ALPHA)\
                            .then_inc(exp_done, 1)
            two_by_two(act, body)
            values_hi(B - 1, 1)

        @block.gpsimd
        def _(pool):
            for i in range(2):
                nc.gpsimd.memset(q_stack[i][:, :, :], 0.0).then_inc(filled, 1)
                nc.gpsimd.memset(v[i][:, :, :, :], 1.0).then_inc(filled, 1)

        @block.vector
        def _(dve):
            for i in range(4):
                dve.wait_ge(stack_loaded[i // 2], 16)
                nc.vector.tensor_copy(stack[:, i, :, :].rearrange("p t n -> p (t n)"), stack_raw[:, i, :])\
                    .then_inc(stack_done, 1)
            dve.wait_ge(pick_loaded, 16)
            nc.vector.tensor_copy(pick[:, :, :], pick_raw[:, :, :]).then_inc(stack_done, 1)

            def prepared(parity, what, t, out):
                if what == "k":
                    return nc.vector.tensor_copy(k_stack[parity][:, t, :], out[:, :])
                if what == "q":
                    nc.vector.tensor_copy(q_stack[parity][0:64, 2 * t, :], out[0:64, :]).then_inc(half_out, 1)
                    return nc.vector.tensor_copy(q_stack[parity][64:128, 2 * t + 1, :], out[64:128, :])
                return nc.vector.tensor_copy(v[parity][:, :, :, 0:D16],
                                             out[:, :].rearrange("p (t h c) -> p t h c", t=TILES, h=HEADS))

            def finished(b, i, out, n):
                if i == 1:
                    nc.vector.reciprocal(inv[:, :], out[:, :]).then_inc(misc_out, 1)
                    return
                dve.wait_ge(misc_out, n)
                nc.vector.tensor_tensor(attended[:, :], out[:, :], inv[:, :], ALU.mult).then_inc(misc_out, 1)
                dve.wait_ge(misc_out, n + 1)
                row = X[:, bass.ds(b, 1), :].rearrange("p a n -> p (a n)")
                nc.vector.scalar_tensor_tensor(out=row, in0=attended[:, :], scalar=gates[:, 1:2], in1=row,
                                               op0=ALU.mult, op1=ALU.add).then_inc(x_done, 1)

            def values_out(b, g):
                dve.wait_ge(av_ready, STEPS * b + TILES * g + TILES)
                dve.wait_ge(av_hi, 2 * b + g + 1)
                nc.vector.tensor_tensor(summed[1][:, g, :], av[g][:, :], summed[0][:, g, :], ALU.subtract)\
                    .then_inc(av_out, 1)

            for n, (what, t) in enumerate(PREPARE):
                if what == "q":
                    dve.wait_ge(filled, 4)
                dve.wait_ge(misc_ready, n + 1)
                prepared(0, what, t, misc[n % 2]).then_inc(misc_out, 1)

            def body(b, parity, first, last):
                for st in range(STEPS):
                    if st == 1 and not first:
                        values_out(b - 1, 1)
                    if st == 5:
                        values_out(b, 0)
                    for n, at, what, t in uses(first, last):
                        if at != st:
                            continue
                        dve.wait_ge(misc_ready, use(b, n, first) + 1)
                        if what == "pick":
                            finished(b - 1, t, bank(parity, n, first), use(b, n, first))
                        else:
                            prepared(1 - parity, what, t, bank(parity, n, first)).then_inc(misc_out, 1)
            two_by_two(dve, body)
            values_out(B - 1, 1)
            for n, (what, t) in enumerate(FINISH):
                dve.wait_ge(misc_ready, LAST + n + 1)
                finished(B - 1, t, misc[(LAST + n) % 2], LAST + n)
            dve.wait_ge(x_done, B)


EXPERTS, SLOTS1, HID = 16, 128, 128
ES = EXPERTS * SLOTS1
QUADS = ES // N


def stage_soft_prepare(nc, gamma_dram, beta_dram, scale_dram, mu_dram, w1_dram, w2_dram, X, ident,
                       token_scale, split, x_dram, xln_dram):
    with ExitStack() as ctx:
        m = Memory(nc, ctx, "sp")
        gamma, beta, scale = m.sb("gamma", [P, N]), m.sb("beta", [P, N]), m.sb("scale", [P, 1])
        RING = B // 2
        xln = m.sb("xln", [P, RING, N])
        xln_square = m.sb("xln_square", [P, N])
        stats = m.sb("stats", [P, B, 6])
        moments = m.sb("moments", [P, B, 2])
        spread = m.sb("spread", [P, B, 1])
        rstd = m.sb("rstd", [P, B, 1])
        rstd2 = m.sb("rstd2", [P, B, 1])
        length = m.sb("length", [P, B])
        raw = [[m.sb(f"raw_{x}", [P, TILES, N]) for x in names] for names in (("mu0", "mu1"), ("w1",), ("w2",))]
        square = m.sb("square", [P, TILES, N])
        ones = m.sb("ones", [P, P])
        mu_length = m.sb("mu_length", [P, TILES])
        mu_inv = m.sb("mu_inv", [P, TILES])
        mu_diagonal = m.sb("mu_diagonal", [P, TILES, P])
        sum_ps = m.ps("sum")
        wide_ps = m.ps("wide")
        loaded, x_stored = m.sem("loaded"), m.sem("x_stored")
        stored = [m.sem(f"stored{i}") for i in range(4)]
        row_done, moments_done, small, spread_done, sqrt_done = (
            m.sem(x) for x in ("row_done", "moments_done", "small", "spread_done", "sqrt_done"))
        centred, by_gamma, xln_done, squared, clamped = (
            m.sem(x) for x in ("centred", "by_gamma", "xln_done", "squared", "clamped"))
        raw_loaded = [[m.sem(f"raw_loaded_{x}") for x in names] for names in (("mu0", "mu1"), ("w1",), ("w2",))]
        hi_done = [m.sem(f"hi_done_{x}") for x in ("mu", "w1", "w2")]
        lo_done = [m.sem(f"lo_done_{x}") for x in ("mu", "w1", "w2")]
        ones_done, mu_squared, sum_ready, mu_clamped = (
            m.sem(x) for x in ("ones_done", "mu_squared", "sum_ready", "mu_clamped"))
        mu_sqrt_done, mu_inv_done, unit_done = m.sem("mu_sqrt_done"), m.sem("mu_inv_done"), m.sem("unit_done")
        diagonal_done, wide_ready = m.sem("diagonal_done"), m.sem("wide_ready")
        block = m.block()
        MU, W1, W2 = range(3)

        def quad(c):
            return slice(TILES * c, TILES * c + TILES)

        def wait_raw(eng, w, c):
            eng.wait_ge(raw_loaded[w][c % len(raw[w])], 16 * (c // len(raw[w])) + 16)

        def buffer(w, c):
            return raw[w][c % len(raw[w])][:, :, :]

        @block.sync
        def _(sp):
            def load(w, c):
                wait(sp, lo_done[w], c - len(raw[w]) + 1)
                sp.dma_start(buffer(w, c), (mu_dram, w1_dram, w2_dram)[w][:, quad(c), :])\
                    .then_inc(raw_loaded[w][c % len(raw[w])], 16)

            load(MU, 0)
            for c in range(QUADS):
                load(W1, c)
                load(W2, c)
                if c + 1 < QUADS:
                    load(MU, c + 1)
                if c == 0:
                    sp.dma_start(gamma[:, :], gamma_dram.partition_broadcast(P)).then_inc(loaded, 16)
                    sp.dma_start(beta[:, :], beta_dram.partition_broadcast(P)).then_inc(loaded, 16)
                    sp.dma_start(scale[:, :], scale_dram.partition_broadcast(P)).then_inc(loaded, 16)
                    sp.dma_start(x_dram.rearrange("b p n -> p b n"), X[:, :, :]).then_inc(x_stored, 16)
                else:
                    for b in range(4 * c - 4, 4 * c):
                        sp.wait_ge(xln_done, b + 1)
                        sp.dma_start(xln_dram[b], xln[:, b % RING, :]).then_inc(stored[b // 4], 16)
            for b in range(B - 4, B):
                sp.wait_ge(xln_done, b + 1)
                sp.dma_start(xln_dram[b], xln[:, b % RING, :]).then_inc(stored[b // 4], 16)
            sp.wait_ge(x_stored, 16)
            for group in stored:
                sp.wait_ge(group, 64)

        @block.tensor
        def _(pe):
            pe.wait_ge(ones_done, 1)
            for c in range(QUADS):
                pe.wait_ge(mu_squared, c + 1)
                wait(pe, mu_clamped, c)
                for j in range(TILES):
                    for t in range(TILES):
                        last = nc.tensor.matmul(sum_ps[:, j:j + 1], square[:, t, cols(j)], ones[:, 0:1], start=t == 0,
                                                stop=t == TILES - 1)
                last.then_inc(sum_ready, 1)
                pe.wait_ge(diagonal_done, TILES * c + TILES)
                wait(pe, unit_done, c)
                for j in range(TILES):
                    last = nc.tensor.matmul(wide_ps[:, cols(j)], ones[:, :], mu_diagonal[:, j, :], start=True, stop=True)
                last.then_inc(wide_ready, 1)

        @block.scalar
        def _(act):
            def split_hi(w, c):
                wait_raw(act, w, c)
                nc.scalar.activation(split[w][0][:, quad(c), :], buffer(w, c), ACT.Copy).then_inc(hi_done[w], 1)

            def square_mu(c):
                wait_raw(act, MU, c)
                wait(act, sum_ready, c)
                nc.scalar.activation(square[:, :, :], buffer(MU, c), ACT.Square).then_inc(mu_squared, 1)

            square_mu(0)
            split_hi(W1, 0)
            for n in range(2):
                act.wait_ge(spread_done, n + 1)
                nc.scalar.activation(spread[:, :, :], spread[:, :, :], ACT.Sqrt).then_inc(sqrt_done, 1)
            for c in range(QUADS):
                if c:
                    split_hi(W1, c)
                act.wait_ge(mu_clamped, c + 1)
                nc.scalar.activation(mu_length[:, :], mu_length[:, :], ACT.Sqrt).then_inc(mu_sqrt_done, 1)
                split_hi(W2, c)
                if c + 1 < QUADS:
                    square_mu(c + 1)
                for b in range(4 * c, 4 * c + 4):
                    act.wait_ge(xln_done, b + 1)
                    wait(act, squared, b)
                    nc.scalar.activation(xln_square[:, :], xln[:, b % RING, :], ACT.Square, accum_out=length[:, b:b + 1])\
                        .then_inc(squared, 1)
                act.wait_ge(unit_done, c + 1)
                split_hi(MU, c)
            act.wait_ge(clamped, 1)
            nc.scalar.activation(length[:, :], length[:, :], ACT.Sqrt).then_inc(sqrt_done, 1)

        @block.gpsimd
        def _(pool):
            def plus_beta(b):
                pool.wait_ge(by_gamma, b + 1)
                nc.gpsimd.tensor_tensor(xln[:, b % RING, :], xln[:, b % RING, :], beta[:, :], ALU.add).then_inc(xln_done, 1)

            pool.wait_ge(loaded, 48)
            for b in range(B):
                pool.wait_ge(centred, b + 1)
                nc.gpsimd.tensor_tensor(xln[:, b % RING, :], xln[:, b % RING, :], gamma[:, :], ALU.mult).then_inc(by_gamma, 1)
                if b % 4:
                    plus_beta(b - 1)
                if b % 4 == 3:
                    plus_beta(b)

        @block.vector
        def _(dve):
            def split_lo(w, c):
                dve.wait_ge(hi_done[w], c + 1)
                nc.vector.tensor_tensor(split[w][1][:, quad(c), :], buffer(w, c), split[w][0][:, quad(c), :],
                                        ALU.subtract).then_inc(lo_done[w], 1)

            nc.vector.memset(ones[:, :], 1.0).then_inc(ones_done, 1)
            for b in range(B):
                nc.vector.bn_stats(stats[:, b, :], X[:, b, :]).then_inc(row_done, 1)
            dve.wait_ge(row_done, B)
            for b in range(B):
                nc.vector.bn_aggr(moments[:, b, :], stats[:, b, :]).then_inc(moments_done, 1)
            split_lo(W1, 0)
            dve.wait_ge(moments_done, B)
            variance = moments[:, :, 1:2]
            nc.vector.tensor_scalar(spread[:, :, :], variance, LN_EPS, None, ALU.add).then_inc(spread_done, 1)
            dve.wait_ge(sqrt_done, 1)
            nc.vector.reciprocal(rstd[:, :, :], spread[:, :, :]).then_inc(small, 1)
            dve.wait_ge(small, 1)
            nc.vector.tensor_tensor(rstd2[:, :, :], variance, rstd[:, :, :], ALU.mult).then_inc(small, 1)
            dve.wait_ge(small, 2)
            nc.vector.tensor_tensor(rstd2[:, :, :], rstd2[:, :, :], rstd[:, :, :], ALU.mult).then_inc(small, 1)
            dve.wait_ge(small, 3)
            nc.vector.tensor_scalar(spread[:, :, :], rstd2[:, :, :], LN_EPS, None, ALU.add).then_inc(spread_done, 1)
            dve.wait_ge(sqrt_done, 2)
            nc.vector.reciprocal(rstd2[:, :, :], spread[:, :, :]).then_inc(small, 1)
            dve.wait_ge(small, 4)
            nc.vector.tensor_tensor(rstd[:, :, :], rstd[:, :, :], rstd2[:, :, :], ALU.mult).then_inc(small, 1)
            dve.wait_ge(small, 5)

            def centre(b):
                if b >= RING:
                    dve.wait_ge(stored[(b - RING) // 4], 64)
                wait(dve, squared, b - RING + 1)
                nc.vector.tensor_scalar(xln[:, b % RING, :], X[:, b, :], moments[:, b, 0:1], rstd[:, b, :],
                                        ALU.subtract, ALU.mult).then_inc(centred, 1)

            for b in range(RING):
                centre(b)

            for c in range(QUADS):
                dve.wait_ge(sum_ready, c + 1)
                nc.vector.tensor_scalar(mu_length[:, :], sum_ps[:, 0:TILES], 1e-24, None, ALU.max).then_inc(mu_clamped, 1)
                if c:
                    split_lo(W1, c)
                dve.wait_ge(mu_sqrt_done, c + 1)
                nc.vector.reciprocal(mu_inv[:, :], mu_length[:, :]).then_inc(mu_inv_done, 1)
                dve.wait_ge(mu_inv_done, c + 1)
                for j in range(TILES):
                    nc.vector.tensor_scalar(mu_diagonal[:, j, :], ident[:, :], mu_inv[:, j:j + 1], None, ALU.mult)\
                        .then_inc(diagonal_done, 1)
                split_lo(W2, c)
                dve.wait_ge(wide_ready, c + 1)
                for t in range(TILES):
                    last = nc.vector.tensor_tensor(raw[MU][c % 2][:, t, :], raw[MU][c % 2][:, t, :], wide_ps[:, :],
                                                   ALU.mult)
                last.then_inc(unit_done, 1)
                split_lo(MU, c)
                if 0 < c < 3:
                    for b in range(RING + 4 * c - 4, RING + 4 * c):
                        centre(b)
            dve.wait_ge(squared, B)
            nc.vector.tensor_scalar(length[:, :], length[:, :], 1e-24, None, ALU.max).then_inc(clamped, 1)
            dve.wait_ge(sqrt_done, 3)
            nc.vector.reciprocal(length[:, :], length[:, :]).then_inc(small, 1)
            dve.wait_ge(small, 6)
            dve.wait_ge(loaded, 48)
            nc.vector.tensor_scalar(token_scale[:, :], length[:, :], scale[:, 0:1], None, ALU.mult).then_inc(small, 1)
            dve.wait_ge(small, 7)


def stage_soft(nc, x_dram, xln_dram, b1_dram, b2_dram, out_dram, gates, ident, token_scale, split, X):
    mu, w1, w2 = split
    with ExitStack() as ctx:
        m = Memory(nc, ctx, "so")
        b1 = m.sb("b1", [P, ES])
        b2 = m.sb("b2", [EXPERTS, N])
        x = m.sb("x", [P, N])
        x_out = m.sb("x_out", [P, N])
        xln = m.sb("xln", [P, N])
        xt = [m.sb(f"xt_{i}", [P, TILES, P], BF16) for i in ("hi", "lo")]
        logits, combine, dispatch_flat, hidden = (X[:, QUADS * i:QUADS * i + QUADS, :].rearrange("p q n -> p (q n)")
                                                  for i in range(4))
        dispatch_t = dispatch_flat.rearrange("p (e n) -> p e n", e=EXPERTS)
        xw = [m.sb(f"xw_{i}", [P, ES], BF16) for i in ("hi", "lo")]
        disp = [m.sb(f"disp_{i}", [P, ES], BF16) for i in ("hi", "lo")]
        comb_t = [m.sb(f"comb_t_{i}", [P, ES], BF16) for i in ("hi", "lo")]
        h = [m.sb(f"h_{i}", [P, ES], BF16) for i in ("hi", "lo")]
        g = [m.sb(f"g_{i}", [P, ES], BF16) for i in ("hi", "lo")]
        neg_scale = m.sb("neg_scale", [P, 1])
        neg_row_max = m.sb("neg_row_max", [P, 1])
        row_sum = m.sb("row_sum", [P, 1])
        out_gain = m.sb("out_gain", [P, 2])
        neg_slot_max = m.sb("neg_slot_max", [P, EXPERTS])
        slot_sum = m.sb("slot_sum", [P, EXPERTS])
        slot_inv = m.sb("slot_inv", [P, EXPERTS])
        comb_sum = m.sb("comb_sum", [P, EXPERTS])
        comb_sum_t = m.sb("comb_sum_t", [EXPERTS, P])
        big = [m.ps(f"big{i}") for i in range(2)]
        tr = [m.ps(f"tr{i}") for i in range(2)]
        small = [m.ps(f"small{i}") for i in range(2)]
        x_ps = m.ps("x_ps")
        out_ps = m.ps("out_ps")

        scale_negated = m.sem("scale_negated")
        b_loaded, x_loaded, xln_loaded, stored = m.sem("b_loaded"), m.sem("x_loaded"), m.sem("xln_loaded"), m.sem("stored")
        xt_ready, xt_hi, xt_lo = m.sem("xt_ready"), m.sem("xt_hi"), m.sem("xt_lo")
        logits_ready, logits_out = m.sem("logits_ready"), m.sem("logits_out")
        xw_ready, xw_hi, xw_lo = m.sem("xw_ready"), m.sem("xw_hi"), m.sem("xw_lo")
        row_max, combine_done = m.sem("row_max"), m.sem("combine_done")
        lt_ready, slot_max, dispatch_done, slot_inverted = m.sem("lt_ready"), m.sem("slot_max"), m.sem("dispatch_done"), m.sem("slot_inverted")
        disp_ready, disp_hi, disp_lo = m.sem("disp_ready"), m.sem("disp_hi"), m.sem("disp_lo")
        comb_ready, comb_hi, comb_lo = m.sem("comb_ready"), m.sem("comb_hi"), m.sem("comb_lo")
        comb_summed, comb_sum_ready, comb_sum_out = m.sem("comb_summed"), m.sem("comb_sum_ready"), m.sem("comb_sum_out")
        h_ready, h_biased, gelu_done, h_hi, h_lo = m.sem("h_ready"), m.sem("h_biased"), m.sem("gelu_done"), m.sem("h_hi"), m.sem("h_lo")
        g_ready, g_hi, g_lo = m.sem("g_ready"), m.sem("g_hi"), m.sem("g_lo")
        out_ready, gain_done, out_done = m.sem("out_ready"), m.sem("gain_done"), m.sem("out_done")
        block = m.block()

        def loop(eng, body):
            body(0)
            with eng.Fori(1, B - 1) as b:
                body(b)

        @block.sync
        def _(sp):
            def store(b):
                sp.wait_ge(out_done, b + 1)
                sp.dma_start(batch_of(out_dram, b), x_out[:, :]).then_inc(stored, 16)

            sp.dma_start(xln[:, :], xln_dram[0]).then_inc(xln_loaded, 16)
            sp.dma_start(b1[:, :], b1_dram.partition_broadcast(P)).then_inc(b_loaded, 16)
            sp.dma_start(b2[:, :], b2_dram).then_inc(b_loaded, 16)
            sp.dma_start(x[:, :], x_dram[0]).then_inc(x_loaded, 16)
            sp.wait_ge(xt_ready, 1)
            sp.dma_start(xln[:, :], xln_dram[1]).then_inc(xln_loaded, 16)

            def next_xln(b):
                sp.wait_ge(xt_ready, b + 2)
                sp.dma_start(xln[:, :], batch_of(xln_dram, b + 2)).then_inc(xln_loaded, 16)

            def store_and_next_x(b):
                store(b)
                sp.wait_ge(stored, 16 * b + 16)
                sp.dma_start(x[:, :], batch_of(x_dram, b + 1)).then_inc(x_loaded, 16)

            def body(b):
                next_xln(b)
                store_and_next_x(b)

            body(0)
            with sp.Fori(1, B - 2) as b:
                body(b)
            store_and_next_x(B - 2)
            store(B - 1)
            sp.wait_ge(stored, 16 * B)

        @block.tensor
        def _(pe):
            def three(out, stat, mov, start=True, stop=True):
                nc.tensor.matmul(out, stat[0], mov[0], start=start, stop=False)
                nc.tensor.matmul(out, stat[0], mov[1], start=False, stop=False)
                return nc.tensor.matmul(out, stat[1], mov[0], start=False, stop=stop)

            def transpose_x(b):
                pe.wait_ge(xln_loaded, 16 * b + 16)
                wait(pe, comb_sum_out, b - 1)
                for t in range(TILES):
                    last = nc.tensor.transpose(x_ps[:, cols(t)], xln[:, cols(t)], ident[:, :])
                last.then_inc(xt_ready, 1)

            def times(weights, c, out):
                for t in range(TILES):
                    last = three(out, [a[:, t, :] for a in xt], [w[:, TILES * c + t, :] for w in weights],
                                 start=t == 0, stop=t == TILES - 1)
                return last

            def make_logits(b, c):
                pe.wait_ge(xt_lo, b + 1)
                if c < 2:
                    wait(pe, xw_lo, 4 * b + c - 1)
                else:
                    pe.wait_ge(logits_out, 4 * b + c - 1)
                times(mu, c, big[c % 2][:, :]).then_inc(logits_ready, 1)

            def make_xw(b, c):
                if c < 2:
                    pe.wait_ge(logits_out, 4 * b + c + 3)
                else:
                    pe.wait_ge(xw_lo, 4 * b + c - 1)
                times(w1, c, big[c % 2][:, :]).then_inc(xw_ready, 1)

            def transpose_logits(b, c):
                pe.wait_ge(logits_out, 4 * b + c + 1)
                if c < 2:
                    wait(pe, comb_lo, 4 * b + c - 1)
                else:
                    pe.wait_ge(dispatch_done, EXPERTS * b + 4 * (c - 1))
                for i in range(4):
                    last = nc.tensor.transpose(tr[c % 2][:, cols(i)], logits[:, cols(4 * c + i)], ident[:, :])
                last.then_inc(lt_ready, 1)

            def transpose_dispatch(b, c):
                pe.wait_ge(dispatch_done, EXPERTS * b + 4 * (c + 3 if c < 2 else c + 1))
                if c >= 2:
                    pe.wait_ge(dispatch_done, EXPERTS * b + EXPERTS)
                    pe.wait_ge(disp_lo, 4 * b + c - 1)
                for i in range(4):
                    last = nc.tensor.transpose(tr[c % 2][:, cols(i)], dispatch_t[:, 4 * c + i, :], ident[:, :])
                last.then_inc(disp_ready, 1)

            def transpose_combine(b, c):
                pe.wait_ge(combine_done, b + 1)
                if c < 2:
                    pe.wait_ge(disp_lo, 4 * b + c + 3)
                else:
                    pe.wait_ge(comb_lo, 4 * b + c - 1)
                for i in range(4):
                    last = nc.tensor.transpose(tr[c % 2][:, cols(i)], combine[:, cols(4 * c + i)], ident[:, :])
                last.then_inc(comb_ready, 1)

            def make_h(b, c):
                pe.wait_ge(disp_lo, 4 * b + c + 1)
                pe.wait_ge(xw_lo, 4 * b + c + 1)
                if c < 2:
                    wait(pe, g_lo, 4 * b + c - 1)
                else:
                    pe.wait_ge(h_biased, EXPERTS * b + 4 * (c - 1))
                for i in range(4):
                    e = 4 * c + i
                    last = three(small[c % 2][:, cols(i)], [a[:, cols(e)] for a in disp], [a[:, cols(e)] for a in xw])
                last.then_inc(h_ready, 1)

            def make_g(b, c):
                pe.wait_ge(h_lo, 4 * b + c + 1)
                pe.wait_ge(comb_lo, 4 * b + c + 1)
                if c < 2:
                    pe.wait_ge(h_biased, EXPERTS * b + 4 * (c + 3))
                else:
                    pe.wait_ge(g_lo, 4 * b + c - 1)
                for i in range(4):
                    e = 4 * c + i
                    last = three(small[c % 2][:, cols(i)], [a[:, cols(e)] for a in h], [a[:, cols(e)] for a in comb_t])
                last.then_inc(g_ready, 1)

            def transpose_sums(b, xts):
                pe.wait_ge(comb_summed, b + 1)
                pe.wait_ge(xt_lo, xts)
                nc.tensor.transpose(x_ps[0:EXPERTS, 0:P], comb_sum[:, :], ident[:, :]).then_inc(comb_sum_ready, 1)

            def make_out(b, c):
                if c == 0:
                    pe.wait_ge(b_loaded, 32)
                    pe.wait_ge(comb_sum_out, b + 1)
                    wait(pe, out_done, b)
                    nc.tensor.matmul(out_ps[:, :], comb_sum_t[:, :], b2[:, :], start=True, stop=False)
                pe.wait_ge(g_lo, 4 * b + c + 1)
                for e in range(4 * c, 4 * c + 4):
                    last = three(out_ps[:, :], [a[:, cols(e)] for a in g], [w[:, e, :] for w in w2],
                                 start=False, stop=e == EXPERTS - 1)
                if c == QUADS - 1:
                    last.then_inc(out_ready, 1)

            transpose_x(0)
            for c in range(QUADS):
                make_logits(0, c)
            for c in range(QUADS):
                make_xw(0, c)
            for c in range(QUADS):
                transpose_logits(0, c)

            def body(b):
                transpose_x(b + 1)
                transpose_dispatch(b, 0)
                transpose_dispatch(b, 1)
                make_logits(b + 1, 0)
                transpose_dispatch(b, 2)
                make_logits(b + 1, 1)
                transpose_dispatch(b, 3)
                make_logits(b + 1, 2)
                make_logits(b + 1, 3)
                transpose_combine(b, 0)
                transpose_combine(b, 1)
                make_h(b, 0)
                make_xw(b + 1, 0)
                transpose_combine(b, 2)
                make_h(b, 1)
                make_xw(b + 1, 1)
                transpose_combine(b, 3)
                make_h(b, 2)
                make_xw(b + 1, 2)
                make_h(b, 3)
                transpose_sums(b, b + 2)
                transpose_logits(b + 1, 0)
                transpose_logits(b + 1, 1)
                make_g(b, 0)
                make_g(b, 1)
                make_xw(b + 1, 3)
                make_out(b, 0)
                transpose_logits(b + 1, 2)
                make_g(b, 2)
                make_out(b, 1)
                transpose_logits(b + 1, 3)
                make_g(b, 3)
                make_out(b, 2)
                make_out(b, 3)
            loop(pe, body)
            for c in range(QUADS):
                transpose_dispatch(B - 1, c)
            for c in range(QUADS):
                transpose_combine(B - 1, c)
            for c in range(QUADS):
                make_h(B - 1, c)
            transpose_sums(B - 1, B)
            for c in range(QUADS):
                make_g(B - 1, c)
            for c in range(QUADS):
                make_out(B - 1, c)

        @block.scalar
        def _(act):
            def hi(ready, count, out, bank, done):
                act.wait_ge(ready, count)
                nc.scalar.activation(out, bank, ACT.Copy).then_inc(done, 1)

            def x_hi(b):
                wait(act, xw_ready, 4 * b)
                hi(xt_ready, b + 1, xt[0][:, :, :].rearrange("p t n -> p (t n)"), x_ps[:, :], xt_hi)

            def scale_logits(b, c):
                wait(act, lt_ready, 4 * b)
                wait(act, row_max, b)
                if c == 0:
                    act.wait_ge(scale_negated, b + 1)
                act.wait_ge(logits_ready, 4 * b + c + 1)
                nc.scalar.activation(logits[:, cols(c, N)], big[c % 2][:, :], ACT.Copy,
                                     scale=neg_scale[:, :]).then_inc(logits_out, 1)

            def xw_hi_out(b, c):
                wait(act, h_ready, 4 * (b - 1) + c + 1)
                hi(xw_ready, 4 * b + c + 1, xw[0][:, cols(c, N)], big[c % 2][:, :], xw_hi)

            def disp_hi_out(b, c):
                wait(act, h_ready, 4 * (b - 1) + c + 1)
                hi(disp_ready, 4 * b + c + 1, disp[0][:, cols(c, N)], tr[c % 2][:, :], disp_hi)

            def comb_hi_out(b, c):
                wait(act, g_ready, 4 * (b - 1) + c + 1)
                hi(comb_ready, 4 * b + c + 1, comb_t[0][:, cols(c, N)], tr[c % 2][:, :], comb_hi)

            def gelu(b, c):
                act.wait_ge(h_biased, EXPERTS * b + 4 * c + 4)
                nc.scalar.activation(hidden[:, cols(c, N)], hidden[:, cols(c, N)], ACT.Gelu).then_inc(gelu_done, 1)

            def g_hi_out(b, c):
                wait(act, out_ready, b)
                hi(g_ready, 4 * b + c + 1, g[0][:, cols(c, N)], small[c % 2][:, :], g_hi)

            def exp_combine(b):
                act.wait_ge(row_max, b + 1)
                wait(act, comb_ready, 4 * b)
                wait(act, comb_summed, b)
                wait(act, gain_done, 2 * b)
                nc.scalar.activation(combine[:, :], logits[:, :], ACT.Exp, bias=neg_row_max[:, :], scale=-1.0,
                                     accum_out=row_sum[:, :]).then_inc(combine_done, 1)

            def exp_dispatch(b, c):
                act.wait_ge(slot_max, 4 * b + c + 1)
                wait(act, disp_ready, 4 * b)
                wait(act, slot_inverted, 4 * b)
                for i in range(4):
                    e = 4 * c + i
                    nc.scalar.activation(dispatch_t[:, e, :], tr[c % 2][:, cols(i)], ACT.Exp,
                                         bias=neg_slot_max[:, e:e + 1], scale=-1.0,
                                         accum_out=slot_sum[:, e:e + 1]).then_inc(dispatch_done, 1)

            x_hi(0)
            for c in range(QUADS):
                scale_logits(0, c)
            for c in range(QUADS):
                xw_hi_out(0, c)
            exp_combine(0)
            for c in range(QUADS):
                exp_dispatch(0, c)

            def body(b):
                x_hi(b + 1)
                disp_hi_out(b, 0)
                disp_hi_out(b, 1)
                scale_logits(b + 1, 0)
                disp_hi_out(b, 2)
                scale_logits(b + 1, 1)
                disp_hi_out(b, 3)
                scale_logits(b + 1, 2)
                scale_logits(b + 1, 3)
                comb_hi_out(b, 0)
                comb_hi_out(b, 1)
                xw_hi_out(b + 1, 0)
                comb_hi_out(b, 2)
                gelu(b, 0)
                xw_hi_out(b + 1, 1)
                comb_hi_out(b, 3)
                gelu(b, 1)
                xw_hi_out(b + 1, 2)
                gelu(b, 2)
                gelu(b, 3)
                exp_dispatch(b + 1, 0)
                g_hi_out(b, 0)
                g_hi_out(b, 1)
                exp_dispatch(b + 1, 1)
                xw_hi_out(b + 1, 3)
                exp_dispatch(b + 1, 2)
                g_hi_out(b, 2)
                exp_dispatch(b + 1, 3)
                g_hi_out(b, 3)
                exp_combine(b + 1)
            loop(act, body)
            for c in range(QUADS):
                disp_hi_out(B - 1, c)
            for c in range(QUADS):
                comb_hi_out(B - 1, c)
            for c in range(QUADS):
                gelu(B - 1, c)
            for c in range(QUADS):
                g_hi_out(B - 1, c)

        @block.vector
        def _(dve):
            def lo(hi_done, count, out, bank, hi, done):
                dve.wait_ge(hi_done, count)
                nc.vector.tensor_tensor(out, bank, hi, ALU.subtract).then_inc(done, 1)

            def x_lo(b):
                lo(xt_hi, b + 1, *[t[:, :, :].rearrange("p t n -> p (t n)") for t in (xt[1],)], x_ps[:, :],
                   xt[0][:, :, :].rearrange("p t n -> p (t n)"), xt_lo)

            def quad_lo(hi_done, b, c, dst, bank, done):
                lo(hi_done, 4 * b + c + 1, dst[1][:, cols(c, N)], bank[c % 2][:, :], dst[0][:, cols(c, N)], done)

            def max_of_rows(b):
                dve.wait_ge(logits_out, 4 * b + 4)
                wait(dve, combine_done, b)
                nc.vector.tensor_reduce(neg_row_max[:, :], logits[:, :], AX_X, ALU.min).then_inc(row_max, 1)

            def max_of_slots(b, c):
                dve.wait_ge(lt_ready, 4 * b + c + 1)
                wait(dve, dispatch_done, EXPERTS * b)
                nc.vector.tensor_reduce(neg_slot_max[:, 4 * c:4 * c + 4], tr[c % 2][:, :].rearrange("p (i n) -> p i n", i=4),
                                        AX_X, ALU.min).then_inc(slot_max, 1)

            def sum_combine(b):
                dve.wait_ge(combine_done, b + 1)
                wait(dve, comb_sum_ready, b)
                nc.vector.tensor_reduce(comb_sum[:, :], combine[:, :].rearrange("p (e s) -> p e s", e=EXPERTS), AX_X, ALU.add)\
                    .then_inc(comb_summed, 1)

            def sums_out(b):
                dve.wait_ge(comb_sum_ready, b + 1)
                wait(dve, out_ready, b)
                nc.vector.tensor_copy(comb_sum_t[:, :], x_ps[0:EXPERTS, 0:P]).then_inc(comb_sum_out, 1)

            def bias_h(b, c):
                e = 4 * c
                if c == 0:
                    dve.wait_ge(dispatch_done, EXPERTS * b + EXPERTS)
                    wait(dve, h_biased, EXPERTS * b)
                    nc.vector.reciprocal(slot_inv[:, :], slot_sum[:, :]).then_inc(slot_inverted, 4)
                    dve.wait_ge(slot_inverted, 4 * b + 4)
                dve.wait_ge(h_ready, 4 * b + c + 1)
                wait(dve, h_lo, 4 * (b - 1) + c + 1)
                for i in range(4):
                    nc.vector.scalar_tensor_tensor(out=hidden[:, cols(e + i)], in0=small[c % 2][:, cols(i)],
                                                   scalar=slot_inv[:, e + i:e + i + 1], in1=b1[:, cols(e + i)],
                                                   op0=ALU.mult, op1=ALU.add).then_inc(h_biased, 1)

            def split_h(b, c):
                dve.wait_ge(gelu_done, 4 * b + c + 1)
                wait(dve, g_ready, 4 * (b - 1) + c + 1)
                nc.vector.tensor_copy(h[0][:, cols(c, N)], hidden[:, cols(c, N)]).then_inc(h_hi, 1)
                lo(h_hi, 4 * b + c + 1, h[1][:, cols(c, N)], hidden[:, cols(c, N)], h[0][:, cols(c, N)], h_lo)

            def finish(b):
                dve.wait_ge(combine_done, b + 1)
                wait(dve, out_done, b)
                nc.vector.reciprocal(out_gain[:, 0:1], row_sum[:, :]).then_inc(gain_done, 1)
                dve.wait_ge(gain_done, 2 * b + 1)
                nc.vector.tensor_scalar(out_gain[:, 1:2], out_gain[:, 0:1], gates[:, 3:4], None, ALU.mult)\
                    .then_inc(gain_done, 1)

            def add_out(b):
                dve.wait_ge(out_ready, b + 1)
                dve.wait_ge(gain_done, 2 * b + 2)
                dve.wait_ge(x_loaded, 16 * b + 16)
                nc.vector.scalar_tensor_tensor(out=x_out[:, :], in0=out_ps[:, :], scalar=out_gain[:, 1:2], in1=x[:, :],
                                               op0=ALU.mult, op1=ALU.add).then_inc(out_done, 1)

            def negate_scale(b):
                wait(dve, logits_out, 4 * b)
                nc.vector.tensor_scalar(neg_scale[:, :], token_scale[:, bass.ds(b, 1)], -1.0, None, ALU.mult)\
                    .then_inc(scale_negated, 1)

            negate_scale(0)
            x_lo(0)
            max_of_rows(0)
            for c in range(QUADS):
                quad_lo(xw_hi, 0, c, xw, big, xw_lo)
            for c in range(QUADS):
                max_of_slots(0, c)
            dve.wait_ge(b_loaded, 32)

            def body(b):
                negate_scale(b + 1)
                x_lo(b + 1)
                for c in range(QUADS):
                    quad_lo(disp_hi, b, c, disp, tr, disp_lo)
                    if c == 1:
                        wait(dve, out_ready, b)
                        if not (isinstance(b, int) and b == 0):
                            add_out(b - 1)
                        finish(b)
                        sum_combine(b)
                quad_lo(comb_hi, b, 0, comb_t, tr, comb_lo)
                quad_lo(comb_hi, b, 1, comb_t, tr, comb_lo)
                bias_h(b, 0)
                quad_lo(xw_hi, b + 1, 0, xw, big, xw_lo)
                quad_lo(comb_hi, b, 2, comb_t, tr, comb_lo)
                bias_h(b, 1)
                quad_lo(xw_hi, b + 1, 1, xw, big, xw_lo)
                split_h(b, 0)
                quad_lo(comb_hi, b, 3, comb_t, tr, comb_lo)
                bias_h(b, 2)
                quad_lo(xw_hi, b + 1, 2, xw, big, xw_lo)
                split_h(b, 1)
                bias_h(b, 3)
                sums_out(b)
                split_h(b, 2)
                max_of_slots(b + 1, 0)
                max_of_slots(b + 1, 1)
                split_h(b, 3)
                quad_lo(g_hi, b, 0, g, small, g_lo)
                quad_lo(g_hi, b, 1, g, small, g_lo)
                quad_lo(xw_hi, b + 1, 3, xw, big, xw_lo)
                max_of_slots(b + 1, 2)
                quad_lo(g_hi, b, 2, g, small, g_lo)
                max_of_slots(b + 1, 3)
                max_of_rows(b + 1)
                quad_lo(g_hi, b, 3, g, small, g_lo)
            loop(dve, body)
            for c in range(QUADS):
                quad_lo(disp_hi, B - 1, c, disp, tr, disp_lo)
            add_out(B - 2)
            finish(B - 1)
            sum_combine(B - 1)
            for c in range(QUADS):
                quad_lo(comb_hi, B - 1, c, comb_t, tr, comb_lo)
            for c in range(QUADS):
                bias_h(B - 1, c)
            for c in range(QUADS):
                split_h(B - 1, c)
            sums_out(B - 1)
            for c in range(QUADS):
                quad_lo(g_hi, B - 1, c, g, small, g_lo)
            add_out(B - 1)
            dve.wait_ge(out_done, B)


def program(nc, ins, out):
    with ExitStack() as ctx:
        m = Memory(nc, ctx, "all")
        gates = m.sb("gates", [P, 4])
        ident = m.sb("ident", [P, P])
        token_scale = m.sb("token_scale", [P, B])
        X = m.sb("x", [P, B, N])
        stats = m.sb("stats", [P, B, 6])
        mean_rstd = m.sb("mean_rstd", [P, B, 2])
        x_dram = nc.dram_tensor("x_between", (B, P, N), F32, kind="Internal").ap()
        xln_dram = nc.dram_tensor("xln_between", (B, P, N), F32, kind="Internal").ap()

        stage_load(nc, ins["x"], ins["gates"], ins["ident"], X, mean_rstd, gates, ident)
        stage_attention0(nc, ins["wq"], ins["wkv"], ins["wout"], ins["bout"], ins["ctx"], X, stats, mean_rstd, gates, ident)

        with ExitStack() as mixture:
            mm = Memory(nc, mixture, "mixture")
            xt = [mm.sb(f"xt_{x}", [P, TILES, TOKENS], BF16) for x in ("hi", "lo")]
            chosen = mm.sb("chosen", [P, TOP_K], mybir.dt.int32)
            route_gain = mm.sb("route_gain", [P, CHUNKS, B])
            stage_route(nc, ins["gate"], ins["iota"], X, xt, stats, mean_rstd, gates, ident, chosen, route_gain)
            stage_ffn0(nc, ins["w1"], ins["b1"], ins["w2"], ins["b2"], X, xt, chosen, route_gain)

        with ExitStack() as cosine:
            mc = Memory(nc, cosine, "cosine")
            units = [[mc.sb(f"{t}_{x}", [P, B, N], BF16) for x in ("hi", "lo")] for t in ("q", "k")]
            stage_unit_heads(nc, ins["ctx"], ins["gather"], ins["scatter"], X, units)
            stage_attention1(nc, ins["ctx"], ins["stack"], ins["pick"], X, gates, ident, units)

        split = [[m.sb(f"{t}_{x}", [P, EXPERTS, N], BF16) for x in ("hi", "lo")] for t in ("soft_mu", "soft_w1", "soft_w2")]
        stage_soft_prepare(nc, ins["gamma"], ins["beta"], ins["scale"], ins["mu"], ins["soft_w1"], ins["soft_w2"], X, ident,
                           token_scale, split, x_dram, xln_dram)
        stage_soft(nc, x_dram, xln_dram, ins["soft_b1"], ins["soft_b2"], out, gates, ident, token_scale, split, X)


def pieces(w):
    return np.ascontiguousarray(w.reshape(TILES, P, QUADS, N).transpose(1, 2, 0, 3).reshape(P, QUADS * TILES, N))


def layouts(i):
    a = {k: np.ascontiguousarray(np.asarray(v)) for k, v in i.items()}
    stack, pick, gather, scatter = head_selectors()
    return {
        "x": a["x"], "ctx": a["ctx_2048"],
        "gates": np.concatenate([a["g_xattn"], a["g_ffn"]])[None, :],
        "ident": np.eye(P, dtype=np.float32),
        "wq": np.ascontiguousarray(a["L0_xattn_Wq"].T), "wkv": np.ascontiguousarray(a["L0_xattn_Wkv"].T),
        "wout": np.ascontiguousarray(a["L0_xattn_Wout"].T.reshape(PAIRS, P, P).transpose(1, 0, 2).reshape(P, N)),
        "bout": a["L0_xattn_bout"][:, None],
        "stack": stack.reshape(P, 4, PAIRS * P), "pick": pick, "gather": gather, "scatter": scatter,
        "gamma": a["L1_ffn_gamma"][None, :], "beta": a["L1_ffn_beta"][None, :], "scale": a["L1_ffn_scale"][None, :],
        "mu": pieces(a["L1_ffn_mu"].reshape(N, ES)),
        "soft_w1": pieces(a["L1_ffn_W1"].transpose(1, 0, 2).reshape(N, ES)),
        "soft_w2": np.ascontiguousarray(a["L1_ffn_W2"].transpose(1, 0, 2)),
        "soft_b1": a["L1_ffn_b1"].reshape(1, ES), "soft_b2": a["L1_ffn_b2"],
        "gate": np.ascontiguousarray(a["L0_ffn_gate_w"].T.reshape(TILES, P, E).transpose(1, 0, 2)),
        "iota": np.arange(E, dtype=np.float32)[None, :],
        "w1": a["L0_ffn_w1"], "w2": a["L0_ffn_w2"], "b2": a["L0_ffn_b2"],
        "b1": np.ascontiguousarray(a["L0_ffn_b1"].reshape(E, DFF // P, P).transpose(0, 2, 1)),
    }


OUT_SHAPE = (B, P, N)


def kernel(**inputs):
    import concourse.bacc as _bacc
    from concourse.bass_utils import run_bass_kernel_spmd as _run

    arrays = {f"in_{name}_dram": a for name, a in layouts(inputs).items()}
    nc = _bacc.Bacc("TRN2", target_bir_lowering=False, num_devices=1)
    ins = {name[3:-5]: nc.dram_tensor(name, a.shape, mybir.dt.from_np(a.dtype), kind="ExternalInput").ap()
           for name, a in arrays.items()}
    out = nc.dram_tensor("out_0_dram", OUT_SHAPE, F32, kind="ExternalOutput").ap()
    program(nc, ins, out)
    r = _run(nc, [arrays], core_ids=[0])
    return r.results[0]["out_0_dram"]
```
